# Optimizing a Trainium2 kernel written in Bass

```python
import numpy as np
import jax
import jax.numpy as jnp

def _softmax(x, axis=-1):
    return jax.nn.softmax(x, axis=axis)

def _gelu(x):
    return jax.nn.gelu(x, approximate=True)

def _silu(x):
    return jax.nn.silu(x)

def _sigmoid(x):
    return jax.nn.sigmoid(x)

def _layernorm(x, axis=-1, eps=1e-05):
    m = jnp.mean(x, axis=axis, keepdims=True)
    v = jnp.var(x, axis=axis, keepdims=True)
    return (x - m) / jnp.sqrt(v + eps)

def _scatter_add(tgt, idx, src, axis=0):
    return tgt.at[idx].add(src)

def _segment_sum(src, seg, n):
    return jax.ops.segment_sum(src, seg, n)
kernel_name = 'mk_adaln_attn_ffn_d1_seqx_r4_6fad38'

def setup_inputs(seed: int=0):
    np.random.seed(seed)
    _w = jnp.asarray

    def _rec_inputs():
        import jax
        import jax.numpy as jnp
        _rk = jax.random.key(seed)
        x = -0.000125 + 0.9999 * jax.random.normal(jax.random.fold_in(_rk, 1), (64, 64, 512), jnp.float32)
        _lenS = 64 - jax.random.randint(jax.random.fold_in(_rk, 7), (64,), 0, max(1, 64 // 4) + 1, jnp.int32)
        _lenS2 = 64 - jax.random.randint(jax.random.fold_in(_rk, 8), (64,), 0, max(1, 64 // 4) + 1, jnp.int32)
        itok_B_0_7 = jax.random.randint(jax.random.fold_in(_rk, 11), (64,), 0, 8, jnp.int32)
        fside_8xS_0 = -0.00162727 + 0.0609077 * jax.random.normal(jax.random.fold_in(_rk, 12), (8, 64), jnp.float32)
        itok_B_0_6 = jax.random.randint(jax.random.fold_in(_rk, 13), (64,), 0, 7, jnp.int32)
        return (x, itok_B_0_7, fside_8xS_0, itok_B_0_6)
    x, itok_B_0_7, fside_8xS_0, itok_B_0_6 = _rec_inputs()

    def _L0_cond_setup():
        import jax, jax.numpy as jnp
        import numpy as np
        B, C, T = (64, 64, 512)
        D, N = (64, 8)
        key = jax.random.key(seed)
        k_x, k_s, k_w, k_b = jax.random.split(key, 4)
        scale = 1.0 / np.sqrt(C)
        x = jax.random.normal(k_x, (B, C, T), dtype=jnp.float32)
        subjects = jax.random.randint(k_s, (B,), 0, N, dtype=jnp.int64)
        weights = jax.random.normal(k_w, (N, C, D), dtype=jnp.float32) * scale
        bias = jax.random.normal(k_b, (N, D), dtype=jnp.float32) * scale
        return {'x': x, 'subjects': subjects, 'weights': weights, 'bias': bias}
    _L0_cond_all = _L0_cond_setup()
    _L0_cond_in = {k: v for k, v in _L0_cond_all.items() if k in ('weights',)}
    del _L0_cond_all

    def _L0_attn_setup():
        import jax, jax.numpy as jnp
        import numpy as np
        B, T, C = (2, 512, 512)
        NH, DH, DHR, L = (16, 128, 64, 128)
        BASE = 10000.0

        def _rope_tables(t, d):
            freq = jnp.arange(1, t + 1, dtype=jnp.float32)[:, None]
            pos = jnp.repeat(jnp.arange(d // 2, dtype=jnp.float32), 2)[None]
            theta = jnp.exp(-pos / d * jnp.log(BASE))
            return (jnp.cos(freq * theta), jnp.sin(freq * theta))

        def _rope(x, t_start=0):
            b, t, d = x.shape
            cos, sin = _rope_tables(t_start + t, d)
            cos, sin = (cos[t_start:t_start + t], sin[t_start:t_start + t])
            xf = x.astype(jnp.float32)
            xr = xf.reshape(b, t, d // 2, 2)
            rot = jnp.stack([-xr[..., 1], xr[..., 0]], axis=-1).reshape(b, t, d)
            return (xf * cos + rot * sin).astype(x.dtype)
        key = jax.random.key(seed)
        ks = jax.random.split(key, 13)
        s = 0.02
        return {'x': jax.random.normal(ks[0], (B, T, C), jnp.float32), 'WA': jax.random.normal(ks[1], (C, 2 * L), jnp.float32) * s, 'bA': jnp.zeros((2 * L,), jnp.float32), 'WB': jax.random.normal(ks[2], (2 * L, DHR), jnp.float32) * s, 'bB': jnp.zeros((DHR,), jnp.float32), 'WC': jax.random.normal(ks[3], (2 * L, DHR * NH), jnp.float32) * s, 'bC': jnp.zeros((DHR * NH,), jnp.float32), 'WUQ': jax.random.normal(ks[4], (L, NH * DH), jnp.float32) * s, 'WUK': jax.random.normal(ks[5], (L, NH * DH), jnp.float32) * s, 'WUV': jax.random.normal(ks[6], (L, NH * DH), jnp.float32) * s, 'WZ': jax.random.normal(ks[7], (NH * DH, C), jnp.float32) * s, 'bZ': jnp.zeros((C,), jnp.float32)}
    _L0_attn_all = _L0_attn_setup()
    _L0_attn_in = {k: v for k, v in _L0_attn_all.items() if k in ('WA', 'bA', 'WB', 'bB', 'WC', 'bC', 'WUQ', 'WUK', 'WUV', 'WZ', 'bZ')}
    del _L0_attn_all

    def _L0_cond2_setup():
        import jax, jax.numpy as jnp
        import numpy as np
        B, T, D_IN, D_OUT = (16, 512, 512, 512)
        N_ADAPTERS, RANK = (8, 16)
        key = jax.random.key(seed)
        k_x, k_w, k_a, k_b, k_s, k_idx = jax.random.split(key, 6)
        x = jax.random.normal(k_x, (B, T, D_IN), dtype=jnp.float32)
        W = jax.random.normal(k_w, (D_OUT, D_IN), dtype=jnp.float32) * (1.0 / np.sqrt(D_IN))
        A = jax.random.normal(k_a, (N_ADAPTERS, RANK, D_IN), dtype=jnp.float32) * 0.02
        Bm = jax.random.normal(k_b, (N_ADAPTERS, D_OUT, RANK), dtype=jnp.float32) * 0.02
        scalings = jnp.ones((N_ADAPTERS,), dtype=jnp.float32)
        adapter_idx = jax.random.randint(k_idx, (B,), 0, N_ADAPTERS, dtype=jnp.int32)
        return {'x': x, 'W': W, 'A': A, 'Bm': Bm, 'scalings': scalings, 'adapter_idx': adapter_idx}
    _L0_cond2_all = _L0_cond2_setup()
    _L0_cond2_in = {k: v for k, v in _L0_cond2_all.items() if k in ('W', 'A', 'Bm', 'scalings')}
    del _L0_cond2_all

    def _L0_ffn_setup():
        import jax, jax.numpy as jnp
        import numpy as np
        B, T, D, E, H = (4, 512, 512, 4, 2048)
        TOPK = 2
        CAPACITY_FACTOR = 1
        key = jax.random.key(seed)
        k0, k1, k2, k3 = jax.random.split(key, 4)
        x = jax.random.normal(k0, (B, T, D), dtype=jnp.float32)
        Wg = jax.random.normal(k1, (D, E), dtype=jnp.float32) * 0.02
        bg = jnp.zeros((E,), dtype=jnp.float32)
        W1 = jax.random.normal(k2, (E, D, H), dtype=jnp.float32) * (1.0 / np.sqrt(D))
        W2 = jax.random.normal(k3, (E, H, D), dtype=jnp.float32) * (1.0 / np.sqrt(H))
        return {'x': x, 'Wg': Wg, 'bg': bg, 'W1': W1, 'W2': W2}
    _L0_ffn_all = _L0_ffn_setup()
    _L0_ffn_in = {k: v for k, v in _L0_ffn_all.items() if k in ('Wg', 'bg', 'W1', 'W2')}
    del _L0_ffn_all
    return {'x': x, 'itok_B_0_7': itok_B_0_7, 'fside_8xS_0': fside_8xS_0, 'itok_B_0_6': itok_B_0_6, 'L0_cond_weights': _L0_cond_in['weights'], 'L0_attn_WA': _L0_attn_in['WA'], 'L0_attn_bA': _L0_attn_in['bA'], 'L0_attn_WB': _L0_attn_in['WB'], 'L0_attn_bB': _L0_attn_in['bB'], 'L0_attn_WC': _L0_attn_in['WC'], 'L0_attn_bC': _L0_attn_in['bC'], 'L0_attn_WUQ': _L0_attn_in['WUQ'], 'L0_attn_WUK': _L0_attn_in['WUK'], 'L0_attn_WUV': _L0_attn_in['WUV'], 'L0_attn_WZ': _L0_attn_in['WZ'], 'L0_attn_bZ': _L0_attn_in['bZ'], 'L0_cond2_W': _L0_cond2_in['W'], 'L0_cond2_A': _L0_cond2_in['A'], 'L0_cond2_Bm': _L0_cond2_in['Bm'], 'L0_cond2_scalings': _L0_cond2_in['scalings'], 'L0_ffn_Wg': _L0_ffn_in['Wg'], 'L0_ffn_bg': _L0_ffn_in['bg'], 'L0_ffn_W1': _L0_ffn_in['W1'], 'L0_ffn_W2': _L0_ffn_in['W2']}

def reference(x, itok_B_0_7, fside_8xS_0, itok_B_0_6, L0_cond_weights, L0_attn_WA, L0_attn_bA, L0_attn_WB, L0_attn_bB, L0_attn_WC, L0_attn_bC, L0_attn_WUQ, L0_attn_WUK, L0_attn_WUV, L0_attn_WZ, L0_attn_bZ, L0_cond2_W, L0_cond2_A, L0_cond2_Bm, L0_cond2_scalings, L0_ffn_Wg, L0_ffn_bg, L0_ffn_W1, L0_ffn_W2):
    import jax
    import jax.numpy as jnp

    def _L0_cond_ref(x, subjects, weights, bias):
        import jax, jax.numpy as jnp
        import numpy as np
        B, C, T = (64, 64, 512)
        D, N = (64, 8)
        w = weights[subjects]
        b = bias[subjects]
        out = jnp.einsum('bct,bcd->bdt', x, w)
        out = out + b[:, :, None]
        return out

    def _L0_attn_ref(x, WA, bA, WB, bB, WC, bC, WUQ, WUK, WUV, WZ, bZ):
        import jax, jax.numpy as jnp
        import numpy as np
        B, T, C = (2, 512, 512)
        NH, DH, DHR, L = (16, 128, 64, 128)
        BASE = 10000.0

        def _rope_tables(t, d):
            freq = jnp.arange(1, t + 1, dtype=jnp.float32)[:, None]
            pos = jnp.repeat(jnp.arange(d // 2, dtype=jnp.float32), 2)[None]
            theta = jnp.exp(-pos / d * jnp.log(BASE))
            return (jnp.cos(freq * theta), jnp.sin(freq * theta))

        def _rope(x, t_start=0):
            b, t, d = x.shape
            cos, sin = _rope_tables(t_start + t, d)
            cos, sin = (cos[t_start:t_start + t], sin[t_start:t_start + t])
            xf = x.astype(jnp.float32)
            xr = xf.reshape(b, t, d // 2, 2)
            rot = jnp.stack([-xr[..., 1], xr[..., 0]], axis=-1).reshape(b, t, d)
            return (xf * cos + rot * sin).astype(x.dtype)
        b, t, _ = x.shape
        h = x @ WA + bA
        kv_lat, q_lat = jnp.split(h, 2, axis=-1)
        kRt = _rope(h @ WB + bB, 0)
        qRt = _rope(h @ WC + bC, 0)
        qRt = qRt.reshape(b, t, NH, DHR).transpose(0, 2, 1, 3)
        q = (q_lat @ WUQ).reshape(b, t, NH, DH).transpose(0, 2, 1, 3)
        k = (kv_lat @ WUK).reshape(b, t, NH, DH).transpose(0, 2, 1, 3)
        v = (kv_lat @ WUV).reshape(b, t, NH, DH).transpose(0, 2, 1, 3)
        qf = jnp.concatenate([q, qRt], axis=-1)
        kf = jnp.concatenate([k, jnp.broadcast_to(kRt[:, None], (b, NH, t, DHR))], axis=-1)
        dk = DH + DHR
        scores = jnp.einsum('bhqd,bhkd->bhqk', qf.astype(jnp.float32), kf.astype(jnp.float32)) * dk ** (-0.5)
        causal = jnp.tril(jnp.ones((t, t), dtype=bool))
        scores = jnp.where(causal, scores, -jnp.inf)
        attn = jax.nn.softmax(scores, axis=-1)
        out = jnp.einsum('bhqk,bhkd->bhqd', attn, v.astype(jnp.float32)).astype(x.dtype)
        out = out.transpose(0, 2, 1, 3).reshape(b, t, NH * DH)
        return out @ WZ + bZ

    def _L0_cond2_ref(x, W, A, Bm, scalings, adapter_idx):
        import jax, jax.numpy as jnp
        import numpy as np
        B, T, D_IN, D_OUT = (16, 512, 512, 512)
        N_ADAPTERS, RANK = (8, 16)
        H = jnp.einsum('btd,od->bto', x, W)
        A_b = A[adapter_idx]
        B_b = Bm[adapter_idx]
        s_b = scalings[adapter_idx]
        xa = jnp.einsum('btd,brd->btr', x, A_b)
        delta = jnp.einsum('btr,bor->bto', xa, B_b)
        delta = jax.lax.stop_gradient(delta * s_b[:, None, None])
        return H + delta

    def _L0_ffn_ref(x, Wg, bg, W1, W2):
        import jax, jax.numpy as jnp
        import numpy as np
        B, T, D, E, H = (4, 512, 512, 4, 2048)
        TOPK = 2
        CAPACITY_FACTOR = 1
        Bq, Tq, Dq = x.shape
        N = Bq * Tq
        capacity = int(N * CAPACITY_FACTOR / E)
        flat_x = x.reshape(N, Dq)
        logits = flat_x @ Wg + bg
        top_vals, top_idx = jax.lax.top_k(logits, TOPK)
        sparse = jnp.full_like(logits, -jnp.inf)
        sparse = sparse.at[jnp.arange(N)[:, None], top_idx].set(top_vals)
        probs = jax.nn.softmax(sparse, axis=-1)
        out = jnp.zeros_like(flat_x)
        for i in range(E):
            assigned = (top_idx == i).any(axis=-1)
            score = jnp.where(assigned, probs[:, i], -jnp.inf)
            sel_p, sel_idx = jax.lax.top_k(score, capacity)
            p = jnp.where(jnp.isfinite(sel_p), sel_p, 0.0)[:, None]
            tok = flat_x[sel_idx]
            h = jax.nn.gelu(tok @ W1[i], approximate=False)
            y = h @ W2[i] * p
            out = out.at[sel_idx].add(y)
        return out.reshape(Bq, Tq, Dq)
    x = x + _L0_attn_ref(_L0_cond_ref(x, itok_B_0_7, L0_cond_weights, fside_8xS_0), L0_attn_WA, L0_attn_bA, L0_attn_WB, L0_attn_bB, L0_attn_WC, L0_attn_bC, L0_attn_WUQ, L0_attn_WUK, L0_attn_WUV, L0_attn_WZ, L0_attn_bZ)
    x = x + _L0_ffn_ref(_L0_cond2_ref(x, L0_cond2_W, L0_cond2_A, L0_cond2_Bm, L0_cond2_scalings, itok_B_0_6), L0_ffn_Wg, L0_ffn_bg, L0_ffn_W1, L0_ffn_W2)
    return x

_drawn_inputs = setup_inputs


def setup_inputs(seed=0):
    import zlib

    import numpy as np

    out = dict(_drawn_inputs(seed))
    spreads = {'L0_attn_bA': (0.0, 0.1),
     'L0_attn_bB': (0.0, 0.8),
     'L0_attn_bC': (0.0, 0.8),
     'L0_attn_bZ': (0.0, 0.1),
     'L0_cond2_scalings': (1.0, 0.553),
     'L0_ffn_bg': (0.0, 0.1)}
    factors = {'fside_8xS_0': 6.009,
     'L0_attn_WB': 6.441,
     'L0_attn_WC': 8.0,
     'L0_attn_WUQ': 8.0,
     'L0_attn_WUK': 6.575}
    for name, (base, spread) in spreads.items():
        noise = np.random.default_rng([zlib.crc32(name.encode()), seed]).standard_normal(out[name].shape)
        drawn = base * np.exp(spread * noise) if base else spread * noise
        out[name] = jnp.asarray(drawn.astype(out[name].dtype))
    for name, factor in factors.items():
        out[name] = (out[name] * factor).astype(out[name].dtype)
    return out
```

```python
from contextlib import ExitStack

import numpy as np

import concourse.bass as bass
from concourse import mybir

F32 = mybir.dt.float32
F32R = mybir.dt.float32r
BF16 = mybir.dt.bfloat16
I32 = mybir.dt.int32
U32 = mybir.dt.uint32
ALU = mybir.AluOpType
ACT = mybir.ActivationFunctionType
AX = mybir.AxisListType.X

P = 128
B, C, T = 64, 64, 512
NSUB, NADAPT, RANK = 8, 8, 16
NH, DH, DR, L = 16, 128, 64, 128
SCALE = float(np.float32((DH + DR) ** -0.5))
MASKED = -1.0e30
TC = T // P
GB = 8
NG = B // GB
GT = GB * C
NPAIR = GT // P
NU = NH // 2
NTOK = B * C
NT = NTOK // P
NE, HID = 4, 2048
CAP = NTOK // NE
NCH = CAP // P
HC = HID // P


TRIALS = 15
TABLES = {
    "always": {"ident": P, "ones": P, "part": 1},
    "attend": {"mask": C, "cosq": NU * C, "sinq": NU * C, "cosk": C, "sink": C},
    "route": {"before": P, "iota": P, "adapter": 1, "tile": NT, "trial": 3 * TRIALS},
}


def const_columns():
    def rope(feature, size):
        theta = np.exp(-(feature // 2).astype(np.float32) / np.float32(size)
                       * np.log(np.float32(10000.0))).astype(np.float32)
        angle = (np.arange(1, C + 1, dtype=np.float32)[None] * theta[:, None]).astype(np.float32)
        sign = np.where(feature % 2 == 0, -1.0, 1.0).astype(np.float32)[:, None]
        return np.cos(angle), np.sin(angle) * sign

    p = np.arange(P)
    pairs = [rope(u * P + p, DR * NH) for u in range(NU)]
    cosk, sink = rope(p % DR, DR)
    trial = np.array([c << (2 * (TRIALS - 1 - i)) for i in range(TRIALS) for c in (1, 2, 3)], np.int32)
    return {
        "ident": np.eye(P), "ones": np.ones((P, P)), "part": p[:, None],
        "mask": np.where(np.arange(C)[None] <= (p % C)[:, None], 0.0, MASKED),
        "cosq": np.concatenate([c for c, _ in pairs], 1), "sinq": np.concatenate([s for _, s in pairs], 1),
        "cosk": cosk, "sink": sink,
        "before": p[:, None] < p[None], "iota": np.broadcast_to(p[None], (P, P)), "adapter": p[:, None] // RANK,
        "tile": np.broadcast_to(np.arange(NT)[None], (P, NT)),
        "trial": np.broadcast_to(trial.view(np.float32), (P, 3 * TRIALS)),
    }


def const_table(name):
    columns = const_columns()
    return np.concatenate([columns[n] for n in TABLES[name]], 1).astype(np.float32)


def split_product(nc, out, pairs, start=True, stop=True):
    last = None
    for n, ((ah, al), (bh, bl)) in enumerate(pairs):
        nc.tensor.matmul(out, ah, bh, start=start and n == 0, stop=False)
        nc.tensor.matmul(out, ah, bl, start=False, stop=False)
        last = nc.tensor.matmul(out, al, bh, start=False, stop=stop and n == len(pairs) - 1)
    return last


def absorb_weights(nc, K, A, W):
    HG = NH // 4
    with ExitStack() as ctx:
        def sb(name, shape, dt=F32):
            return ctx.enter_context(nc.sbuf_tensor(name, shape, dt))

        def bank(name):
            return ctx.enter_context(nc.psum_tensor(name, [P, 512], F32))

        def sem(name):
            return ctx.enter_context(nc.semaphore(name))

        up = {n: sb(f"up_{n}", [P, NH * DH]) for n in "qkv"}
        wz = sb("wz_raw", [P, NH, T])
        wa = sb("wa_raw", [P, TC, 2 * L])
        wc = sb("wc_raw", [P, 2, DR * NH])
        wb = sb("wb_raw", [P, 2, DR])
        upT = {n: sb(f"upT_{n}", [P, 2, 512]) for n in "qkv"}
        bank_t = {n: bank(f"w_t{n}") for n in "qkv"}
        bank_a = bank("w_a")
        bank_m = [bank(f"w_m{i}") for i in range(4)]

        consts_in = sem("consts_in")
        up_in = {n: sem(f"up{n}_in") for n in "qkv"}
        wz_in = [sem(f"wz_in{i}") for i in range(HG)]
        small_in = sem("small_in")
        t_mm = {n: sem(f"w_t{n}_mm") for n in "qkv"}
        t_ev = {n: sem(f"w_t{n}_ev") for n in "qkv"}
        a_mm, a_hi, a_lo = sem("w_a_mm"), sem("w_a_hi"), sem("w_a_lo")
        m_mm, m_hi, m_lo = sem("w_m_mm"), sem("w_m_hi"), sem("w_m_lo")
        s_hi, s_lo = sem("w_s_hi"), sem("w_s_lo")
        zeroed = sem("w_zeroed")

        block = ctx.enter_context(nc.Block())
        wz_d = A["WZ"].rearrange("(h d) n -> d h n", d=DH)

        @block.sync
        def _(sp):
            sp.dma_start(K["always"][:, :], A["always"]).then_inc(consts_in, 16)
            for n, name in (("q", "WUQ"), ("k", "WUK"), ("v", "WUV")):
                sp.dma_start(up[n][:, :], A[name]).then_inc(up_in[n], 16)
            for i in range(HG):
                sp.dma_start(wz[:, 4 * i:4 * i + 4, :], wz_d[:, 4 * i:4 * i + 4, :]).then_inc(wz_in[i], 16)
            with nc.allow_non_contiguous_dma(reason="a few small vectors, once"):
                sp.dma_start(wa[:, :, :], A["WA"].rearrange("(c p) n -> p c n", p=P)).then_inc(small_in, 16)
                sp.dma_start(wc[:, :, :], A["WC"].rearrange("(c p) n -> p c n", p=P)).then_inc(small_in, 16)
                sp.dma_start(wb[:, :, :], A["WB"].rearrange("(c p) n -> p c n", p=P)).then_inc(small_in, 16)
                sp.dma_start(K["bA"][:, :], A["bA"].rearrange("(c p) -> p c", p=P)).then_inc(small_in, 16)
                sp.dma_start(K["bC"][:, :], A["bC"].rearrange("(c p) -> p c", p=P)).then_inc(small_in, 16)
                for h in range(2):
                    sp.dma_start(K["bB"][h * DR:(h + 1) * DR, :],
                                 A["bB"].rearrange("(p o) -> p o", o=1)).then_inc(small_in, 16)
                    sp.dma_start(K["wsub"][h * C:(h + 1) * C, :, :],
                                 A["cond_weights"].rearrange("n c d -> c n d")).then_inc(small_in, 16)
                sp.dma_start(K["bZ"][:, :], A["bZ"].partition_broadcast(P)).then_inc(small_in, 16)
                sp.dma_start(K["attend"][:, :], A["attend"]).then_inc(small_in, 16)
                sp.dma_start(K["fside"][:, :], A["fside"]).then_inc(small_in, 16)
                sp.dma_start(K["subj"][:, :], A["subj"].partition_broadcast(NSUB)).then_inc(small_in, 16)

        SMALL = 16 * 13

        @block.scalar
        def _(act):
            for i in range(HG):
                s = i % 2
                for n in "qv":
                    act.wait_ge(t_mm[n], i + 1)
                    if i >= 2:
                        act.wait_ge(a_mm if n == "q" else m_mm, i - 1 if n == "q" else 4 * (i - 1))
                    nc.scalar.copy(upT[n][:, s, :], bank_t[n][:, :]).then_inc(t_ev[n], 1)
                act.wait_ge(a_mm, i + 1)
                nc.scalar.copy(W["Ah"][:, 512 * i:512 * i + 512], bank_a[:, :]).then_inc(a_hi, 1)
                for j in range(4):
                    act.wait_ge(m_mm, 4 * i + j + 1)
                    nc.scalar.copy(W["Mh"][:, 4 * i + j, :], bank_m[j][:, :]).then_inc(m_hi, 1)
            act.wait_ge(small_in, SMALL)
            nc.scalar.copy(W["WAh"][:, :, :], wa[:, :, :]).then_inc(s_hi, 1)
            nc.scalar.copy(W["WCh"][:, :, :], wc[:, :, :]).then_inc(s_hi, 1)
            nc.scalar.copy(W["WBh"][:, :, :, :],
                           wb[:, :, :].unsqueeze(2).to_broadcast([P, 2, 2, DR])).then_inc(s_hi, 1)

        @block.gpsimd
        def _(pool):
            nc.gpsimd.memset(K["wblk"][:, :, :], 0.0).then_inc(zeroed, 1)
            nc.gpsimd.memset(K["qrope"][:, :, :, :], 0.0).then_inc(zeroed, 1)
            pool.wait_ge(s_hi, 1)
            nc.gpsimd.tensor_tensor(W["WAl"][:, :, :], wa[:, :, :], W["WAh"][:, :, :].bitcast(F32),
                                    ALU.subtract).then_inc(s_lo, 1)
            pool.wait_ge(s_hi, 2)
            nc.gpsimd.tensor_tensor(W["WCl"][:, :, :], wc[:, :, :], W["WCh"][:, :, :].bitcast(F32),
                                    ALU.subtract).then_inc(s_lo, 1)
            pool.wait_ge(s_hi, 3)
            nc.gpsimd.tensor_tensor(W["WBl"][:, :, :, :],
                                    wb[:, :, :].unsqueeze(2).to_broadcast([P, 2, 2, DR]),
                                    W["WBh"][:, :, :, :].bitcast(F32), ALU.subtract).then_inc(s_lo, 1)

        @block.vector
        def _(dve):
            for i in range(HG):
                s = i % 2
                dve.wait_ge(t_mm["k"], i + 1)
                if i >= 2:
                    dve.wait_ge(a_mm, i - 1)
                nc.vector.tensor_copy(upT["k"][:, s, :], bank_t["k"][:, :]).then_inc(t_ev["k"], 1)
                dve.wait_ge(a_hi, i + 1)
                nc.vector.tensor_tensor(W["Al"][:, 512 * i:512 * i + 512], bank_a[:, :],
                                        W["Ah"][:, 512 * i:512 * i + 512].bitcast(F32),
                                        ALU.subtract).then_inc(a_lo, 1)
                for j in range(4):
                    h = 4 * i + j
                    dve.wait_ge(m_hi, h + 1)
                    nc.vector.tensor_tensor(W["Ml"][:, h, :], bank_m[j][:, :], W["Mh"][:, h, :].bitcast(F32),
                                            ALU.subtract).then_inc(m_lo, 1)
            dve.wait_ge(small_in, SMALL)
            nc.vector.tensor_scalar(K["sel"][:, :], K["subj"][:, :], K.parts["part"][0:NSUB, :], None,
                                    ALU.is_equal).then_inc(zeroed, 1)

        @block.tensor
        def _(pe):
            def transposes(i):
                for n in "qkv":
                    pe.wait_ge(up_in[n], 16)
                    if i >= 1:
                        pe.wait_ge(t_ev[n], i)
                    for j in range(4):
                        h = 4 * i + j
                        last = nc.tensor.transpose(bank_t[n][:, j * P:(j + 1) * P], up[n][:, h * P:(h + 1) * P],
                                                   K.parts["ident"])
                    last.then_inc(t_mm[n], 1)

            pe.wait_ge(consts_in, 16)
            transposes(0)
            for i in range(HG):
                s = i % 2
                if i + 1 < HG:
                    transposes(i + 1)
                pe.wait_ge(t_ev["q"], i + 1)
                pe.wait_ge(t_ev["k"], i + 1)
                if i >= 1:
                    pe.wait_ge(a_lo, i)
                for j in range(4):
                    cols = slice(j * P, (j + 1) * P)
                    last = nc.tensor.matmul(bank_a[:, cols], upT["q"][:, s, cols], upT["k"][:, s, cols],
                                            start=True, stop=True)
                last.then_inc(a_mm, 1)
                pe.wait_ge(t_ev["v"], i + 1)
                pe.wait_ge(wz_in[i], 16)
                for j in range(4):
                    if i >= 1:
                        pe.wait_ge(m_lo, 4 * (i - 1) + j + 1)
                    nc.tensor.matmul(bank_m[j][:, :], upT["v"][:, s, j * P:(j + 1) * P], wz[:, 4 * i + j, :],
                                     start=True, stop=True).then_inc(m_mm, 1)


def attention(nc, K, A, W, out):
    with ExitStack() as ctx:
        def sb(name, shape, dt=F32):
            return ctx.enter_context(nc.sbuf_tensor(name, shape, dt))

        def bank(name):
            return ctx.enter_context(nc.psum_tensor(name, [P, 512], F32))

        def sem(name):
            return ctx.enter_context(nc.semaphore(name))

        x_cond = sb("x_cond", [P, NPAIR, T])
        x_res = sb("x_res", [P, NPAIR, T])
        cond_h, cond_l = sb("cond_h", [P, TC, GT], F32R), sb("cond_l", [P, TC, GT], F32R)
        lat32 = sb("lat32", [P, 2, GT])
        lat_h, lat_l = sb("lat_h", [P, 2, GT], F32R), sb("lat_l", [P, 2, GT], F32R)
        kv_tok = sb("kv_tok", [P, NPAIR, L])
        k_rope = sb("k_rope", [P, GT])
        raw, swapped = sb("rope_raw", [P, GT]), sb("rope_swapped", [P, GT])
        by_cos, by_sin = sb("rope_cos", [P, GT]), sb("rope_sin", [P, GT])
        cond32 = (raw, swapped)
        bias_bc = by_cos
        bias_sel = by_sin[0:NSUB, :].rearrange("n (b d) -> n b d", b=GB)
        q_nope = sb("q_nope", [P, GB, 2, C])
        score = sb("score", [P, GB, C])
        prob = sb("prob", [P, 2, GB, C])
        rmax, rsum, rinv = sb("rmax", [P, GB]), sb("rsum", [P, GB]), sb("rinv", [P, GB])
        wait_here = sb("wait_here", [1, 1])
        probT = sb("probT", [P, NPAIR, P])
        mix_h = sb("mix_h", [P, 2, 2, NPAIR, 2, C], F32R)
        mix_l = sb("mix_l", [P, 2, 2, NPAIR, 2, C], F32R)
        q_rope = K["qrope"]
        bank_a, bank_b, bank_d, bank_s = bank("bank_a"), bank("bank_b"), bank("bank_d"), bank("bank_s")
        bank_o = [bank(f"bank_o{t}") for t in range(NPAIR)]

        names = """x_in xres_in xres_biased x2_out wblk_ready bias_sel_ready bias_mm bias_ev cond_mm cond_ev cond_hi
            cond_lo lat_mm lat_ev lat_hi lat_lo kb_mm kvt_mm kvt_ev raw_ev swap_ev cos_ev sin_ev rope_done
            qc_mm qn0_mm qn1_mm qn0_ev qn1_ev score_mm score_ev max_ev sub_ev exp_ev sum_ev inv_ev prob_ev pt_mm pt_ev
            mixe_mm mixo_mm mixe_hi mixo_hi mixe_lo mixo_lo wz_mm x2_ev""".split()
        S = {n: sem("at_" + n) for n in names}

        block = ctx.enter_context(nc.Block())
        x_d = A["x"].rearrange("(g n j) c t -> g (j c) n t", n=NPAIR, j=2)
        out_d = out.rearrange("(g n j) c t -> g (j c) n t", n=NPAIR, j=2)
        NR = NU + 1

        def over_groups(eng, first, body):
            first()
            with eng.Fori(0, NG - 1) as g:
                body(g, True)
            body(NG - 1, False)

        @block.sync
        def _(sp):
            def first():
                sp.dma_start(x_cond[:, :, :], x_d[0]).then_inc(S["x_in"], 16)
                sp.dma_start(x_res[:, :, :], x_d[0]).then_inc(S["xres_in"], 16)

            def body(g, more):
                if more:
                    sp.wait_ge(S["cond_mm"], g * TC + TC)
                    sp.dma_start(x_cond[:, :, :], x_d[g + 1]).then_inc(S["x_in"], 16)
                sp.wait_ge(S["x2_ev"], g * NPAIR + NPAIR)
                sp.dma_start(out_d[g], x_res[:, :, :]).then_inc(S["x2_out"], 16)
                sp.wait_ge(S["x2_out"], g * 16 + 16)
                if more:
                    sp.dma_start(x_res[:, :, :], x_d[g + 1]).then_inc(S["xres_in"], 16)

            over_groups(sp, first, body)

        @block.gpsimd
        def _(pool):
            def bias_rows(g):
                nc.gpsimd.tensor_tensor(bias_sel[:, :, :],
                                        K["sel"][:, bass.ds(g * GB, GB)].unsqueeze(2).to_broadcast([NSUB, GB, C]),
                                        K["fside"][:, :].unsqueeze(1).to_broadcast([NSUB, GB, C]),
                                        ALU.mult).then_inc(S["bias_sel_ready"], 1)

            def cond_lo(g, c, first=False):
                pool.wait_ge(S["cond_hi"], g * TC + c + 1)
                nc.gpsimd.tensor_tensor(cond_l[:, c, :], cond32[c % 2][:, :], cond_h[:, c, :].bitcast(F32),
                                        ALU.subtract).then_inc(S["cond_lo"], 1)

            def rope_products(r, cos, sin, first=False):
                pool.wait_ge(S["raw_ev"], r + 1)
                if not first:
                    pool.wait_ge(S["rope_done"], r)
                v = raw[:, :].rearrange("p (b t) -> p b t", b=GB)
                w = swapped[:, :].rearrange("p (b t) -> p b t", b=GB)
                nc.gpsimd.tensor_tensor(by_cos[:, :].rearrange("p (b t) -> p b t", b=GB), v,
                                        cos.unsqueeze(1).to_broadcast([P, GB, C]), ALU.mult).then_inc(S["cos_ev"], 1)
                pool.wait_ge(S["swap_ev"], r + 1)
                nc.gpsimd.tensor_tensor(by_sin[:, :].rearrange("p (b t) -> p b t", b=GB), w,
                                        sin.unsqueeze(1).to_broadcast([P, GB, C]), ALU.mult).then_inc(S["sin_ev"], 1)

            def q_rope_products(g, u):
                rope_products(g * NR + 1 + u, K.parts["cosq"][:, u * C:(u + 1) * C], K.parts["sinq"][:, u * C:(u + 1) * C])

            def first():
                bias_rows(0)
                for c in range(TC):
                    cond_lo(0, c)
                rope_products(0, K.parts["cosk"], K.parts["sink"], first=True)

            def body(g, more):
                q_rope_products(g, 0)
                for u in range(NU):
                    if u + 1 < NU:
                        q_rope_products(g, u + 1)
                    elif more:
                        pool.wait_ge(S["rope_done"], g * NR + NR)
                        bias_rows(g + 1)
                    pool.wait_ge(S["inv_ev"], g * NU + u + 1)
                    nc.gpsimd.tensor_tensor(prob[:, u % 2, :, :], prob[:, u % 2, :, :],
                                            rinv[:, :].unsqueeze(2).to_broadcast([P, GB, C]),
                                            ALU.mult).then_inc(S["prob_ev"], 1)
                    if u == 2:
                        pool.wait_ge(S["xres_in"], g * 16 + 16)
                        nc.gpsimd.tensor_tensor(x_res[:, :, :], x_res[:, :, :],
                                                K["bZ"][:, :].unsqueeze(1).to_broadcast([P, NPAIR, T]),
                                                ALU.add).then_inc(S["xres_biased"], 1)
                if more:
                    for c in range(TC):
                        cond_lo(g + 1, c)
                    rope_products((g + 1) * NR, K.parts["cosk"], K.parts["sink"])

            over_groups(pool, first, body)

        @block.scalar
        def _(act):
            def bias_evac(g):
                act.wait_ge(S["bias_mm"], g + 1)
                nc.scalar.copy(bias_bc[:, :], bank_s[:, :]).then_inc(S["bias_ev"], 1)

            def cond_hi(g, c):
                act.wait_ge(S["cond_ev"], g * TC + c + 1)
                nc.scalar.copy(cond_h[:, c, :], cond32[c % 2][:, :]).then_inc(S["cond_hi"], 1)

            def latent(g, i):
                act.wait_ge(S["lat_mm"], g * 2 + i + 1)
                nc.scalar.activation(lat32[:, i, :], (bank_a, bank_s)[i][:, :], ACT.Identity,
                                     bias=K["bA"][:, i:i + 1]).then_inc(S["lat_ev"], 1)
                act.wait_ge(S["lat_ev"], g * 2 + i + 1)
                nc.scalar.copy(lat_h[:, i, :], lat32[:, i, :]).then_inc(S["lat_hi"], 1)

            def kv_tokens(g):
                act.wait_ge(S["kvt_mm"], g + 1)
                nc.scalar.copy(kv_tok[:, :, :], bank_b[:, :].rearrange("p (n l) -> p n l", n=NPAIR)
                               ).then_inc(S["kvt_ev"], 1)

            def rope_raw(r, ready, count, source, bias, first=False):
                act.wait_ge(ready, count)
                if not first:
                    act.wait_ge(S["swap_ev"], r)
                    act.wait_ge(S["cos_ev"], r)
                nc.scalar.activation(raw[:, :], source[:, :], ACT.Identity, bias=bias).then_inc(S["raw_ev"], 1)

            def q_rope_raw(g, u):
                rope_raw(g * NR + 1 + u, S["qc_mm"], g * NU + u + 1, bank_a, K["bC"][:, u:u + 1])

            def q_nope_evac(g, u, h):
                act.wait_ge(S[f"qn{h}_mm"], g * NU + u + 1)
                nc.scalar.copy(q_nope[:, :, h, :], (bank_b, bank_d)[h][:, :].rearrange("p (b t) -> p b t", b=GB)
                               ).then_inc(S[f"qn{h}_ev"], 1)

            def prob_transposed(g, u):
                act.wait_ge(S["pt_mm"], g * NU + u + 1)
                nc.scalar.copy(probT[:, :, :], bank_a[:, :].rearrange("p (n q) -> p n q", n=NPAIR)
                               ).then_inc(S["pt_ev"], 1)

            def mix_hi(g, u):
                for j, (k, bk) in enumerate((("mixe", bank_b), ("mixo", bank_d))):
                    act.wait_ge(S[k + "_mm"], g * NU + u + 1)
                    nc.scalar.copy(mix_h[:, u % 2, :, :, j, :].rearrange("p h n t -> p n h t"),
                                   bk[:, :].rearrange("p (n h t) -> p n h t", n=NPAIR, h=2)
                                   ).then_inc(S[k + "_hi"], 1)

            def first():
                bias_evac(0)
                for c in range(TC):
                    cond_hi(0, c)
                latent(0, 0)
                latent(0, 1)
                kv_tokens(0)
                rope_raw(0, S["kb_mm"], 1, bank_d, K["bB"][:, 0:1], first=True)

            def body(g, more):
                q_rope_raw(g, 0)
                for h in range(2):
                    q_nope_evac(g, 0, h)
                for u in range(NU):
                    if u + 1 < NU:
                        q_rope_raw(g, u + 1)
                    act.wait_ge(S["sub_ev"], g * NU + u + 1)
                    nc.scalar.activation(prob[:, u % 2, :, :], score[:, :, :], ACT.Exp).then_inc(S["exp_ev"], 1)
                    if u + 1 < NU:
                        q_nope_evac(g, u + 1, 0)
                    if u >= 1:
                        prob_transposed(g, u - 1)
                    if u + 1 < NU:
                        q_nope_evac(g, u + 1, 1)
                    if u >= 1:
                        mix_hi(g, u - 1)
                if more:
                    bias_evac(g + 1)
                prob_transposed(g, NU - 1)
                if more:
                    cond_hi(g + 1, 0)
                mix_hi(g, NU - 1)
                if more:
                    for c in range(1, TC):
                        cond_hi(g + 1, c)
                    latent(g + 1, 0)
                    latent(g + 1, 1)
                    kv_tokens(g + 1)
                    rope_raw((g + 1) * NR, S["kb_mm"], g + 2, bank_d, K["bB"][:, 0:1])

            over_groups(act, first, body)

        @block.vector
        def _(dve):
            COND_BANK = (bank_d, bank_s, bank_a, bank_s)

            def group_inputs(g):
                for j in range(GB):
                    h, n = j % 2, j // 2
                    rows = slice(h * C, (h + 1) * C)
                    s = dve.value_load(K["subj"][0:1, bass.ds(g * GB + j, 1)], min_val=0, max_val=NSUB - 1)
                    nc.vector.tensor_copy(K["wblk"][rows, n, rows], K["wsub"][rows, bass.ds(s, 1), :].squeeze(1)
                                          ).then_inc(S["wblk_ready"], 1)

            def cond_evac(g, c, first=False):
                dve.wait_ge(S["bias_ev"], g + 1)
                dve.wait_ge(S["cond_mm"], g * TC + c + 1)
                if not first or c >= 2:
                    dve.wait_ge(S["cond_lo"], g * TC + c - 1)
                nc.vector.tensor_tensor(cond32[c % 2][:, :], COND_BANK[c][:, :], bias_bc[:, :],
                                        ALU.add).then_inc(S["cond_ev"], 1)

            def latent_lo(g, i):
                dve.wait_ge(S["lat_hi"], g * 2 + i + 1)
                nc.vector.tensor_tensor(lat_l[:, i, :], lat32[:, i, :], lat_h[:, i, :].bitcast(F32),
                                        ALU.subtract).then_inc(S["lat_lo"], 1)

            def rope_swap(r, first=False):
                dve.wait_ge(S["raw_ev"], r + 1)
                if not first:
                    dve.wait_ge(S["sin_ev"], r)
                nc.vector.memset(wait_here[:, :], 0.0)
                nc.vector.stream_shuffle(swapped[:, :], raw[:, :], [i ^ 1 for i in range(32)]
                                         ).then_inc(S["swap_ev"], 1)

            def rope_add_keys(r):
                dve.wait_ge(S["sin_ev"], r + 1)
                nc.vector.tensor_tensor(k_rope[:, :], by_cos[:, :], by_sin[:, :], ALU.add).then_inc(S["rope_done"], 1)

            def rope_add_queries(r):
                dve.wait_ge(S["sin_ev"], r + 1)
                for h in range(2):
                    rows = slice(h * DR, (h + 1) * DR)
                    last = nc.vector.tensor_tensor(q_rope[rows, :, h, :],
                                                   by_cos[rows, :].rearrange("p (b t) -> p b t", b=GB),
                                                   by_sin[rows, :].rearrange("p (b t) -> p b t", b=GB), ALU.add)
                last.then_inc(S["rope_done"], 1)

            def mix_lo(g, u):
                for j, (k, bk) in enumerate((("mixe", bank_b), ("mixo", bank_d))):
                    view = mix_h[:, u % 2, :, :, j, :].rearrange("p h n t -> p n h t")
                    dve.wait_ge(S[k + "_hi"], g * NU + u + 1)
                    nc.vector.tensor_tensor(mix_l[:, u % 2, :, :, j, :].rearrange("p h n t -> p n h t"),
                                            bk[:, :].rearrange("p (n h t) -> p n h t", n=NPAIR, h=2),
                                            view.bitcast(F32), ALU.subtract).then_inc(S[k + "_lo"], 1)

            def per_batch(row):
                return row[:, :].unsqueeze(2).to_broadcast([P, GB, C])

            def softmax_in(g, u):
                n = g * NU + u + 1
                dve.wait_ge(S["score_mm"], n)
                if u:
                    dve.wait_ge(S["exp_ev"], n - 1)
                nc.vector.scalar_tensor_tensor(out=score[:, :, :],
                                               in0=bank_s[:, :].rearrange("p (b t) -> p b t", b=GB), scalar=SCALE,
                                               in1=K.parts["mask"].unsqueeze(1).to_broadcast([P, GB, C]),
                                               op0=ALU.mult, op1=ALU.add).then_inc(S["score_ev"], 1)
                dve.wait_ge(S["score_ev"], n)
                nc.vector.tensor_reduce(rmax[:, :], score[:, :, :], AX, ALU.max).then_inc(S["max_ev"], 1)
                dve.wait_ge(S["max_ev"], n)
                nc.vector.tensor_tensor(score[:, :, :], score[:, :, :], per_batch(rmax),
                                        ALU.subtract).then_inc(S["sub_ev"], 1)

            def softmax_sum(g, u):
                n = g * NU + u + 1
                dve.wait_ge(S["exp_ev"], n)
                nc.vector.tensor_reduce(rsum[:, :], prob[:, u % 2, :, :], AX, ALU.add).then_inc(S["sum_ev"], 1)
                dve.wait_ge(S["sum_ev"], n)
                if u:
                    dve.wait_ge(S["prob_ev"], n - 1)
                nc.vector.reciprocal(rinv[:, :], rsum[:, :]).then_inc(S["inv_ev"], 1)

            def first():
                group_inputs(0)
                for c in range(TC):
                    cond_evac(0, c, first=True)
                latent_lo(0, 0)
                latent_lo(0, 1)
                rope_swap(0, first=True)
                rope_add_keys(0)

            def body(g, more):
                r0 = g * NR + 1
                rope_swap(r0)
                rope_add_queries(r0)
                for u in range(NU):
                    softmax_in(g, u)
                    if u + 1 < NU:
                        rope_swap(r0 + u + 1)
                    softmax_sum(g, u)
                    if u + 1 < NU:
                        rope_add_queries(r0 + u + 1)
                    if u >= 1:
                        mix_lo(g, u - 1)
                    if u == 1 and more:
                        dve.wait_ge(S["cond_mm"], g * TC + TC)
                        group_inputs(g + 1)
                if more:
                    cond_evac(g + 1, 0)
                mix_lo(g, NU - 1)
                if more:
                    for c in range(1, TC):
                        cond_evac(g + 1, c)
                    latent_lo(g + 1, 0)
                    latent_lo(g + 1, 1)
                    rope_swap((g + 1) * NR)
                    rope_add_keys((g + 1) * NR)
                dve.wait_ge(S["xres_biased"], g + 1)
                for t in range(NPAIR):
                    dve.wait_ge(S["wz_mm"], g * NPAIR + t + 1)
                    nc.vector.tensor_tensor(x_res[:, t, :], bank_o[t][:, :], x_res[:, t, :],
                                            ALU.add).then_inc(S["x2_ev"], 1)

            over_groups(dve, first, body)

        @block.tensor
        def _(pe):
            def wz(g, u, t):
                if t == 0:
                    pe.wait_ge(S["mixe_lo"], g * NU + u + 1)
                    pe.wait_ge(S["mixo_lo"], g * NU + u + 1)
                pairs = [((mix_h[:, u % 2, h, t, :, :].rearrange("p j t -> p (j t)"),
                           mix_l[:, u % 2, h, t, :, :].rearrange("p j t -> p (j t)")),
                          (W["Mh"][:, 2 * u + h, :], W["Ml"][:, 2 * u + h, :])) for h in range(2)]
                last = split_product(nc, bank_o[t][:, :], pairs, start=u == 0, stop=u == NU - 1)
                if u == NU - 1:
                    last.then_inc(S["wz_mm"], 1)

            def bias_rows(g):
                pe.wait_ge(S["bias_sel_ready"], g + 1)
                nc.tensor.matmul(bank_s[:, :], K.parts["ones"][0:NSUB, :], bias_sel[:, :, :].rearrange("n b d -> n (b d)"),
                                 start=True, stop=True).then_inc(S["bias_mm"], 1)

            def cond(g, c, bk):
                if c == 0:
                    pe.wait_ge(S["x_in"], g * 16 + 16)
                    pe.wait_ge(S["wblk_ready"], g * GB + GB)
                for n in range(NPAIR):
                    last = nc.tensor.matmul(bk[:, n * P:(n + 1) * P], x_cond[:, n, c * P:(c + 1) * P],
                                            K["wblk"][:, n, :], start=True, stop=True)
                last.then_inc(S["cond_mm"], 1)

            def latent(g, i, bk):
                pe.wait_ge(S["cond_lo"], g * TC + TC)
                split_product(nc, bk[:, :], [((W["WAh"][:, c, i * L:(i + 1) * L], W["WAl"][:, c, i * L:(i + 1) * L]),
                                              (cond_h[:, c, :], cond_l[:, c, :])) for c in range(TC)]
                              ).then_inc(S["lat_mm"], 1)

            def kv_tokens(g):
                pe.wait_ge(S["lat_ev"], g * 2 + 1)
                for n in range(NPAIR):
                    last = nc.tensor.transpose(bank_b[:, n * P:(n + 1) * P], lat32[:, 0, n * P:(n + 1) * P], K.parts["ident"])
                last.then_inc(S["kvt_mm"], 1)

            def rope_keys(g):
                pe.wait_ge(S["lat_lo"], g * 2 + 2)
                split_product(nc, bank_d[:, :], [((W["WBh"][:, i, :, :].rearrange("p j d -> p (j d)"),
                                                   W["WBl"][:, i, :, :].rearrange("p j d -> p (j d)")),
                                                  (lat_h[:, i, :], lat_l[:, i, :])) for i in range(2)]
                              ).then_inc(S["kb_mm"], 1)

            def q_rope_mm(g, u):
                cols = slice(u * P, (u + 1) * P)
                split_product(nc, bank_a[:, :], [((W["WCh"][:, i, cols], W["WCl"][:, i, cols]),
                                                  (lat_h[:, i, :], lat_l[:, i, :])) for i in range(2)]
                              ).then_inc(S["qc_mm"], 1)

            def q_nope_mm(g, u, h):
                cols = slice((2 * u + h) * P, (2 * u + h + 1) * P)
                split_product(nc, (bank_b, bank_d)[h][:, :], [((W["Ah"][:, cols], W["Al"][:, cols]),
                                                               (lat_h[:, 1, :], lat_l[:, 1, :]))]
                              ).then_inc(S[f"qn{h}_mm"], 1)

            def scores(g, u):
                pe.wait_ge(S["qn0_ev"], g * NU + u + 1)
                pe.wait_ge(S["qn1_ev"], g * NU + u + 1)
                pe.wait_ge(S["rope_done"], g * NR + u + 2)
                if u:
                    pe.wait_ge(S["score_ev"], g * NU + u)
                for b in range(GB):
                    cols = slice(b * C, (b + 1) * C)
                    nc.tensor.matmul(bank_s[:, cols], q_nope[:, b, :, :].rearrange("p h t -> p (h t)"),
                                     lat32[:, 0, cols], start=True, stop=False)
                    last = nc.tensor.matmul(bank_s[:, cols], q_rope[:, b, :, :].rearrange("p h t -> p (h t)"),
                                            k_rope[:, cols], start=False, stop=True)
                last.then_inc(S["score_mm"], 1)

            def prob_transpose(g, u):
                pe.wait_ge(S["prob_ev"], g * NU + u + 1)
                for n in range(NPAIR):
                    last = nc.tensor.transpose(bank_a[:, n * P:(n + 1) * P],
                                               prob[:, u % 2, 2 * n:2 * n + 2, :].rearrange("p j k -> p (j k)"),
                                               K.parts["ident"])
                last.then_inc(S["pt_mm"], 1)

            def mix(g, u, j):
                rows = slice(j * C, (j + 1) * C)
                bk = (bank_b, bank_d)[j]
                pe.wait_ge(S["pt_ev"], g * NU + u + 1)
                for n in range(NPAIR):
                    last = nc.tensor.matmul(bk[:, n * P:(n + 1) * P], kv_tok[rows, n, :], probT[rows, n, :],
                                            start=True, stop=True)
                last.then_inc(S[("mixe_mm", "mixo_mm")[j]], 1)

            def first():
                bias_rows(0)
                cond(0, 0, bank_d)
                pe.wait_ge(S["bias_ev"], 1)
                cond(0, 1, bank_s)
                cond(0, 2, bank_a)
                pe.wait_ge(S["cond_ev"], 2)
                cond(0, 3, bank_s)
                latent(0, 0, bank_a)
                latent(0, 1, bank_s)
                kv_tokens(0)
                rope_keys(0)

            def body(g, more):
                pe.wait_ge(S["lat_ev"], g * 2 + 2)
                q_rope_mm(g, 0)
                pe.wait_ge(S["kvt_ev"], g + 1)
                q_nope_mm(g, 0, 0)
                pe.wait_ge(S["raw_ev"], g * NR + 1)
                q_nope_mm(g, 0, 1)
                for u in range(NU):
                    scores(g, u)
                    if u + 1 < NU:
                        pe.wait_ge(S["raw_ev"], g * NR + u + 2)
                        if u >= 2:
                            pe.wait_ge(S["pt_ev"], g * NU + u - 1)
                        q_rope_mm(g, u + 1)
                    if u >= 2:
                        wz(g, u - 2, 0)
                    if u + 1 < NU:
                        if u >= 2:
                            pe.wait_ge(S["mixe_lo"], g * NU + u - 1)
                        q_nope_mm(g, u + 1, 0)
                    if u >= 1:
                        if u + 1 < NU:
                            pe.wait_ge(S["raw_ev"], g * NR + u + 3)
                        else:
                            pe.wait_ge(S["pt_ev"], g * NU + u - 1)
                        prob_transpose(g, u - 1)
                    if u + 1 < NU:
                        if u >= 2:
                            pe.wait_ge(S["mixo_lo"], g * NU + u - 1)
                        q_nope_mm(g, u + 1, 1)
                    if u >= 2:
                        wz(g, u - 2, 1)
                    if u >= 1:
                        if u + 1 < NU:
                            pe.wait_ge(S["qn0_ev"], g * NU + u + 2)
                        else:
                            pe.wait_ge(S["mixe_lo"], g * NU + u - 1)
                        mix(g, u - 1, 0)
                        if u + 1 < NU:
                            pe.wait_ge(S["qn1_ev"], g * NU + u + 2)
                        else:
                            pe.wait_ge(S["mixo_lo"], g * NU + u - 1)
                        mix(g, u - 1, 1)
                    if u >= 2:
                        wz(g, u - 2, 2)
                        wz(g, u - 2, 3)
                n = g * NU + NU
                g1 = g + 1
                pe.wait_ge(S["score_ev"], n)
                if more:
                    bias_rows(g1)
                wz(g, NU - 2, 0)
                pe.wait_ge(S["pt_ev"], n - 1)
                prob_transpose(g, NU - 1)
                pe.wait_ge(S["mixo_lo"], n - 1)
                if more:
                    cond(g1, 0, bank_d)
                wz(g, NU - 2, 1)
                pe.wait_ge(S["mixe_lo"], n - 1)
                mix(g, NU - 1, 0)
                if more:
                    pe.wait_ge(S["cond_ev"], g1 * TC + 1)
                mix(g, NU - 1, 1)
                if more:
                    pe.wait_ge(S["bias_ev"], g1 + 1)
                    cond(g1, 1, bank_s)
                    pe.wait_ge(S["pt_ev"], n)
                    cond(g1, 2, bank_a)
                wz(g, NU - 2, 2)
                if more:
                    pe.wait_ge(S["cond_ev"], g1 * TC + 2)
                    cond(g1, 3, bank_s)
                wz(g, NU - 2, 3)
                wz(g, NU - 1, 0)
                if more:
                    latent(g1, 0, bank_a)
                wz(g, NU - 1, 1)
                if more:
                    latent(g1, 1, bank_s)
                wz(g, NU - 1, 2)
                if more:
                    kv_tokens(g1)
                wz(g, NU - 1, 3)
                if more:
                    rope_keys(g1)

            over_groups(pe, first, body)


EARLY = 4
SLOTS = NG - EARLY


def slot_of(g):
    return g % 2 if g < EARLY + 2 else g - EARLY


def routing(nc, K, A, x2, flat, R):
    with ExitStack() as ctx:
        def sb(name, shape, dt=F32):
            return ctx.enter_context(nc.sbuf_tensor(name, shape, dt))

        def bank(name):
            return ctx.enter_context(nc.psum_tensor(name, [P, 512], F32))

        def sem(name):
            return ctx.enter_context(nc.semaphore(name))

        NR = NADAPT * RANK
        EJ = NE * NT
        load_table(nc, ctx, K, "route")
        c = K.parts
        w_raw = sb("w_raw", [P, TC, T])
        a_raw = sb("a_raw", [NR, T])
        b_raw = sb("b_raw", [P, TC, NADAPT, RANK])
        wg = sb("wg", [P, TC, NE])
        bg = sb("bg", [P, NE])
        adapt, scal = sb("adapt", [P, B], I32), sb("scal", [P, 1])
        lora_sel = sb("lora_sel", [P, B])
        WTh, WTl = sb("WTh", [P, TC, T], F32R), sb("WTl", [P, TC, T], F32R)
        ATh, ATl = sb("ATh", [P, TC, NR], F32R), sb("ATl", [P, TC, NR], F32R)
        BTh, BTl = sb("BTh", [NR, T], F32R), sb("BTl", [NR, T], F32R)
        WGh, WGl = sb("WGh", [P, TC + 1, NE], F32R), sb("WGl", [P, TC + 1, NE], F32R)
        x_in_sb = sb("x_in_sb", [P, 2, NPAIR, T])
        xTh, xTl = sb("xTh", [P, SLOTS, TC, GT], F32R), sb("xTl", [P, SLOTS, TC, GT], F32R)
        low32 = sb("low32", [NR, GT])
        lowh, lowl = sb("lowh", [NR, SLOTS, GT], F32R), sb("lowl", [NR, SLOTS, GT], F32R)
        flat_sb = sb("flat_sb", [P, 4, T])
        logit = sb("logit", [P, NT, NE])
        bank_t = [bank(f"r_t{i}") for i in range(TC)]
        bank_x, bank_l, bank_f = bank("r_x"), bank("r_l"), [bank("r_f0"), bank("r_f1")]

        cmpk = sb("cmpk", [P, NE, NT, NE])
        rank, top = sb("rank", [P, NT, NE]), sb("top", [P, NT, NE])
        lmax = sb("lmax", [P, NT])
        ex, ey, ek, ep, e2 = (sb(n, [P, NT, NE]) for n in ("ex", "ey", "ek", "ep", "e2"))
        ei = sb("ei", [P, NT, NE], I32)
        esum, einv = sb("esum", [P, NT]), sb("einv", [P, NT])
        gate, key = sb("gate", [P, NE, NT]), sb("key", [P, NE, NT])
        thr = sb("thr", [P, NE], I32)
        cand = sb("cand", [P, NE, 3], I32)
        above = sb("above", [P, NE, 3, NT])
        count = sb("count", [P, NE, 3])
        hit = sb("hit", [P, NE, 3])
        step_bits = sb("step_bits", [P, NE], I32)
        positive = sb("positive", [P, NE])
        thrf = sb("thrf", [P, NE])
        over, same = sb("over", [P, NE, NT]), sb("same", [P, NE, NT])
        need = sb("need", [P, NE])
        mark = sb("mark", [P, NE, NT], BF16)
        ones_b, before_b = sb("ones_b", [P, P], BF16), sb("before_b", [P, P], BF16)
        iota_b = sb("iota_b", [P, P], BF16)
        chosen = sb("chosen", [P, NE, NT])
        pos = sb("pos", [P, NE, NT], I32)
        pos_lo, pos_hi = sb("pos_lo", [P, NE, NT], I32), sb("pos_hi", [P, NE, NT], I32)
        slot_lo, slot_hi = sb("slot_lo", [P, NE, NT]), sb("slot_hi", [P, NE, NT])
        part3 = sb("part3", [P, 3, NE, NT], BF16)
        rest = sb("rest", [P, 2, NE, NT])
        is_hi = sb("is_hi", [P, EJ, NCH], BF16)
        NV = 5
        value = sb("value", [P, EJ, NV], BF16)
        row = sb("row", [P, EJ, NV, NCH], BF16)
        is_lo = sb("is_lo", [P, 4, P], BF16)
        listed = sb("listed", [P, NV, NCH])
        tokf = sb("tokf", [P, NCH])

        names = """w_in a_in wt_mm wt_hi wt_lo at_mm at_hi at_lo bt_mm bt_hi bt_lo wg_mm wg_hi wg_lo sel_ready
            xt_mm xt_hi xt_lo low_mm low_ev low_hi low_lo lg_mm lg_ev fl_mm fl_ev
            chain count_ready count_mm prefix_ready prefix_mm lo_ready list_mm list_ev table_in""".split()
        S = {n: sem("rt_" + n) for n in names}
        x_in = [sem(f"rt_x_in{k}") for k in range(2)]
        fl_out = [sem(f"rt_fl_out{k}") for k in range(4)]
        x_d = x2.rearrange("(g n j) c t -> g (j c) n t", n=NPAIR, j=2)
        flat_d = flat.rearrange("(n p) t -> n p t", p=P)

        block = ctx.enter_context(nc.Block())

        @block.sync
        def _(sp):
            sp.dma_start(w_raw[:, :, :], A["W"].rearrange("(c p) n -> p c n", p=P)).then_inc(S["w_in"], 16)
            sp.dma_start(a_raw[:, :], A["A"].rearrange("n r d -> (n r) d")).then_inc(S["w_in"], 16)
            for g in range(2):
                sp.dma_start(x_in_sb[:, g, :, :], x_d[g]).then_inc(x_in[g], 16)
            with nc.allow_non_contiguous_dma(reason="small operands, once"):
                for i in range(TC):
                    sp.dma_start(b_raw[:, i, :, :], A["Bm"][:, i * P:(i + 1) * P, :].rearrange("n p r -> p n r")
                                 ).then_inc(S["a_in"], 16)
                sp.dma_start(wg[:, :, :], A["Wg"].rearrange("(c p) e -> p c e", p=P)).then_inc(S["a_in"], 16)
                sp.dma_start(bg[:, :], A["bg"].partition_broadcast(P)).then_inc(S["a_in"], 16)
                sp.dma_start(adapt[:, :], A["adapt"].partition_broadcast(P)).then_inc(S["a_in"], 16)
                for n in range(NADAPT):
                    sp.dma_start(scal[n * RANK:(n + 1) * RANK, :],
                                 A["scalings"][n:n + 1].partition_broadcast(RANK)).then_inc(S["a_in"], 16)
            sp.dma_start(K["route"][:, :], A["route"]).then_inc(S["table_in"], 16)
            for g in range(2, NG):
                sp.wait_ge(S["xt_mm"], (g - 1) * TC)
                sp.dma_start(x_in_sb[:, g % 2, :, :], x_d[g]).then_inc(x_in[g % 2], 16)

        A_IN = 16 * (TC + 3 + NADAPT)

        @block.gpsimd
        def _(pool):
            def store(n, k):
                pool.wait_ge(S["fl_ev"], n + 1)
                pool.dma_start(flat_d[n], flat_sb[:, k, :]).then_inc(fl_out[k], 16)

            for n in range(NT):
                store(n, n % 4)
            for k in range(4):
                pool.wait_ge(fl_out[k], 16 * (NT // 4))

        @block.scalar
        def _(act):
            def copy(out, bk, ready, count, done):
                act.wait_ge(S[ready], count)
                nc.scalar.copy(out, bk).then_inc(S[done], 1)

            for i in range(TC):
                copy(WTh[:, i, :], bank_t[i][:, :], "wt_mm", i + 1, "wt_hi")
            copy(ATh[:, :, :], bank_x[:, :].rearrange("p (c n) -> p c n", c=TC), "at_mm", 1, "at_hi")
            copy(BTh[:, :], bank_f[0][:, :], "bt_mm", 1, "bt_hi")
            copy(WGh[:, :, :], bank_l[:, 0:(TC + 1) * NE].rearrange("p (c e) -> p c e", e=NE), "wg_mm", 1, "wg_hi")

            def front(g):
                s = slot_of(g)
                for i in range(TC):
                    copy(xTh[:, s, i, :], bank_t[i][:, :], "xt_mm", g * TC + i + 1, "xt_hi")
                act.wait_ge(S["low_ev"], g + 1)
                nc.scalar.copy(lowh[:, s, :], low32[:, :]).then_inc(S["low_hi"], 1)

            def back(g):
                for t in range(NPAIR):
                    n = g * NPAIR + t
                    act.wait_ge(S["fl_mm"], n + 1)
                    if n >= 4:
                        act.wait_ge(fl_out[n % 4], 16 * (n // 4))
                    nc.scalar.copy(flat_sb[:, n % 4, :], bank_f[n % 2][:, :]).then_inc(S["fl_ev"], 1)

            front(0)
            for g in range(EARLY):
                front(g + 1)
                back(g)
            for g in range(EARLY + 1, NG):
                front(g)
            for g in range(EARLY, NG):
                back(g)

        @block.vector
        def _(dve):
            v = nc.vector
            steps = [0]

            def link(instruction):
                steps[0] += 1
                instruction.then_inc(S["chain"], 1)
                dve.wait_ge(S["chain"], steps[0])

            def low_part(out, bk, hi, ready, count, done):
                dve.wait_ge(S[ready], count)
                v.tensor_tensor(out, bk, hi.bitcast(F32), ALU.subtract).then_inc(S[done], 1)

            for i in range(TC):
                low_part(WTl[:, i, :], bank_t[i][:, :], WTh[:, i, :], "wt_hi", i + 1, "wt_lo")
            low_part(ATl[:, :, :], bank_x[:, :].rearrange("p (c n) -> p c n", c=TC), ATh[:, :, :], "at_hi", 1, "at_lo")
            low_part(BTl[:, :], bank_f[0][:, :], BTh[:, :], "bt_hi", 1, "bt_lo")
            low_part(WGl[:, :, :], bank_l[:, 0:(TC + 1) * NE].rearrange("p (c e) -> p c e", e=NE), WGh[:, :, :],
                     "wg_hi", 1, "wg_lo")
            dve.wait_ge(S["a_in"], A_IN)
            dve.wait_ge(S["table_in"], 16)
            link(v.tensor_scalar(lora_sel[:, :], adapt[:, :], c["adapter"], None, ALU.is_equal))
            link(v.tensor_scalar(lora_sel[:, :], lora_sel[:, :], scal[:, :], None, ALU.mult))

            def front(g):
                s = slot_of(g)
                for i in range(TC):
                    low_part(xTl[:, s, i, :], bank_t[i][:, :], xTh[:, s, i, :], "xt_hi", g * TC + i + 1, "xt_lo")
                dve.wait_ge(S["low_mm"], g + 1)
                v.tensor_tensor(low32[:, :].rearrange("p (b t) -> p b t", b=GB),
                                bank_x[:, :].rearrange("p (b t) -> p b t", b=GB),
                                lora_sel[:, g * GB:(g + 1) * GB].unsqueeze(2).to_broadcast([NR, GB, C]),
                                ALU.mult).then_inc(S["low_ev"], 1)
                dve.wait_ge(S["low_hi"], g + 1)
                v.tensor_tensor(lowl[:, s, :], low32[:, :], lowh[:, s, :].bitcast(F32),
                                ALU.subtract).then_inc(S["low_lo"], 1)

            def logits_out(g):
                dve.wait_ge(S["lg_mm"], g + 1)
                v.tensor_tensor(logit[:, g * NPAIR:(g + 1) * NPAIR, :],
                                bank_l[:, 0:NPAIR * NE].rearrange("p (t e) -> p t e", e=NE),
                                bg[:, :].unsqueeze(1).to_broadcast([P, NPAIR, NE]), ALU.add).then_inc(S["lg_ev"], 1)

            for g in range(NG):
                front(g)
                if g:
                    logits_out(g - 1)
            logits_out(NG - 1)
            dve.wait_ge(S["lg_ev"], NG)

            link(v.memset(cmpk[:, :, :, :], 0.0))
            for k in range(NE):
                one = logit[:, :, k:k + 1]
                if k + 1 < NE:
                    v.tensor_tensor(cmpk[:, k, :, k + 1:NE], one.to_broadcast([P, NT, NE - 1 - k]),
                                    logit[:, :, k + 1:NE], ALU.is_ge)
                if k:
                    v.tensor_tensor(cmpk[:, k, :, 0:k], one.to_broadcast([P, NT, k]), logit[:, :, 0:k], ALU.is_gt)
            link(v.tensor_reduce(lmax[:, :], logit[:, :, :], AX, ALU.max))
            link(v.tensor_reduce(rank[:, :, :], cmpk[:, :, :, :].rearrange("p k j e -> p j e k"), AX, ALU.add))
            link(v.tensor_scalar(top[:, :, :], rank[:, :, :], 1.5, None, ALU.is_lt))

            link(v.tensor_tensor(ex[:, :, :], logit[:, :, :], lmax[:, :].unsqueeze(2).to_broadcast([P, NT, NE]),
                                 ALU.subtract))
            link(v.tensor_scalar(ex[:, :, :], ex[:, :, :], -87.0, None, ALU.max))
            link(v.tensor_scalar(ey[:, :, :], ex[:, :, :], float(np.float32(np.log2(np.e))), 12582912.0,
                                 ALU.mult, ALU.add))
            link(v.tensor_scalar(ek[:, :, :], ey[:, :, :], 12582912.0, None, ALU.subtract))
            link(v.scalar_tensor_tensor(out=ex[:, :, :], in0=ek[:, :, :], scalar=-0.693359375, in1=ex[:, :, :],
                                        op0=ALU.mult, op1=ALU.add))
            link(v.scalar_tensor_tensor(out=ex[:, :, :], in0=ek[:, :, :], scalar=2.12194440e-4, in1=ex[:, :, :],
                                        op0=ALU.mult, op1=ALU.add))
            coefficients = [1.0 / n for n in (5040.0, 720.0, 120.0, 24.0, 6.0, 2.0, 1.0)]
            link(v.tensor_scalar(ep[:, :, :], ex[:, :, :], coefficients[0], None, ALU.mult))
            for k in coefficients[1:]:
                link(v.scalar_tensor_tensor(out=ep[:, :, :], in0=ep[:, :, :], scalar=k, in1=ex[:, :, :],
                                            op0=ALU.add, op1=ALU.mult))
            link(v.tensor_scalar(ei[:, :, :], ek[:, :, :], 127.0, 8388608.0, ALU.add, ALU.mult))
            link(v.scalar_tensor_tensor(out=e2[:, :, :], in0=ep[:, :, :], scalar=1.0,
                                        in1=ei[:, :, :].bitcast(F32), op0=ALU.add, op1=ALU.mult))
            link(v.tensor_tensor(e2[:, :, :], e2[:, :, :], top[:, :, :], ALU.mult))
            link(v.tensor_reduce(esum[:, :], e2[:, :, :], AX, ALU.add))
            link(v.reciprocal(einv[:, :], esum[:, :]))
            link(v.tensor_tensor(gate[:, :, :].rearrange("p e j -> p j e"), e2[:, :, :],
                                 einv[:, :].unsqueeze(2).to_broadcast([P, NT, NE]), ALU.mult))
            link(v.scalar_tensor_tensor(out=key[:, :, :].rearrange("p e j -> p j e"), in0=top[:, :, :], scalar=-1.0,
                                        in1=gate[:, :, :].rearrange("p e j -> p j e"), op0=ALU.add, op1=ALU.add))

            counts = [0]

            def total(mask, width):
                link(v.tensor_reduce(count[:, :, 0:width], mask, AX, ALU.add))
                counts[0] += 1
                v.tensor_copy(hit[:, :, 0:width], count[:, :, 0:width]).then_inc(S["count_ready"], 1)
                dve.wait_ge(S["count_mm"], counts[0])

            totals = bank_l[:, 0:NE * 3].rearrange("p (e c) -> p e c", c=3)
            link(v.memset(hit[:, :, :], 0.0))
            link(v.tensor_scalar(above[:, :, 0, :], key[:, :, :], 0.0, None, ALU.is_ge))
            total(above[:, :, 0:1, :], 1)
            link(v.tensor_scalar(positive[:, :].unsqueeze(2), totals[:, :, 0:1], float(CAP), None, ALU.is_ge))
            link(v.memset(thr[:, :], 0))
            for i in range(TRIALS):
                trial = c["trial"][:, 3 * i:3 * i + 3].bitcast(I32)
                link(v.tensor_tensor(cand[:, :, :], thr[:, :].unsqueeze(2).to_broadcast([P, NE, 3]),
                                     trial.unsqueeze(1).to_broadcast([P, NE, 3]), ALU.bitwise_or))
                link(v.tensor_tensor(above[:, :, :, :], key[:, :, :].unsqueeze(2).to_broadcast([P, NE, 3, NT]),
                                     cand[:, :, :].bitcast(F32).unsqueeze(3).to_broadcast([P, NE, 3, NT]),
                                     ALU.is_ge))
                total(above[:, :, :, :], 3)
                link(v.tensor_scalar(hit[:, :, :], totals, float(CAP), float(1 << (2 * (TRIALS - 1 - i))),
                                     ALU.is_ge, ALU.mult))
                with nc.allow_low_precision(reason="at most three equal powers of two: exact"):
                    link(v.tensor_reduce(step_bits[:, :], hit[:, :, :], AX, ALU.add))
                link(v.tensor_tensor(thr[:, :], thr[:, :], step_bits[:, :], ALU.bitwise_or))
            link(v.tensor_tensor(thrf[:, :], thr[:, :].bitcast(F32), positive[:, :], ALU.mult))
            link(v.scalar_tensor_tensor(out=thrf[:, :], in0=positive[:, :], scalar=-1.0, in1=thrf[:, :],
                                        op0=ALU.add, op1=ALU.add))

            limit = thrf[:, :].unsqueeze(2).to_broadcast([P, NE, NT])
            link(v.tensor_tensor(over[:, :, :], key[:, :, :], limit, ALU.is_gt))
            link(v.tensor_tensor(same[:, :, :], key[:, :, :], limit, ALU.is_equal))
            total(over[:, :, :].unsqueeze(2), 1)
            link(v.tensor_scalar(need[:, :].unsqueeze(2), totals[:, :, 0:1], -1.0, float(CAP), ALU.mult, ALU.add))
            link(v.tensor_copy(ones_b[:, :], c["ones"]))
            link(v.tensor_copy(before_b[:, :], c["before"]))
            link(v.tensor_copy(iota_b[:, :], c["iota"]))
            earlier = bank_x[:, 0:EJ].rearrange("p (e j) -> p e j", e=NE)
            v.tensor_copy(mark[:, :, :], same[:, :, :]).then_inc(S["prefix_ready"], 1)
            dve.wait_ge(S["prefix_mm"], 1)
            link(v.tensor_tensor(chosen[:, :, :], earlier, need[:, :].unsqueeze(2).to_broadcast([P, NE, NT]),
                                 ALU.is_lt))
            link(v.tensor_tensor(chosen[:, :, :], chosen[:, :, :], same[:, :, :], ALU.mult))
            link(v.tensor_tensor(chosen[:, :, :], chosen[:, :, :], over[:, :, :], ALU.add))
            v.tensor_copy(mark[:, :, :], chosen[:, :, :]).then_inc(S["prefix_ready"], 1)
            val = value[:, :, :].rearrange("p (e j) v -> p e j v", e=NE)
            v.tensor_copy(val[:, :, :, 0], c["tile"].unsqueeze(1).to_broadcast([P, NE, NT]))
            v.tensor_copy(val[:, :, :, 1], c["part"].unsqueeze(2).to_broadcast([P, NE, NT]))
            link(v.tensor_copy(part3[:, 0, :, :], gate[:, :, :]))
            link(v.tensor_tensor(rest[:, 0, :, :], gate[:, :, :], part3[:, 0, :, :], ALU.subtract))
            link(v.tensor_copy(part3[:, 1, :, :], rest[:, 0, :, :]))
            link(v.tensor_tensor(rest[:, 1, :, :], rest[:, 0, :, :], part3[:, 1, :, :], ALU.subtract))
            link(v.tensor_copy(part3[:, 2, :, :], rest[:, 1, :, :]))
            for k in range(3):
                link(v.tensor_copy(val[:, :, :, 2 + k], part3[:, k, :, :]))
            dve.wait_ge(S["prefix_mm"], 2)
            link(v.scalar_tensor_tensor(out=rest[:, 0, :, :], in0=earlier, scalar=1.0, in1=chosen[:, :, :],
                                        op0=ALU.add, op1=ALU.mult))
            link(v.tensor_scalar(pos[:, :, :], rest[:, 0, :, :], 1.0, None, ALU.subtract))
            v.tensor_scalar(pos_lo[:, :, :], pos[:, :, :], P - 1, None, ALU.bitwise_and)
            link(v.tensor_scalar(pos_hi[:, :, :], pos[:, :, :], 7, None, ALU.arith_shift_right))
            link(v.tensor_copy(slot_lo[:, :, :], pos_lo[:, :, :]))
            link(v.tensor_copy(slot_hi[:, :, :], pos_hi[:, :, :]))
            link(v.tensor_tensor(is_hi[:, :, :],
                                 slot_hi[:, :, :].rearrange("p e j -> p (e j)").unsqueeze(2).to_broadcast([P, EJ, NCH]),
                                 c["iota"][:, 0:NCH].unsqueeze(1).to_broadcast([P, EJ, NCH]), ALU.is_equal))
            for e in range(NE):
                mine = slice(e * NT, (e + 1) * NT)
                link(v.tensor_tensor(row[:, mine, :, :], is_hi[:, mine, :].unsqueeze(2).to_broadcast([P, NT, NV, NCH]),
                                     value[:, mine, :].unsqueeze(3).to_broadcast([P, NT, NV, NCH]), ALU.mult))
                for j in range(NT):
                    n = e * NT + j
                    if n >= 4:
                        dve.wait_ge(S["list_mm"], n - 3)
                    v.tensor_scalar(is_lo[:, n % 4, :], iota_b[:, :], slot_lo[:, e, j:j + 1], None,
                                    ALU.is_equal).then_inc(S["lo_ready"], 1)
                dve.wait_ge(S["list_mm"], (e + 1) * NT)
                link(v.tensor_copy(listed[:, :, :], bank_l[:, 0:NV * NCH].rearrange("p (v c) -> p v c", v=NV)))
                v.scalar_tensor_tensor(out=R["token"][:, e * NCH:(e + 1) * NCH], in0=listed[:, 0, :], scalar=float(P),
                                       in1=listed[:, 1, :], op0=ALU.mult, op1=ALU.add)
                link(v.tensor_tensor(tokf[:, :], listed[:, 2, :], listed[:, 3, :], ALU.add))
                v.tensor_tensor(R["gate"][:, e * NCH:(e + 1) * NCH], tokf[:, :], listed[:, 4, :], ALU.add).then_inc(S["list_ev"], 1)
                dve.wait_ge(S["list_ev"], e + 1)

        @block.tensor
        def _(pe):
            ident = c["ident"]
            pe.wait_ge(S["w_in"], 32)
            for i in range(TC):
                for o in range(TC):
                    last = nc.tensor.transpose(bank_t[i][:, o * P:(o + 1) * P], w_raw[:, o, i * P:(i + 1) * P], ident)
                last.then_inc(S["wt_mm"], 1)
            for i in range(TC):
                last = nc.tensor.transpose(bank_x[:, i * P:(i + 1) * P], a_raw[:, i * P:(i + 1) * P], ident)
            last.then_inc(S["at_mm"], 1)
            pe.wait_ge(S["a_in"], A_IN)
            for o in range(TC):
                last = nc.tensor.transpose(bank_f[0][:, o * P:(o + 1) * P],
                                           b_raw[:, o, :, :].rearrange("p n r -> p (n r)"), ident)
            last.then_inc(S["bt_mm"], 1)
            for i in range(TC + 1):
                for o in range(TC):
                    left = w_raw[:, o, i * P:(i + 1) * P] if i < TC else b_raw[:, o, :, :].rearrange("p n r -> p (n r)")
                    last = nc.tensor.matmul(bank_l[:, i * NE:(i + 1) * NE], left, wg[:, o, :],
                                            start=o == 0, stop=o == TC - 1)
            last.then_inc(S["wg_mm"], 1)

            def front(g):
                s = slot_of(g)
                pe.wait_ge(x_in[g % 2], 16 * (g // 2 + 1))
                if g:
                    pe.wait_ge(S["xt_lo"], g * TC)
                else:
                    pe.wait_ge(S["wt_lo"], TC)
                for i in range(TC):
                    for t in range(NPAIR):
                        last = nc.tensor.transpose(bank_t[i][:, t * P:(t + 1) * P],
                                                   x_in_sb[:, g % 2, t, i * P:(i + 1) * P], ident)
                    last.then_inc(S["xt_mm"], 1)
                pe.wait_ge(S["at_lo"], 1)
                if g:
                    pe.wait_ge(S["low_ev"], g)
                for i in range(TC):
                    pe.wait_ge(S["xt_lo"], g * TC + i + 1)
                    last = split_product(nc, bank_x[:, :], [((ATh[:, i, :], ATl[:, i, :]),
                                                             (xTh[:, s, i, :], xTl[:, s, i, :]))],
                                         start=i == 0, stop=i == TC - 1)
                last.then_inc(S["low_mm"], 1)

            def operands(g, t):
                s, cols = slot_of(g), slice(t * P, (t + 1) * P)
                return [(xTh[:, s, i, cols], xTl[:, s, i, cols]) for i in range(TC)] + [(lowh[:, s, cols],
                                                                                         lowl[:, s, cols])]

            def logits(g):
                pe.wait_ge(S["low_lo"], g + 1)
                pe.wait_ge(S["wg_lo"], 1)
                if g:
                    pe.wait_ge(S["lg_ev"], g)
                for t in range(NPAIR):
                    last = split_product(nc, bank_l[:, t * NE:(t + 1) * NE],
                                         [(x, (WGh[:, i, :], WGl[:, i, :])) for i, x in enumerate(operands(g, t))])
                last.then_inc(S["lg_mm"], 1)

            def project(g, t):
                n = g * NPAIR + t
                pe.wait_ge(S["bt_lo"], 1)
                if n >= 2:
                    pe.wait_ge(S["fl_ev"], n - 1)
                weights = [(WTh[:, i, :], WTl[:, i, :]) for i in range(TC)] + [(BTh[:, :], BTl[:, :])]
                split_product(nc, bank_f[n % 2][:, :], list(zip(operands(g, t), weights))).then_inc(S["fl_mm"], 1)

            front(0)
            for g in range(EARLY):
                front(g + 1)
                logits(g)
                for t in range(NPAIR):
                    project(g, t)
            for g in range(EARLY + 1, NG):
                front(g)
                logits(g - 1)
            logits(NG - 1)

            late = [(g, t) for g in range(EARLY, NG) for t in range(NPAIR)]
            done = [0, 0]

            def count_total():
                done[0] += 1
                pe.wait_ge(S["count_ready"], done[0])
                nc.tensor.matmul(bank_l[:, 0:NE * 3], c["ones"], hit[:, :, :].rearrange("p e c -> p (e c)"),
                                 start=True, stop=True).then_inc(S["count_mm"], 1)

            def prefix():
                done[1] += 1
                pe.wait_ge(S["prefix_ready"], done[1])
                all_marks = mark[:, :, :].rearrange("p e j -> p (e j)")
                out = bank_x[:, 0:EJ].rearrange("p (e j) -> p e j", e=NE)
                nc.tensor.matmul(bank_x[:, 0:EJ], before_b[:, :], all_marks, start=True, stop=False)
                for j in range(NT - 1):
                    last = nc.tensor.matmul(out[:, :, j + 1:NT], ones_b[:, :],
                                            mark[:, :, j:j + 1].to_broadcast([P, NE, NT - 1 - j]),
                                            start=False, stop=j == NT - 2)
                last.then_inc(S["prefix_mm"], 1)

            for i in range(TRIALS + 1):
                count_total()
                if late:
                    project(*late.pop(0))
            count_total()
            prefix()
            prefix()
            for g, t in late:
                project(g, t)
            for e in range(NE):
                if e:
                    pe.wait_ge(S["list_ev"], e)
                for j in range(NT):
                    n = e * NT + j
                    pe.wait_ge(S["lo_ready"], n + 1)
                    nc.tensor.matmul(bank_l[:, 0:NV * NCH], is_lo[:, n % 4, :],
                                     row[:, n, :, :].rearrange("p v c -> p (v c)"),
                                     start=j == 0, stop=j == NT - 1).then_inc(S["list_mm"], 1)


def experts(nc, K, A, out, flat, R):
    with ExitStack() as ctx:
        def sb(name, shape, dt=F32):
            return ctx.enter_context(nc.sbuf_tensor(name, shape, dt))

        def bank(name):
            return ctx.enter_context(nc.psum_tensor(name, [P, 512], F32))

        def sem(name):
            return ctx.enter_context(nc.semaphore(name))

        BT = 512
        CH = BT // P
        PER = CAP // BT
        NB = NE * PER
        PAIRS = HC // 2
        tok_in, tok_out = sb("tok_in", [P, CH], I32), sb("tok_out", [P, CH], I32)
        rows = sb("rows", [P, CH, T])
        xh, xl = sb("xh", [P, 2, TC, BT], F32R), sb("xl", [P, 2, TC, BT], F32R)
        w1_raw = sb("w1_raw", [P, PAIRS, TC, 2, P])
        w2_raw = sb("w2_raw", [P, PAIRS, 2, T])
        w1h, w1l = sb("w1h", [P, 2, TC, P], F32R), sb("w1l", [P, 2, TC, P], F32R)
        w2h, w2l = sb("w2h", [P, 2, T], F32R), sb("w2l", [P, 2, T], F32R)
        hid = sb("hid", [P, 2, BT])
        hh, hl = sb("hh", [P, 2, BT], F32R), sb("hl", [P, 2, BT], F32R)
        y_sb = sb("y_sb", [P, CH, T])
        wait_here = sb("wait_there", [1, 3])
        bank_x = [bank("e_x0"), bank("e_x1")]
        bank_h = [bank("e_h0"), bank("e_h1")]
        bank_y = [bank(f"e_y{i}") for i in range(CH)]
        names = """w1_hi w1_lo w2_hi w2_lo index_in index_out rows_in xt_mm xt_hi xt_lo h_mm h_act h_hi h_lo
            y_mm y_ev scattered here""".split()
        S = {n: sem("ex_" + n) for n in names}
        waited = [sem(f"ex_waited{k}") for k in range(2)]
        w_in = [sem(f"ex_w_in{m}") for m in range(PAIRS)]
        block = ctx.enter_context(nc.Block())
        w1_d = A["W1"].rearrange("e (c p) (m n) -> e m p c n", p=P, n=2 * P)
        w2_d = A["W2"].rearrange("e (m k p) n -> e m p k n", p=P, k=2)
        out_rows = out.rearrange("b c t -> (b c) t")

        LOOP = (HC - 4) // 2
        Y0 = 2

        def over_batches(eng, first, body):
            first()
            with eng.Fori(0, NB - 1) as b:
                body(b, True)
            body(NB - 1, False)

        def w_arrived(eng, b, pair):
            eng.wait_ge(w_in[pair], (b // PER + 1) * 32)

        def rounds(eng, b, more, one):
            with eng.Fori(0, LOOP) as i:
                for k in range(2):
                    one(b * HC + 2 * i + 2 + k, k, (b, i + 2, k), (b, i + 1 + k, 1 - k))
            last = b * HC + HC
            one(last - 2, 0, (b + 1, 0, 0) if more else None, (b, PAIRS - 1, 1))
            one(last - 1, 1, (b + 1, 0, 1) if more else None, (b + 1, 0, 0) if more else None)

        def seam(b, one):
            n = b * HC + HC
            one(n, 0, (b + 1, 1, 0), (b + 1, 0, 1))
            one(n + 1, 1, (b + 1, 1, 1), (b + 1, 1, 0))

        @block.sync
        def _(sp):
            def load(e, m):
                with nc.allow_non_contiguous_dma(reason="rows of 1 KiB"):
                    sp.dma_start(w1_raw[:, m, :, :, :].rearrange("p c k n -> p c (k n)"), w1_d[e, m]
                                 ).then_inc(w_in[m], 16)
                sp.dma_start(w2_raw[:, m, :, :], w2_d[e, m]).then_inc(w_in[m], 16)

            for m in range(PAIRS):
                load(0, m)
            with sp.Fori(1, NE) as e:
                for m in range(PAIRS):
                    for n in ("w1_hi", "w1_lo", "w2_hi", "w2_lo"):
                        sp.wait_ge(S[n], (e * PER - 1) * HC + 2 * m + 2)
                    load(e, m)

        @block.gpsimd
        def _(pool):
            def w1_low(n, k, b, pair, chunk):
                pool.wait_ge(S["w1_hi"], n + 1)
                nc.gpsimd.tensor_tensor(w1l[:, k, :, :], w1_raw[:, pair, :, chunk, :], w1h[:, k, :, :].bitcast(F32),
                                        ALU.subtract).then_inc(S["w1_lo"], 1)

            def w2_low(n, k, b, pair, chunk):
                pool.wait_ge(S["w2_hi"], n + 1)
                nc.gpsimd.tensor_tensor(w2l[:, k, :], w2_raw[:, pair, chunk, :], w2h[:, k, :].bitcast(F32),
                                        ALU.subtract).then_inc(S["w2_lo"], 1)

            def one(n, k, w1, w2):
                if w1:
                    w1_low(n + 2, k, *w1)
                if w2:
                    w2_low(n + 1, 1 - k, *w2)

            def take_waits(b, k):
                pool.wait_ge(waited[k], b + 1)
                nc.gpsimd.tensor_tensor(wait_here[:, 1 + k:2 + k], wait_here[:, 0:1], wait_here[:, 0:1],
                                        ALU.add).then_inc(waited[k], 1)

            def gather(b):
                pool.wait_ge(S["index_in"], b + 1)
                take_waits(b, 0)
                for c in range(CH):
                    pool.indirect_dma_start(rows[:, c, :], None, flat,
                                            bass.IndirectOffsetOnAxis(ap=tok_in[:, c:c + 1], axis=0)
                                            ).then_inc(S["rows_in"], 16)

            def scatter(b):
                pool.wait_ge(S["index_out"], b + 1)
                pool.wait_ge(S["y_ev"], (b + 1) * CH)
                take_waits(b, 1)
                for c in range(CH):
                    pool.indirect_dma_start(out_rows, bass.IndirectOffsetOnAxis(ap=tok_out[:, c:c + 1], axis=0),
                                            y_sb[:, c, :], None, compute_op=ALU.add).then_inc(S["scattered"], 16)

            def first():
                nc.gpsimd.memset(wait_here[:, :], 0.0).then_inc(S["here"], 1)
                pool.wait_ge(S["here"], 1)
                for k in range(2):
                    pool.sem_inc(waited[k], 1)
                gather(0)
                w1_low(0, 0, 0, 0, 0)
                w1_low(1, 1, 0, 0, 1)
                w2_low(0, 0, 0, 0, 0)
                one(0, 0, (0, 1, 0), (0, 0, 1))
                one(1, 1, (0, 1, 1), (0, 1, 0))

            def body(b, more):
                if more:
                    gather(b + 1)
                rounds(pool, b, more, one)
                scatter(b)
                if more:
                    seam(b, one)
                pool.wait_ge(S["scattered"], (b + 1) * CH * 16)

            over_batches(pool, first, body)

        @block.scalar
        def _(act):
            def w1_high(n, k, b, pair, chunk):
                w_arrived(act, b, pair)
                nc.scalar.copy(w1h[:, k, :, :], w1_raw[:, pair, :, chunk, :]).then_inc(S["w1_hi"], 1)

            def w2_high(n, k, b, pair, chunk):
                w_arrived(act, b, pair)
                nc.scalar.copy(w2h[:, k, :], w2_raw[:, pair, chunk, :]).then_inc(S["w2_hi"], 1)

            def gelu(n, k):
                act.wait_ge(S["h_mm"], n + 1)
                nc.scalar.activation(hid[:, k, :], bank_h[k][:, :], ACT.Gelu).then_inc(S["h_act"], 1)

            def one(n, k, w1, w2, between=None):
                gelu(n, k)
                if w1:
                    w1_high(n + 2, k, *w1)
                if between:
                    between()
                if w2:
                    act.wait_ge(S["y_mm"], n + Y0)
                    w2_high(n + 1, 1 - k, *w2)

            def x_high(b):
                for i in range(TC):
                    act.wait_ge(S["xt_mm"], b * TC + i + 1)
                    nc.scalar.copy(xh[:, b % 2, i, :], bank_x[i % 2][:, :]).then_inc(S["xt_hi"], 1)

            def gated(b):
                act.wait_ge(S["y_mm"], b * HC + HC + Y0)
                for c in (0, 2):
                    nc.scalar.activation(y_sb[:, c, :], bank_y[c][:, :], ACT.Copy,
                                         scale=R["gate"][:, bass.ds(b * CH + c, 1)]).then_inc(S["y_ev"], 1)

            def first():
                w1_high(0, 0, 0, 0, 0)
                w1_high(1, 1, 0, 0, 1)
                w2_high(0, 0, 0, 0, 0)
                x_high(0)
                one(0, 0, (0, 1, 0), (0, 0, 1))
                one(1, 1, (0, 1, 1), (0, 1, 0))

            def body(b, more):
                for i in range(LOOP):
                    for k in range(2):
                        one(b * HC + 2 * i + 2 + k, k, (b, i + 2, k), (b, i + 1 + k, 1 - k))
                last = b * HC + HC
                if more:
                    x_high(b + 1)
                one(last - 2, 0, (b + 1, 0, 0) if more else None, (b, PAIRS - 1, 1))
                one(last - 1, 1, (b + 1, 0, 1) if more else None, (b + 1, 0, 0) if more else None)
                if more:
                    one(last, 0, (b + 1, 1, 0), (b + 1, 0, 1), between=lambda: gated(b))
                    one(last + 1, 1, (b + 1, 1, 1), (b + 1, 1, 0))
                else:
                    gated(b)

            over_batches(act, first, body)

        @block.vector
        def _(dve):
            def one(n, k, w1=None, w2=None):
                dve.wait_ge(S["h_act"], n + 1)
                dve.wait_ge(S["y_mm"], n + Y0 - 1)
                nc.vector.tensor_copy(hh[:, k, :], hid[:, k, :]).then_inc(S["h_hi"], 1)
                dve.wait_ge(S["h_hi"], n + 1)
                nc.vector.tensor_tensor(hl[:, k, :], hid[:, k, :], hh[:, k, :].bitcast(F32),
                                        ALU.subtract).then_inc(S["h_lo"], 1)

            def index_in(b):
                nc.vector.tensor_copy(tok_in[:, :], R["token"][:, bass.ds(b * CH, CH)]).then_inc(S["index_in"], 1)

            def x_low(b):
                for i in range(TC):
                    dve.wait_ge(S["xt_hi"], b * TC + i + 1)
                    nc.vector.tensor_tensor(xl[:, b % 2, i, :], bank_x[i % 2][:, :], xh[:, b % 2, i, :].bitcast(F32),
                                            ALU.subtract).then_inc(S["xt_lo"], 1)

            def gated(b):
                dve.wait_ge(S["y_mm"], b * HC + HC + Y0)
                for c in (1, 3):
                    nc.vector.tensor_scalar(y_sb[:, c, :], bank_y[c][:, :], R["gate"][:, bass.ds(b * CH + c, 1)],
                                            None, ALU.mult).then_inc(S["y_ev"], 1)

            def first():
                index_in(0)
                x_low(0)
                one(0, 0)
                one(1, 1)

            def body(b, more):
                if more:
                    index_in(b + 1)
                with dve.Fori(0, LOOP) as i:
                    for k in range(2):
                        one(b * HC + 2 * i + 2 + k, k)
                last = b * HC + HC
                nc.vector.tensor_copy(tok_out[:, :], R["token"][:, bass.ds(b * CH, CH)]).then_inc(S["index_out"], 1)
                if more:
                    x_low(b + 1)
                one(last - 2, 0)
                one(last - 1, 1)
                if more:
                    one(last, 0)
                gated(b)
                if more:
                    one(last + 1, 1)

            over_batches(dve, first, body)

        @block.tensor
        def _(pe):
            def hidden(n, k, b):
                pe.wait_ge(S["w1_lo"], n + 1)
                split_product(nc, bank_h[k][:, :], [((w1h[:, k, i, :], w1l[:, k, i, :]),
                                                     (xh[:, b % 2, i, :], xl[:, b % 2, i, :])) for i in range(TC)]
                              ).then_inc(S["h_mm"], 1)

            def spend(n, k, start=False, stop=False):
                pe.wait_ge(S["h_lo"], n + 1)
                pe.wait_ge(S["w2_lo"], n + 1)
                for c in range(CH):
                    cols = slice(c * P, (c + 1) * P)
                    last = split_product(nc, bank_y[c][:, :], [((hh[:, k, cols], hl[:, k, cols]),
                                                                (w2h[:, k, :], w2l[:, k, :]))], start=start, stop=stop)
                last.then_inc(S["y_mm"], 1)

            def x_transposes(b, i):
                pe.wait_ge(S["rows_in"], (b + 1) * CH * 16)
                for c in range(CH):
                    last = nc.tensor.transpose(bank_x[i % 2][:, c * P:(c + 1) * P], rows[:, c, i * P:(i + 1) * P],
                                               K.parts["ident"])
                last.then_inc(S["xt_mm"], 1)

            def x_free(b, i):
                pe.wait_ge(S["xt_lo"], b * TC + i - 1)

            def first():
                pe.sem_inc(S["y_mm"], Y0)
                for i in range(TC):
                    if i >= 2:
                        x_free(0, i)
                    x_transposes(0, i)
                pe.wait_ge(S["xt_lo"], TC)
                hidden(0, 0, 0)
                hidden(1, 1, 0)
                spend(0, 0, start=True)

            def body(b, more):
                n = b * HC
                with pe.Fori(0, LOOP) as i:
                    for k in range(2):
                        m = n + 2 * i + 2 + k
                        hidden(m, k, b)
                        spend(m - 1, 1 - k)
                last = n + HC
                if more:
                    x_transposes(b + 1, 0)
                    x_transposes(b + 1, 1)
                hidden(last - 2, 0, b)
                if more:
                    x_free(b + 1, 2)
                    x_transposes(b + 1, 2)
                    x_free(b + 1, 3)
                    x_transposes(b + 1, 3)
                spend(last - 3, 1)
                hidden(last - 1, 1, b)
                spend(last - 2, 0)
                if more:
                    pe.wait_ge(S["xt_lo"], (b + 1) * TC + TC)
                    hidden(last, 0, b + 1)
                spend(last - 1, 1, stop=True)
                if more:
                    hidden(last + 1, 1, b + 1)
                    pe.wait_ge(S["y_ev"], (b + 1) * CH)
                    spend(last, 0, start=True)

            over_batches(pe, first, body)


class Kept(dict):
    pass


def load_table(nc, ctx, K, name):
    K[name] = ctx.enter_context(nc.sbuf_tensor(f"table_{name}", [P, sum(TABLES[name].values())], F32))
    at = 0
    for part, width in TABLES[name].items():
        K.parts[part] = K[name][:, at:at + width]
        at += width


def block_program(nc, A, out):
    with ExitStack() as ctx:
        K = Kept()
        K.parts = {}
        load_table(nc, ctx, K, "always")
        with ExitStack() as early:
            def eb(name, shape, dt=F32):
                return early.enter_context(nc.sbuf_tensor(name, shape, dt))

            load_table(nc, early, K, "attend")
            K.update(bA=eb("bA", [P, 2]), bC=eb("bC", [P, NU]), bB=eb("bB", [P, 1]), bZ=eb("bZ", [P, T]),
                     wsub=eb("wsub", [P, NSUB, C]), fside=eb("fside", [NSUB, C]), subj=eb("subj", [NSUB, B], I32),
                     sel=eb("sel", [NSUB, B]), wblk=eb("wblk", [P, NPAIR, P]), qrope=eb("q_rope", [P, GB, 2, C]))
            W = dict(WAh=eb("WAh", [P, TC, 2 * L], F32R), WAl=eb("WAl", [P, TC, 2 * L], F32R),
                     WCh=eb("WCh", [P, 2, DR * NH], F32R), WCl=eb("WCl", [P, 2, DR * NH], F32R),
                     WBh=eb("WBh", [P, 2, 2, DR], F32R), WBl=eb("WBl", [P, 2, 2, DR], F32R),
                     Ah=eb("Ah", [P, NH * L], F32R), Al=eb("Al", [P, NH * L], F32R),
                     Mh=eb("Mh", [P, NH, T], F32R), Ml=eb("Ml", [P, NH, T], F32R))
            absorb_weights(nc, K, A, W)
            attention(nc, K, A, W, out)
        flat = nc.dram_tensor("flat_dram", (NTOK, T), F32, kind="Internal").ap()
        R = dict(token=ctx.enter_context(nc.sbuf_tensor("slot_token", [P, NE * NCH], I32)),
                 gate=ctx.enter_context(nc.sbuf_tensor("slot_gate", [P, NE * NCH], F32)))
        routing(nc, K, A, out, flat, R)
        experts(nc, K, A, out, flat, R)


_INS = {'x': 'x', 'subj': 'itok_B_0_7', 'fside': 'fside_8xS_0', 'adapt': 'itok_B_0_6', 'cond_weights': 'L0_cond_weights',
        'WA': 'L0_attn_WA', 'bA': 'L0_attn_bA', 'WB': 'L0_attn_WB', 'bB': 'L0_attn_bB', 'WC': 'L0_attn_WC',
        'bC': 'L0_attn_bC', 'WUQ': 'L0_attn_WUQ', 'WUK': 'L0_attn_WUK', 'WUV': 'L0_attn_WUV', 'WZ': 'L0_attn_WZ',
        'bZ': 'L0_attn_bZ', 'W': 'L0_cond2_W', 'A': 'L0_cond2_A', 'Bm': 'L0_cond2_Bm',
        'scalings': 'L0_cond2_scalings', 'Wg': 'L0_ffn_Wg', 'bg': 'L0_ffn_bg', 'W1': 'L0_ffn_W1', 'W2': 'L0_ffn_W2'}


def kernel(**inputs):
    import concourse.bacc as _bacc
    from concourse.bass_utils import run_bass_kernel_spmd as _run

    nc = _bacc.Bacc("TRN2", target_bir_lowering=False, num_devices=1)
    arrays = {f"in_{short}_dram": np.ascontiguousarray(inputs[name]) for short, name in _INS.items()}
    arrays.update({f"in_{name}_dram": const_table(name) for name in TABLES})
    args = {name[3:-5]: nc.dram_tensor(name, a.shape, mybir.dt.from_np(a.dtype), kind="ExternalInput").ap()
            for name, a in arrays.items()}
    out = nc.dram_tensor("out_0_dram", (B, C, T), F32, kind="ExternalOutput").ap()
    block_program(nc, args, out)
    r = _run(nc, [arrays], core_ids=[0])
    return r.results[0]["out_0_dram"]
```

```python
from contextlib import ExitStack

import numpy as np

import concourse.bass as bass
from concourse import mybir

F32 = mybir.dt.float32
F32R = mybir.dt.float32r
BF16 = mybir.dt.bfloat16
I32 = mybir.dt.int32
U32 = mybir.dt.uint32
ALU = mybir.AluOpType
ACT = mybir.ActivationFunctionType
AX = mybir.AxisListType.X

P = 128
B, C, T = 64, 64, 512
NSUB, NADAPT, RANK = 8, 8, 16
NH, DH, DR, L = 16, 128, 64, 128
SCALE = float(np.float32((DH + DR) ** -0.5))
MASKED = -1.0e30
TC = T // P
GB = 8
NG = B // GB
GT = GB * C
NPAIR = GT // P
NU = NH // 2
NTOK = B * C
NT = NTOK // P
NE, HID = 4, 2048
CAP = NTOK // NE
NCH = CAP // P
HC = HID // P


TRIALS = 15
TABLES = {
    "always": {"ident": P, "ones": P, "part": 1},
    "attend": {"mask": C, "cosq": NU * C, "sinq": NU * C, "cosk": C, "sink": C},
    "route": {"before": P, "iota": P, "adapter": 1, "tile": NT, "fold": NE, "trial": 3 * TRIALS},
}


def const_columns():
    def rope(feature, size):
        theta = np.exp(-(feature // 2).astype(np.float32) / np.float32(size)
                       * np.log(np.float32(10000.0))).astype(np.float32)
        angle = (np.arange(1, C + 1, dtype=np.float32)[None] * theta[:, None]).astype(np.float32)
        sign = np.where(feature % 2 == 0, -1.0, 1.0).astype(np.float32)[:, None]
        return np.cos(angle), np.sin(angle) * sign

    p = np.arange(P)
    pairs = [rope(u * P + p, DR * NH) for u in range(NU)]
    cosk, sink = rope(p % DR, DR)
    trial = np.array([c << (2 * (TRIALS - 1 - i)) for i in range(TRIALS) for c in (1, 2, 3)], np.int32)
    return {
        "ident": np.eye(P), "ones": np.ones((P, P)), "part": p[:, None],
        "mask": np.where(np.arange(C)[None] <= (p % C)[:, None], 0.0, MASKED),
        "cosq": np.concatenate([c for c, _ in pairs], 1), "sinq": np.concatenate([s for _, s in pairs], 1),
        "cosk": cosk, "sink": sink,
        "before": p[:, None] < p[None], "iota": np.broadcast_to(p[None], (P, P)), "adapter": p[:, None] // RANK,
        "tile": np.broadcast_to(np.arange(NT)[None], (P, NT)),
        "fold": p[:, None] % NE == np.arange(NE)[None],
        "trial": np.broadcast_to(trial.view(np.float32), (P, 3 * TRIALS)),
    }


def const_table(name):
    columns = const_columns()
    return np.concatenate([columns[n] for n in TABLES[name]], 1).astype(np.float32)


def split_product(nc, out, pairs, start=True, stop=True):
    last = None
    for n, ((ah, al), (bh, bl)) in enumerate(pairs):
        nc.tensor.matmul(out, ah, bh, start=start and n == 0, stop=False)
        nc.tensor.matmul(out, ah, bl, start=False, stop=False)
        last = nc.tensor.matmul(out, al, bh, start=False, stop=stop and n == len(pairs) - 1)
    return last


def absorb_weights(nc, K, A, W):
    HG = NH // 4
    with ExitStack() as ctx:
        def sb(name, shape, dt=F32):
            return ctx.enter_context(nc.sbuf_tensor(name, shape, dt))

        def bank(name):
            return ctx.enter_context(nc.psum_tensor(name, [P, 512], F32))

        def sem(name):
            return ctx.enter_context(nc.semaphore(name))

        up = {n: sb(f"up_{n}", [P, NH * DH]) for n in "qkv"}
        wz = sb("wz_raw", [P, NH, T])
        wa = sb("wa_raw", [P, TC, 2 * L])
        wc = sb("wc_raw", [P, 2, DR * NH])
        wb = sb("wb_raw", [P, 2, DR])
        upT = {n: sb(f"upT_{n}", [P, 2, 512]) for n in "qkv"}
        bank_t = {n: bank(f"w_t{n}") for n in "qkv"}
        bank_a = bank("w_a")
        bank_m = [bank(f"w_m{i}") for i in range(4)]

        consts_in = sem("consts_in")
        up_in = {n: sem(f"up{n}_in") for n in "qkv"}
        wz_in = [sem(f"wz_in{i}") for i in range(HG)]
        small_in = sem("small_in")
        t_mm = {n: sem(f"w_t{n}_mm") for n in "qkv"}
        t_ev = {n: sem(f"w_t{n}_ev") for n in "qkv"}
        a_mm, a_hi, a_lo = sem("w_a_mm"), sem("w_a_hi"), sem("w_a_lo")
        m_mm, m_hi, m_lo = sem("w_m_mm"), sem("w_m_hi"), sem("w_m_lo")
        s_hi, s_lo = sem("w_s_hi"), sem("w_s_lo")
        zeroed = sem("w_zeroed")

        block = ctx.enter_context(nc.Block())
        wz_d = A["WZ"].rearrange("(h d) n -> d h n", d=DH)

        @block.sync
        def _(sp):
            sp.dma_start(K["always"][:, :], A["always"]).then_inc(consts_in, 16)
            for n, name in (("q", "WUQ"), ("k", "WUK"), ("v", "WUV")):
                sp.dma_start(up[n][:, :], A[name]).then_inc(up_in[n], 16)
            for i in range(HG):
                sp.dma_start(wz[:, 4 * i:4 * i + 4, :], wz_d[:, 4 * i:4 * i + 4, :]).then_inc(wz_in[i], 16)
            with nc.allow_non_contiguous_dma(reason="a few small vectors, once"):
                sp.dma_start(wa[:, :, :], A["WA"].rearrange("(c p) n -> p c n", p=P)).then_inc(small_in, 16)
                sp.dma_start(wc[:, :, :], A["WC"].rearrange("(c p) n -> p c n", p=P)).then_inc(small_in, 16)
                sp.dma_start(wb[:, :, :], A["WB"].rearrange("(c p) n -> p c n", p=P)).then_inc(small_in, 16)
                sp.dma_start(K["bA"][:, :], A["bA"].rearrange("(c p) -> p c", p=P)).then_inc(small_in, 16)
                sp.dma_start(K["bC"][:, :], A["bC"].rearrange("(c p) -> p c", p=P)).then_inc(small_in, 16)
                for h in range(2):
                    sp.dma_start(K["bB"][h * DR:(h + 1) * DR, :],
                                 A["bB"].rearrange("(p o) -> p o", o=1)).then_inc(small_in, 16)
                    sp.dma_start(K["wsub"][h * C:(h + 1) * C, :, :],
                                 A["cond_weights"].rearrange("n c d -> c n d")).then_inc(small_in, 16)
                sp.dma_start(K["bZ"][:, :], A["bZ"].partition_broadcast(P)).then_inc(small_in, 16)
                sp.dma_start(K["attend"][:, :], A["attend"]).then_inc(small_in, 16)
                sp.dma_start(K["fside"][:, :], A["fside"]).then_inc(small_in, 16)
                sp.dma_start(K["subj"][:, :], A["subj"].partition_broadcast(NSUB)).then_inc(small_in, 16)

        SMALL = 16 * 13

        @block.scalar
        def _(act):
            for i in range(HG):
                s = i % 2
                for n in "qv":
                    act.wait_ge(t_mm[n], i + 1)
                    if i >= 2:
                        act.wait_ge(a_mm if n == "q" else m_mm, i - 1 if n == "q" else 4 * (i - 1))
                    nc.scalar.copy(upT[n][:, s, :], bank_t[n][:, :]).then_inc(t_ev[n], 1)
                act.wait_ge(a_mm, i + 1)
                nc.scalar.copy(W["Ah"][:, 512 * i:512 * i + 512], bank_a[:, :]).then_inc(a_hi, 1)
                for j in range(4):
                    act.wait_ge(m_mm, 4 * i + j + 1)
                    nc.scalar.copy(W["Mh"][:, 4 * i + j, :], bank_m[j][:, :]).then_inc(m_hi, 1)
            act.wait_ge(small_in, SMALL)
            nc.scalar.copy(W["WAh"][:, :, :], wa[:, :, :]).then_inc(s_hi, 1)
            nc.scalar.copy(W["WCh"][:, :, :], wc[:, :, :]).then_inc(s_hi, 1)
            nc.scalar.copy(W["WBh"][:, :, :, :],
                           wb[:, :, :].unsqueeze(2).to_broadcast([P, 2, 2, DR])).then_inc(s_hi, 1)

        @block.gpsimd
        def _(pool):
            nc.gpsimd.memset(K["wblk"][:, :, :], 0.0).then_inc(zeroed, 1)
            nc.gpsimd.memset(K["qrope"][:, :, :, :], 0.0).then_inc(zeroed, 1)
            pool.wait_ge(s_hi, 1)
            nc.gpsimd.tensor_tensor(W["WAl"][:, :, :], wa[:, :, :], W["WAh"][:, :, :].bitcast(F32),
                                    ALU.subtract).then_inc(s_lo, 1)
            pool.wait_ge(s_hi, 2)
            nc.gpsimd.tensor_tensor(W["WCl"][:, :, :], wc[:, :, :], W["WCh"][:, :, :].bitcast(F32),
                                    ALU.subtract).then_inc(s_lo, 1)
            pool.wait_ge(s_hi, 3)
            nc.gpsimd.tensor_tensor(W["WBl"][:, :, :, :],
                                    wb[:, :, :].unsqueeze(2).to_broadcast([P, 2, 2, DR]),
                                    W["WBh"][:, :, :, :].bitcast(F32), ALU.subtract).then_inc(s_lo, 1)

        @block.vector
        def _(dve):
            for i in range(HG):
                s = i % 2
                dve.wait_ge(t_mm["k"], i + 1)
                if i >= 2:
                    dve.wait_ge(a_mm, i - 1)
                nc.vector.tensor_copy(upT["k"][:, s, :], bank_t["k"][:, :]).then_inc(t_ev["k"], 1)
                dve.wait_ge(a_hi, i + 1)
                nc.vector.tensor_tensor(W["Al"][:, 512 * i:512 * i + 512], bank_a[:, :],
                                        W["Ah"][:, 512 * i:512 * i + 512].bitcast(F32),
                                        ALU.subtract).then_inc(a_lo, 1)
                for j in range(4):
                    h = 4 * i + j
                    dve.wait_ge(m_hi, h + 1)
                    nc.vector.tensor_tensor(W["Ml"][:, h, :], bank_m[j][:, :], W["Mh"][:, h, :].bitcast(F32),
                                            ALU.subtract).then_inc(m_lo, 1)
            dve.wait_ge(small_in, SMALL)
            nc.vector.tensor_scalar(K["sel"][:, :], K["subj"][:, :], K.parts["part"][0:NSUB, :], None,
                                    ALU.is_equal).then_inc(zeroed, 1)

        @block.tensor
        def _(pe):
            def transposes(i):
                for n in "qkv":
                    pe.wait_ge(up_in[n], 16)
                    if i >= 1:
                        pe.wait_ge(t_ev[n], i)
                    for j in range(4):
                        h = 4 * i + j
                        last = nc.tensor.transpose(bank_t[n][:, j * P:(j + 1) * P], up[n][:, h * P:(h + 1) * P],
                                                   K.parts["ident"])
                    last.then_inc(t_mm[n], 1)

            pe.wait_ge(consts_in, 16)
            transposes(0)
            for i in range(HG):
                s = i % 2
                if i + 1 < HG:
                    transposes(i + 1)
                pe.wait_ge(t_ev["q"], i + 1)
                pe.wait_ge(t_ev["k"], i + 1)
                if i >= 1:
                    pe.wait_ge(a_lo, i)
                for j in range(4):
                    cols = slice(j * P, (j + 1) * P)
                    last = nc.tensor.matmul(bank_a[:, cols], upT["q"][:, s, cols], upT["k"][:, s, cols],
                                            start=True, stop=True)
                last.then_inc(a_mm, 1)
                pe.wait_ge(t_ev["v"], i + 1)
                pe.wait_ge(wz_in[i], 16)
                for j in range(4):
                    if i >= 1:
                        pe.wait_ge(m_lo, 4 * (i - 1) + j + 1)
                    nc.tensor.matmul(bank_m[j][:, :], upT["v"][:, s, j * P:(j + 1) * P], wz[:, 4 * i + j, :],
                                     start=True, stop=True).then_inc(m_mm, 1)


def attention(nc, K, A, W, out):
    with ExitStack() as ctx:
        def sb(name, shape, dt=F32):
            return ctx.enter_context(nc.sbuf_tensor(name, shape, dt))

        def bank(name):
            return ctx.enter_context(nc.psum_tensor(name, [P, 512], F32))

        def sem(name):
            return ctx.enter_context(nc.semaphore(name))

        x_cond = sb("x_cond", [P, NPAIR, T])
        x_res = sb("x_res", [P, NPAIR, T])
        cond_h, cond_l = sb("cond_h", [P, TC, GT], F32R), sb("cond_l", [P, TC, GT], F32R)
        lat32 = sb("lat32", [P, 2, GT])
        lat_h, lat_l = sb("lat_h", [P, 2, GT], F32R), sb("lat_l", [P, 2, GT], F32R)
        kv_tok = sb("kv_tok", [P, NPAIR, L])
        k_rope = sb("k_rope", [P, GT])
        raw, swapped = sb("rope_raw", [P, GT]), sb("rope_swapped", [P, GT])
        by_cos, by_sin = sb("rope_cos", [P, GT]), sb("rope_sin", [P, GT])
        cond32 = (raw, swapped)
        bias_bc = by_cos
        bias_sel = by_sin[0:NSUB, :].rearrange("n (b d) -> n b d", b=GB)
        q_nope = sb("q_nope", [P, GB, 2, C])
        score = sb("score", [P, GB, C])
        prob = sb("prob", [P, 2, GB, C])
        rmax, rsum, rinv = sb("rmax", [P, GB]), sb("rsum", [P, GB]), sb("rinv", [P, GB])
        wait_here = sb("wait_here", [1, 1])
        probT = sb("probT", [P, NPAIR, P])
        mix_h = sb("mix_h", [P, 2, 2, NPAIR, 2, C], F32R)
        mix_l = sb("mix_l", [P, 2, 2, NPAIR, 2, C], F32R)
        q_rope = K["qrope"]
        bank_a, bank_b, bank_d, bank_s = bank("bank_a"), bank("bank_b"), bank("bank_d"), bank("bank_s")
        bank_o = [bank(f"bank_o{t}") for t in range(NPAIR)]

        names = """x_in xres_in xres_biased x2_out wblk_ready bias_sel_ready bias_mm bias_ev cond_mm cond_ev cond_hi
            cond_lo_even cond_lo_odd lat_mm lat_ev lat_hi lat_lo kb_mm kvt_mm kvt_ev raw_ev swap_ev cos_ev sin_ev rope_done
            qc_mm qn0_mm qn1_mm qn0_ev qn1_ev score_mm score_ev max_ev sub_ev exp_ev sum_ev inv_ev prob_ev pt_mm pt_ev
            mixe_mm mixo_mm mixe_hi mixo_hi mixe_lo mixo_lo wz_mm x2_ev""".split()
        S = {n: sem("at_" + n) for n in names}

        block = ctx.enter_context(nc.Block())
        x_d = A["x"].rearrange("(g n j) c t -> g (j c) n t", n=NPAIR, j=2)
        out_d = out.rearrange("(g n j) c t -> g (j c) n t", n=NPAIR, j=2)
        NR = NU + 1

        def over_groups(eng, first, body):
            first()
            with eng.Fori(0, NG - 1) as g:
                body(g, True)
            body(NG - 1, False)

        @block.sync
        def _(sp):
            def first():
                sp.dma_start(x_cond[:, :, :], x_d[0]).then_inc(S["x_in"], 16)
                sp.dma_start(x_res[:, :, :], x_d[0]).then_inc(S["xres_in"], 16)

            def body(g, more):
                if more:
                    sp.wait_ge(S["cond_mm"], g * TC + TC)
                    sp.dma_start(x_cond[:, :, :], x_d[g + 1]).then_inc(S["x_in"], 16)
                for t in range(NPAIR):
                    sp.wait_ge(S["x2_ev"], g * NPAIR + t + 1)
                    sp.dma_start(out_d[g, :, t, :], x_res[:, t, :]).then_inc(S["x2_out"], 16)
                sp.wait_ge(S["x2_out"], (g + 1) * NPAIR * 16)
                if more:
                    sp.dma_start(x_res[:, :, :], x_d[g + 1]).then_inc(S["xres_in"], 16)

            over_groups(sp, first, body)

        @block.gpsimd
        def _(pool):
            def bias_rows(g):
                nc.gpsimd.tensor_tensor(bias_sel[:, :, :],
                                        K["sel"][:, bass.ds(g * GB, GB)].unsqueeze(2).to_broadcast([NSUB, GB, C]),
                                        K["fside"][:, :].unsqueeze(1).to_broadcast([NSUB, GB, C]),
                                        ALU.mult).then_inc(S["bias_sel_ready"], 1)

            def cond_lo(g):
                for c in range(0, TC, 2):
                    pool.wait_ge(S["cond_hi"], g * TC + c + 1)
                    nc.gpsimd.tensor_tensor(cond_l[:, c, :], cond32[0][:, :], cond_h[:, c, :].bitcast(F32),
                                            ALU.subtract).then_inc(S["cond_lo_even"], 1)

            def rope_cos(r, cos, first=False):
                pool.wait_ge(S["raw_ev"], r + 1)
                if not first:
                    pool.wait_ge(S["rope_done"], r)
                v = raw[:, :].rearrange("p (b t) -> p b t", b=GB)
                nc.gpsimd.tensor_tensor(by_cos[:, :].rearrange("p (b t) -> p b t", b=GB), v,
                                        cos.unsqueeze(1).to_broadcast([P, GB, C]), ALU.mult).then_inc(S["cos_ev"], 1)

            def q_rope_cos(g, u):
                rope_cos(g * NR + 1 + u, K.parts["cosq"][:, u * C:(u + 1) * C])

            def first():
                bias_rows(0)
                cond_lo(0)
                rope_cos(0, K.parts["cosk"], first=True)

            def body(g, more):
                q_rope_cos(g, 0)
                for u in range(NU):
                    if u + 1 < NU:
                        q_rope_cos(g, u + 1)
                    elif more:
                        pool.wait_ge(S["rope_done"], g * NR + NR)
                        bias_rows(g + 1)
                    pool.wait_ge(S["inv_ev"], g * NU + u + 1)
                    nc.gpsimd.tensor_tensor(prob[:, u % 2, :, :], prob[:, u % 2, :, :],
                                            rinv[:, :].unsqueeze(2).to_broadcast([P, GB, C]),
                                            ALU.mult).then_inc(S["prob_ev"], 1)
                    if NU - NPAIR <= u:
                        if u == NU - NPAIR:
                            pool.wait_ge(S["xres_in"], g * 16 + 16)
                        t = u - (NU - NPAIR)
                        nc.gpsimd.tensor_tensor(x_res[:, t, :], x_res[:, t, :], K["bZ"][:, :],
                                                ALU.add).then_inc(S["xres_biased"], 1)
                if more:
                    cond_lo(g + 1)
                    rope_cos((g + 1) * NR, K.parts["cosk"])

            over_groups(pool, first, body)

        @block.scalar
        def _(act):
            def bias_evac(g):
                act.wait_ge(S["bias_mm"], g + 1)
                nc.scalar.copy(bias_bc[:, :], bank_s[:, :]).then_inc(S["bias_ev"], 1)

            def cond_hi(g, c):
                act.wait_ge(S["cond_ev"], g * TC + c + 1)
                nc.scalar.copy(cond_h[:, c, :], cond32[c % 2][:, :]).then_inc(S["cond_hi"], 1)

            def latent(g, i):
                act.wait_ge(S["lat_mm"], g * 2 + i + 1)
                nc.scalar.activation(lat32[:, i, :], (bank_a, bank_s)[i][:, :], ACT.Identity,
                                     bias=K["bA"][:, i:i + 1]).then_inc(S["lat_ev"], 1)
                act.wait_ge(S["lat_ev"], g * 2 + i + 1)
                nc.scalar.copy(lat_h[:, i, :], lat32[:, i, :]).then_inc(S["lat_hi"], 1)

            def kv_tokens(g):
                act.wait_ge(S["kvt_mm"], g + 1)
                nc.scalar.copy(kv_tok[:, :, :], bank_b[:, :].rearrange("p (n l) -> p n l", n=NPAIR)
                               ).then_inc(S["kvt_ev"], 1)

            def rope_raw(r, ready, count, source, bias, first=False):
                act.wait_ge(ready, count)
                if not first:
                    act.wait_ge(S["swap_ev"], r)
                    act.wait_ge(S["cos_ev"], r)
                nc.scalar.activation(raw[:, :], source[:, :], ACT.Identity, bias=bias).then_inc(S["raw_ev"], 1)

            def q_rope_raw(g, u):
                rope_raw(g * NR + 1 + u, S["qc_mm"], g * NU + u + 1, bank_a, K["bC"][:, u:u + 1])

            def q_nope_evac(g, u, h):
                act.wait_ge(S[f"qn{h}_mm"], g * NU + u + 1)
                nc.scalar.copy(q_nope[:, :, h, :], (bank_b, bank_d)[h][:, :].rearrange("p (b t) -> p b t", b=GB)
                               ).then_inc(S[f"qn{h}_ev"], 1)

            def prob_transposed(g, u):
                act.wait_ge(S["pt_mm"], g * NU + u + 1)
                nc.scalar.copy(probT[:, :, :], bank_a[:, :].rearrange("p (n q) -> p n q", n=NPAIR)
                               ).then_inc(S["pt_ev"], 1)

            def mix_hi(g, u):
                for j, (k, bk) in enumerate((("mixe", bank_b), ("mixo", bank_d))):
                    act.wait_ge(S[k + "_mm"], g * NU + u + 1)
                    nc.scalar.copy(mix_h[:, u % 2, :, :, j, :].rearrange("p h n t -> p n h t"),
                                   bk[:, :].rearrange("p (n h t) -> p n h t", n=NPAIR, h=2)
                                   ).then_inc(S[k + "_hi"], 1)

            def first():
                bias_evac(0)
                for c in range(TC):
                    cond_hi(0, c)
                latent(0, 0)
                latent(0, 1)
                kv_tokens(0)
                rope_raw(0, S["kb_mm"], 1, bank_d, K["bB"][:, 0:1], first=True)

            def body(g, more):
                q_rope_raw(g, 0)
                for h in range(2):
                    q_nope_evac(g, 0, h)
                for u in range(NU):
                    if u + 1 < NU:
                        q_rope_raw(g, u + 1)
                    act.wait_ge(S["sub_ev"], g * NU + u + 1)
                    nc.scalar.activation(prob[:, u % 2, :, :], score[:, :, :], ACT.Exp).then_inc(S["exp_ev"], 1)
                    if u + 1 < NU:
                        q_nope_evac(g, u + 1, 0)
                    if u >= 1:
                        prob_transposed(g, u - 1)
                    if u + 1 < NU:
                        q_nope_evac(g, u + 1, 1)
                    if u >= 1:
                        mix_hi(g, u - 1)
                if more:
                    bias_evac(g + 1)
                prob_transposed(g, NU - 1)
                if more:
                    cond_hi(g + 1, 0)
                mix_hi(g, NU - 1)
                if more:
                    for c in range(1, TC):
                        cond_hi(g + 1, c)
                    latent(g + 1, 0)
                    latent(g + 1, 1)
                    kv_tokens(g + 1)
                    rope_raw((g + 1) * NR, S["kb_mm"], g + 2, bank_d, K["bB"][:, 0:1])

            over_groups(act, first, body)

        @block.vector
        def _(dve):
            COND_BANK = (bank_d, bank_s, bank_a, bank_s)

            def group_inputs(g, batches):
                for j in batches:
                    h, n = j % 2, j // 2
                    rows = slice(h * C, (h + 1) * C)
                    s = dve.value_load(K["subj"][0:1, bass.ds(g * GB + j, 1)], min_val=0, max_val=NSUB - 1)
                    nc.vector.tensor_copy(K["wblk"][rows, n, rows], K["wsub"][rows, bass.ds(s, 1), :].squeeze(1)
                                          ).then_inc(S["wblk_ready"], 1)

            def cond_evac(g, c, first=False):
                dve.wait_ge(S["bias_ev"], g + 1)
                dve.wait_ge(S["cond_mm"], g * TC + c + 1)
                if not first or c >= 2:
                    dve.wait_ge(S[("cond_lo_even", "cond_lo_odd")[c % 2]], g * (TC // 2) + c // 2)
                nc.vector.tensor_tensor(cond32[c % 2][:, :], COND_BANK[c][:, :], bias_bc[:, :],
                                        ALU.add).then_inc(S["cond_ev"], 1)

            def cond_lo(g, c):
                dve.wait_ge(S["cond_hi"], g * TC + c + 1)
                nc.vector.tensor_tensor(cond_l[:, c, :], cond32[1][:, :], cond_h[:, c, :].bitcast(F32),
                                        ALU.subtract).then_inc(S["cond_lo_odd"], 1)

            def latent_lo(g, i):
                dve.wait_ge(S["lat_hi"], g * 2 + i + 1)
                nc.vector.tensor_tensor(lat_l[:, i, :], lat32[:, i, :], lat_h[:, i, :].bitcast(F32),
                                        ALU.subtract).then_inc(S["lat_lo"], 1)

            def rope_sin(r, sin, first=False):
                dve.wait_ge(S["raw_ev"], r + 1)
                if not first:
                    dve.wait_ge(S["sin_ev"], r)
                nc.vector.memset(wait_here[:, :], 0.0)
                nc.vector.stream_shuffle(swapped[:, :], raw[:, :], [i ^ 1 for i in range(32)]
                                         ).then_inc(S["swap_ev"], 1)
                dve.wait_ge(S["swap_ev"], r + 1)
                if not first:
                    dve.wait_ge(S["rope_done"], r)
                nc.vector.tensor_tensor(by_sin[:, :].rearrange("p (b t) -> p b t", b=GB),
                                        swapped[:, :].rearrange("p (b t) -> p b t", b=GB),
                                        sin.unsqueeze(1).to_broadcast([P, GB, C]), ALU.mult).then_inc(S["sin_ev"], 1)

            def q_rope_sin(g, u):
                rope_sin(g * NR + 1 + u, K.parts["sinq"][:, u * C:(u + 1) * C])

            def rope_add_keys(r):
                dve.wait_ge(S["cos_ev"], r + 1)
                dve.wait_ge(S["sin_ev"], r + 1)
                nc.vector.tensor_tensor(k_rope[:, :], by_cos[:, :], by_sin[:, :], ALU.add).then_inc(S["rope_done"], 1)

            def rope_add_queries(r):
                dve.wait_ge(S["cos_ev"], r + 1)
                dve.wait_ge(S["sin_ev"], r + 1)
                for h in range(2):
                    rows = slice(h * DR, (h + 1) * DR)
                    last = nc.vector.tensor_tensor(q_rope[rows, :, h, :],
                                                   by_cos[rows, :].rearrange("p (b t) -> p b t", b=GB),
                                                   by_sin[rows, :].rearrange("p (b t) -> p b t", b=GB), ALU.add)
                last.then_inc(S["rope_done"], 1)

            def mix_lo(g, u):
                for j, (k, bk) in enumerate((("mixe", bank_b), ("mixo", bank_d))):
                    view = mix_h[:, u % 2, :, :, j, :].rearrange("p h n t -> p n h t")
                    dve.wait_ge(S[k + "_hi"], g * NU + u + 1)
                    nc.vector.tensor_tensor(mix_l[:, u % 2, :, :, j, :].rearrange("p h n t -> p n h t"),
                                            bk[:, :].rearrange("p (n h t) -> p n h t", n=NPAIR, h=2),
                                            view.bitcast(F32), ALU.subtract).then_inc(S[k + "_lo"], 1)

            def per_batch(row):
                return row[:, :].unsqueeze(2).to_broadcast([P, GB, C])

            def score_in(g, u):
                n = g * NU + u + 1
                dve.wait_ge(S["score_mm"], n)
                if u:
                    dve.wait_ge(S["exp_ev"], n - 1)
                nc.vector.scalar_tensor_tensor(out=score[:, :, :],
                                               in0=bank_s[:, :].rearrange("p (b t) -> p b t", b=GB), scalar=SCALE,
                                               in1=K.parts["mask"].unsqueeze(1).to_broadcast([P, GB, C]),
                                               op0=ALU.mult, op1=ALU.add).then_inc(S["score_ev"], 1)

            def less_max(g, u):
                n = g * NU + u + 1
                dve.wait_ge(S["score_ev"], n)
                nc.vector.tensor_reduce(rmax[:, :], score[:, :, :], AX, ALU.max).then_inc(S["max_ev"], 1)
                dve.wait_ge(S["max_ev"], n)
                nc.vector.tensor_tensor(score[:, :, :], score[:, :, :], per_batch(rmax),
                                        ALU.subtract).then_inc(S["sub_ev"], 1)

            def softmax_sum(g, u):
                n = g * NU + u + 1
                dve.wait_ge(S["exp_ev"], n)
                nc.vector.tensor_reduce(rsum[:, :], prob[:, u % 2, :, :], AX, ALU.add).then_inc(S["sum_ev"], 1)
                dve.wait_ge(S["sum_ev"], n)
                if u:
                    dve.wait_ge(S["prob_ev"], n - 1)
                nc.vector.reciprocal(rinv[:, :], rsum[:, :]).then_inc(S["inv_ev"], 1)

            def x2_tile(g, t):
                dve.wait_ge(S["xres_biased"], g * NPAIR + t + 1)
                dve.wait_ge(S["wz_mm"], g * NPAIR + t + 1)
                nc.vector.tensor_tensor(x_res[:, t, :], bank_o[t][:, :], x_res[:, t, :],
                                        ALU.add).then_inc(S["x2_ev"], 1)

            def head(g, prev=None):
                rope_sin(g * NR, K.parts["sink"], first=prev is None)
                rope_add_keys(g * NR)
                q_rope_sin(g, 0)
                rope_add_queries(g * NR + 1)
                if prev is not None:
                    for t in range(NPAIR - 1):
                        x2_tile(prev, t)
                q_rope_sin(g, 1)
                score_in(g, 0)
                rope_add_queries(g * NR + 2)
                less_max(g, 0)
                softmax_sum(g, 0)
                if prev is not None:
                    x2_tile(prev, NPAIR - 1)

            def first():
                group_inputs(0, range(GB))
                for c in range(TC):
                    cond_evac(0, c, first=True)
                    if c % 2:
                        cond_lo(0, c)
                latent_lo(0, 0)
                latent_lo(0, 1)
                head(0)

            def body(g, more):
                for u in range(1, NU):
                    score_in(g, u)
                    less_max(g, u)
                    if u + 1 < NU:
                        q_rope_sin(g, u + 1)
                    softmax_sum(g, u)
                    if u + 1 < NU:
                        rope_add_queries(g * NR + u + 2)
                    mix_lo(g, u - 1)
                    if more:
                        if u == 1:
                            dve.wait_ge(S["cond_mm"], g * TC + TC)
                            group_inputs(g + 1, (0, ))
                        group_inputs(g + 1, (u, ))
                if more:
                    cond_evac(g + 1, 0)
                mix_lo(g, NU - 1)
                if more:
                    cond_evac(g + 1, 1)
                    cond_evac(g + 1, 2)
                    cond_lo(g + 1, 1)
                    cond_evac(g + 1, 3)
                    cond_lo(g + 1, 3)
                    latent_lo(g + 1, 0)
                    latent_lo(g + 1, 1)
                    head(g + 1, prev=g)
                else:
                    for t in range(NPAIR):
                        x2_tile(g, t)

            over_groups(dve, first, body)

        @block.tensor
        def _(pe):
            def wz(g, u, t):
                if t == 0:
                    pe.wait_ge(S["mixe_lo"], g * NU + u + 1)
                    pe.wait_ge(S["mixo_lo"], g * NU + u + 1)
                pairs = [((mix_h[:, u % 2, h, t, :, :].rearrange("p j t -> p (j t)"),
                           mix_l[:, u % 2, h, t, :, :].rearrange("p j t -> p (j t)")),
                          (W["Mh"][:, 2 * u + h, :], W["Ml"][:, 2 * u + h, :])) for h in range(2)]
                last = split_product(nc, bank_o[t][:, :], pairs, start=u == 0, stop=u == NU - 1)
                if u == NU - 1:
                    last.then_inc(S["wz_mm"], 1)

            def bias_rows(g):
                pe.wait_ge(S["bias_sel_ready"], g + 1)
                nc.tensor.matmul(bank_s[:, :], K.parts["ones"][0:NSUB, :], bias_sel[:, :, :].rearrange("n b d -> n (b d)"),
                                 start=True, stop=True).then_inc(S["bias_mm"], 1)

            def cond(g, c, bk):
                if c == 0:
                    pe.wait_ge(S["x_in"], g * 16 + 16)
                    pe.wait_ge(S["wblk_ready"], g * GB + GB)
                for n in range(NPAIR):
                    last = nc.tensor.matmul(bk[:, n * P:(n + 1) * P], x_cond[:, n, c * P:(c + 1) * P],
                                            K["wblk"][:, n, :], start=True, stop=True)
                last.then_inc(S["cond_mm"], 1)

            def latent(g, i, bk):
                if i == 0:
                    pe.wait_ge(S["cond_ev"], g * TC + 3)
                for c in range(TC):
                    pe.wait_ge(S[("cond_lo_even", "cond_lo_odd")[c % 2]], g * (TC // 2) + c // 2 + 1)
                    last = split_product(nc, bk[:, :], [((W["WAh"][:, c, i * L:(i + 1) * L],
                                                          W["WAl"][:, c, i * L:(i + 1) * L]),
                                                         (cond_h[:, c, :], cond_l[:, c, :]))],
                                         start=c == 0, stop=c == TC - 1)
                last.then_inc(S["lat_mm"], 1)

            def kv_tokens(g):
                pe.wait_ge(S["lat_ev"], g * 2 + 1)
                for n in range(NPAIR):
                    last = nc.tensor.transpose(bank_b[:, n * P:(n + 1) * P], lat32[:, 0, n * P:(n + 1) * P], K.parts["ident"])
                last.then_inc(S["kvt_mm"], 1)

            def rope_keys(g):
                pe.wait_ge(S["lat_lo"], g * 2 + 2)
                split_product(nc, bank_d[:, :], [((W["WBh"][:, i, :, :].rearrange("p j d -> p (j d)"),
                                                   W["WBl"][:, i, :, :].rearrange("p j d -> p (j d)")),
                                                  (lat_h[:, i, :], lat_l[:, i, :])) for i in range(2)]
                              ).then_inc(S["kb_mm"], 1)

            def q_rope_mm(g, u):
                cols = slice(u * P, (u + 1) * P)
                split_product(nc, bank_a[:, :], [((W["WCh"][:, i, cols], W["WCl"][:, i, cols]),
                                                  (lat_h[:, i, :], lat_l[:, i, :])) for i in range(2)]
                              ).then_inc(S["qc_mm"], 1)

            def q_nope_mm(g, u, h):
                cols = slice((2 * u + h) * P, (2 * u + h + 1) * P)
                split_product(nc, (bank_b, bank_d)[h][:, :], [((W["Ah"][:, cols], W["Al"][:, cols]),
                                                               (lat_h[:, 1, :], lat_l[:, 1, :]))]
                              ).then_inc(S[f"qn{h}_mm"], 1)

            def scores(g, u):
                pe.wait_ge(S["qn0_ev"], g * NU + u + 1)
                pe.wait_ge(S["qn1_ev"], g * NU + u + 1)
                if u:
                    pe.wait_ge(S["score_ev"], g * NU + u)
                for b in range(GB):
                    cols = slice(b * C, (b + 1) * C)
                    nc.tensor.matmul(bank_s[:, cols], q_nope[:, b, :, :].rearrange("p h t -> p (h t)"),
                                     lat32[:, 0, cols], start=b == 0, stop=False)
                pe.wait_ge(S["rope_done"], g * NR + u + 2)
                for b in range(GB):
                    cols = slice(b * C, (b + 1) * C)
                    last = nc.tensor.matmul(bank_s[:, cols], q_rope[:, b, :, :].rearrange("p h t -> p (h t)"),
                                            k_rope[:, cols], start=False, stop=b == GB - 1)
                last.then_inc(S["score_mm"], 1)

            def prob_transpose(g, u):
                pe.wait_ge(S["prob_ev"], g * NU + u + 1)
                for n in range(NPAIR):
                    last = nc.tensor.transpose(bank_a[:, n * P:(n + 1) * P],
                                               prob[:, u % 2, 2 * n:2 * n + 2, :].rearrange("p j k -> p (j k)"),
                                               K.parts["ident"])
                last.then_inc(S["pt_mm"], 1)

            def mix(g, u, j):
                rows = slice(j * C, (j + 1) * C)
                bk = (bank_b, bank_d)[j]
                pe.wait_ge(S["pt_ev"], g * NU + u + 1)
                for n in range(NPAIR):
                    last = nc.tensor.matmul(bk[:, n * P:(n + 1) * P], kv_tok[rows, n, :], probT[rows, n, :],
                                            start=True, stop=True)
                last.then_inc(S[("mixe_mm", "mixo_mm")[j]], 1)

            def first():
                bias_rows(0)
                cond(0, 0, bank_d)
                pe.wait_ge(S["bias_ev"], 1)
                cond(0, 1, bank_s)
                cond(0, 2, bank_a)
                pe.wait_ge(S["cond_ev"], 2)
                cond(0, 3, bank_s)
                latent(0, 0, bank_a)
                latent(0, 1, bank_s)
                kv_tokens(0)
                head(0)

            def head(g, prev=None):
                rope_keys(g)
                q_rope_mm(g, 0)
                pe.wait_ge(S["kvt_ev"], g + 1)
                q_nope_mm(g, 0, 0)
                pe.wait_ge(S["raw_ev"], g * NR + 1)
                q_nope_mm(g, 0, 1)
                if prev is not None:
                    wz(prev, NU - 1, 2)
                pe.wait_ge(S["raw_ev"], g * NR + 2)
                q_rope_mm(g, 1)
                scores(g, 0)
                q_nope_mm(g, 1, 0)
                q_nope_mm(g, 1, 1)
                if prev is not None:
                    wz(prev, NU - 1, 3)

            def body(g, more):
                for u in range(1, NU):
                    scores(g, u)
                    if u + 1 < NU:
                        pe.wait_ge(S["raw_ev"], g * NR + u + 2)
                        if u >= 2:
                            pe.wait_ge(S["pt_ev"], g * NU + u - 1)
                        q_rope_mm(g, u + 1)
                    if u >= 2:
                        wz(g, u - 2, 0)
                    if u + 1 < NU:
                        if u >= 2:
                            pe.wait_ge(S["mixe_lo"], g * NU + u - 1)
                        q_nope_mm(g, u + 1, 0)
                    if u >= 1:
                        if u + 1 < NU:
                            pe.wait_ge(S["raw_ev"], g * NR + u + 3)
                        else:
                            pe.wait_ge(S["pt_ev"], g * NU + u - 1)
                        prob_transpose(g, u - 1)
                    if u + 1 < NU:
                        if u >= 2:
                            pe.wait_ge(S["mixo_lo"], g * NU + u - 1)
                        q_nope_mm(g, u + 1, 1)
                    if u >= 2:
                        wz(g, u - 2, 1)
                    if u >= 1:
                        if u + 1 < NU:
                            pe.wait_ge(S["qn0_ev"], g * NU + u + 2)
                        else:
                            pe.wait_ge(S["mixe_lo"], g * NU + u - 1)
                        mix(g, u - 1, 0)
                        if u + 1 < NU:
                            pe.wait_ge(S["qn1_ev"], g * NU + u + 2)
                        else:
                            pe.wait_ge(S["mixo_lo"], g * NU + u - 1)
                        mix(g, u - 1, 1)
                    if u >= 2:
                        wz(g, u - 2, 2)
                        wz(g, u - 2, 3)
                n = g * NU + NU
                g1 = g + 1
                pe.wait_ge(S["score_ev"], n)
                if more:
                    bias_rows(g1)
                wz(g, NU - 2, 0)
                pe.wait_ge(S["pt_ev"], n - 1)
                prob_transpose(g, NU - 1)
                pe.wait_ge(S["mixo_lo"], n - 1)
                if more:
                    cond(g1, 0, bank_d)
                wz(g, NU - 2, 1)
                pe.wait_ge(S["mixe_lo"], n - 1)
                mix(g, NU - 1, 0)
                if more:
                    pe.wait_ge(S["cond_ev"], g1 * TC + 1)
                mix(g, NU - 1, 1)
                if more:
                    pe.wait_ge(S["bias_ev"], g1 + 1)
                    cond(g1, 1, bank_s)
                    pe.wait_ge(S["pt_ev"], n)
                    cond(g1, 2, bank_a)
                wz(g, NU - 2, 2)
                if more:
                    pe.wait_ge(S["cond_ev"], g1 * TC + 2)
                    cond(g1, 3, bank_s)
                wz(g, NU - 2, 3)
                if more:
                    latent(g1, 0, bank_a)
                    latent(g1, 1, bank_s)
                wz(g, NU - 1, 0)
                wz(g, NU - 1, 1)
                if more:
                    kv_tokens(g1)
                    head(g1, prev=g)
                else:
                    wz(g, NU - 1, 2)
                    wz(g, NU - 1, 3)

            over_groups(pe, first, body)


EARLY = 2
SLOTS = NG - EARLY


def slot_of(g):
    return g % 2 if g < EARLY + 2 else g - EARLY


def routing(nc, K, A, x2, flat, R):
    with ExitStack() as ctx:
        def sb(name, shape, dt=F32):
            return ctx.enter_context(nc.sbuf_tensor(name, shape, dt))

        def bank(name):
            return ctx.enter_context(nc.psum_tensor(name, [P, 512], F32))

        def sem(name):
            return ctx.enter_context(nc.semaphore(name))

        NR = NADAPT * RANK
        EJ = NE * NT
        load_table(nc, ctx, K, "route")
        c = K.parts
        NV = 5
        raw = sb("routing_raw", [P, TC * T + T + TC * NR])
        w_raw = raw[:, 0:TC * T].rearrange("p (c n) -> p c n", c=TC)
        a_raw = raw[:, TC * T:TC * T + T]
        b_raw = raw[:, TC * T + T:].rearrange("p (c n r) -> p c n r", c=TC, n=NADAPT)
        row = raw[:, 0:EJ * NV * NCH // 2].bitcast(BF16).rearrange("p (n v c) -> p n v c", v=NV, c=NCH)
        is_hi = raw[:, TC * T + T:].bitcast(BF16).rearrange("p (n c) -> p n c", c=NCH)
        wg = sb("wg", [P, TC, NE])
        bg = sb("bg", [P, NE])
        adapt, scal = sb("adapt", [P, B], I32), sb("scal", [P, 1])
        lora_sel = sb("lora_sel", [P, B])
        WTh, WTl = sb("WTh", [P, TC, T], F32R), sb("WTl", [P, TC, T], F32R)
        ATh, ATl = sb("ATh", [P, TC, NR], F32R), sb("ATl", [P, TC, NR], F32R)
        BTh, BTl = sb("BTh", [NR, T], F32R), sb("BTl", [NR, T], F32R)
        WG = sb("WG", [P, TC + 1, 2, NE], F32R)
        logitT = sb("logitT", [2 * NE, GT])
        x_in_sb = sb("x_in_sb", [P, 2, NPAIR, T])
        xTh, xTl = sb("xTh", [P, SLOTS, TC, GT], F32R), sb("xTl", [P, SLOTS, TC, GT], F32R)
        low32 = sb("low32", [NR, GT])
        lowh, lowl = sb("lowh", [NR, SLOTS, GT], F32R), sb("lowl", [NR, SLOTS, GT], F32R)
        flat_sb = sb("flat_sb", [P, 4, T])
        logit = sb("logit", [P, NT, NE])
        bank_t = [bank(f"r_t{i}") for i in range(TC)]
        bank_x, bank_l, bank_f = bank("r_x"), bank("r_l"), [bank("r_f0"), bank("r_f1")]

        cmpk = sb("cmpk", [P, NE, NT, NE])
        rank, top = sb("rank", [P, NT, NE]), sb("top", [P, NT, NE])
        lmax = sb("lmax", [P, NT])
        ex, ey, ek, ep, e2 = (sb(n, [P, NT, NE]) for n in ("ex", "ey", "ek", "ep", "e2"))
        ei = sb("ei", [P, NT, NE], I32)
        esum, einv = sb("esum", [P, NT]), sb("einv", [P, NT])
        gate, key = sb("gate", [P, NE, NT]), sb("key", [P, NE, NT])
        thr = sb("thr", [P, NE], I32)
        cand = sb("cand", [P, NE, 3], I32)
        above = sb("above", [P, NE, 3, NT])
        count = sb("count", [P, NE, 3])
        hit = sb("hit", [P, NE, 3])
        step_bits = sb("step_bits", [P, NE], I32)
        positive = sb("positive", [P, NE])
        thrf = sb("thrf", [P, NE])
        over, same = sb("over", [P, NE, NT]), sb("same", [P, NE, NT])
        need = sb("need", [P, NE])
        mark = sb("mark", [P, NE, NT], BF16)
        ones_b, before_b = sb("ones_b", [P, P], BF16), sb("before_b", [P, P], BF16)
        iota_b = sb("iota_b", [P, P], BF16)
        chosen = sb("chosen", [P, NE, NT])
        pos = sb("pos", [P, NE, NT], I32)
        pos_lo, pos_hi = sb("pos_lo", [P, NE, NT], I32), sb("pos_hi", [P, NE, NT], I32)
        slot_lo, slot_hi = sb("slot_lo", [P, NE, NT]), sb("slot_hi", [P, NE, NT])
        part3 = sb("part3", [P, 3, NE, NT], BF16)
        rest = sb("rest", [P, 2, NE, NT])
        value = sb("value", [P, EJ, NV], BF16)
        LQ, LBUF = NT // 2, 4
        is_lo = x_in_sb[:, :, :, :].rearrange("p k n t -> p (k n t)").bitcast(BF16).rearrange(
            "p (q j s) -> p q j s", q=LBUF, j=LQ)
        listed = sb("listed", [P, NV, NCH])
        tokf = sb("tokf", [P, NCH])

        names = """w_in a_in wt_mm wt_hi wt_lo at_mm at_hi at_lo bt_mm bt_hi bt_lo wg_mm wg_hi wg_lo sel_ready
            xt_mm xt_hi xt_lo low_mm low_ev low_hi low_lo lgt_mm lgt_ev lg_mm lg_ev fl_mm fl_ev
            chain count_ready count_mm hi_ready row_ready prefix_ready prefix_mm lo_ready list_mm list_ev table_in""".split()
        S = {n: sem("rt_" + n) for n in names}
        x_in = [sem(f"rt_x_in{k}") for k in range(2)]
        fl_out = [sem(f"rt_fl_out{k}") for k in range(4)]
        x_d = x2.rearrange("(g n j) c t -> g (j c) n t", n=NPAIR, j=2)
        flat_d = flat.rearrange("(n p) t -> n p t", p=P)

        block = ctx.enter_context(nc.Block())

        @block.sync
        def _(sp):
            sp.dma_start(w_raw[:, :, :], A["W"].rearrange("(c p) n -> p c n", p=P)).then_inc(S["w_in"], 16)
            sp.dma_start(a_raw[:, :], A["A"].rearrange("n r d -> (n r) d")).then_inc(S["w_in"], 16)
            for g in range(2):
                sp.dma_start(x_in_sb[:, g, :, :], x_d[g]).then_inc(x_in[g], 16)
            with nc.allow_non_contiguous_dma(reason="small operands, once"):
                for i in range(TC):
                    sp.dma_start(b_raw[:, i, :, :], A["Bm"][:, i * P:(i + 1) * P, :].rearrange("n p r -> p n r")
                                 ).then_inc(S["a_in"], 16)
                sp.dma_start(wg[:, :, :], A["Wg"].rearrange("(c p) e -> p c e", p=P)).then_inc(S["a_in"], 16)
                sp.dma_start(bg[:, :], A["bg"].partition_broadcast(P)).then_inc(S["a_in"], 16)
                sp.dma_start(adapt[:, :], A["adapt"].partition_broadcast(P)).then_inc(S["a_in"], 16)
                for n in range(NADAPT):
                    sp.dma_start(scal[n * RANK:(n + 1) * RANK, :],
                                 A["scalings"][n:n + 1].partition_broadcast(RANK)).then_inc(S["a_in"], 16)
            sp.dma_start(K["route"][:, :], A["route"]).then_inc(S["table_in"], 16)
            for g in range(2, NG):
                sp.wait_ge(S["xt_mm"], (g - 1) * TC)
                sp.dma_start(x_in_sb[:, g % 2, :, :], x_d[g]).then_inc(x_in[g % 2], 16)

        A_IN = 16 * (TC + 3 + NADAPT)

        @block.gpsimd
        def _(pool):
            pool.wait_ge(S["hi_ready"], 1)
            for e in range(NE):
                mine = slice(e * NT, (e + 1) * NT)
                nc.gpsimd.tensor_tensor(row[:, mine, :, :], is_hi[:, mine, :].unsqueeze(2).to_broadcast([P, NT, NV, NCH]),
                                        value[:, mine, :].unsqueeze(3).to_broadcast([P, NT, NV, NCH]),
                                        ALU.mult).then_inc(S["row_ready"], 1)

        @block.scalar
        def _(act):
            def copy(out, bk, ready, count, done):
                act.wait_ge(S[ready], count)
                nc.scalar.copy(out, bk).then_inc(S[done], 1)

            for i in range(TC):
                copy(WTh[:, i, :], bank_t[i][:, :], "wt_mm", i + 1, "wt_hi")
            copy(ATh[:, :, :], bank_x[:, :].rearrange("p (c n) -> p c n", c=TC), "at_mm", 1, "at_hi")
            copy(BTh[:, :], bank_f[0][:, :], "bt_mm", 1, "bt_hi")
            copy(WG[:, :, 0, :], bank_l[:, 0:(TC + 1) * NE].rearrange("p (c e) -> p c e", e=NE), "wg_mm", 1, "wg_hi")

            def logits(g):
                copy(logitT[:, :], bank_l[0:2 * NE, :], "lgt_mm", g + 1, "lgt_ev")

            def front(g):
                s = slot_of(g)
                for i in range(TC):
                    copy(xTh[:, s, i, :], bank_t[i][:, :], "xt_mm", g * TC + i + 1, "xt_hi")
                if g:
                    logits(g - 1)
                act.wait_ge(S["low_ev"], g + 1)
                nc.scalar.copy(lowh[:, s, :], low32[:, :]).then_inc(S["low_hi"], 1)

            def back_tile(n):
                act.wait_ge(S["fl_mm"], n + 1)
                if n >= 4:
                    act.wait_ge(fl_out[n % 4], 16 * (n // 4))
                nc.scalar.copy(flat_sb[:, n % 4, :], bank_f[n % 2][:, :]).then_inc(S["fl_ev"], 1)
                act.wait_ge(S["fl_ev"], n + 1)
                act.dma_start(flat_d[n], flat_sb[:, n % 4, :]).then_inc(fl_out[n % 4], 16)

            def back(g):
                for t in range(NPAIR):
                    back_tile(g * NPAIR + t)

            for g in range(NG):
                front(g)
                if 1 <= g <= EARLY:
                    back(g - 1)
            back_tile(EARLY * NPAIR)
            logits(NG - 1)
            for n in range(EARLY * NPAIR + 1, NT):
                back_tile(n)
            for k in range(4):
                act.wait_ge(fl_out[k], 16 * (NT // 4))

        @block.vector
        def _(dve):
            v = nc.vector
            steps = [0]

            def link(instruction):
                steps[0] += 1
                instruction.then_inc(S["chain"], 1)
                dve.wait_ge(S["chain"], steps[0])

            def low_part(out, bk, hi, ready, count, done):
                dve.wait_ge(S[ready], count)
                v.tensor_tensor(out, bk, hi.bitcast(F32), ALU.subtract).then_inc(S[done], 1)

            for i in range(TC):
                low_part(WTl[:, i, :], bank_t[i][:, :], WTh[:, i, :], "wt_hi", i + 1, "wt_lo")
            low_part(ATl[:, :, :], bank_x[:, :].rearrange("p (c n) -> p c n", c=TC), ATh[:, :, :], "at_hi", 1, "at_lo")
            low_part(BTl[:, :], bank_f[0][:, :], BTh[:, :], "bt_hi", 1, "bt_lo")
            low_part(WG[:, :, 1, :], bank_l[:, 0:(TC + 1) * NE].rearrange("p (c e) -> p c e", e=NE), WG[:, :, 0, :],
                     "wg_hi", 1, "wg_lo")
            dve.wait_ge(S["a_in"], A_IN)
            dve.wait_ge(S["table_in"], 16)
            link(v.tensor_scalar(lora_sel[:, :], adapt[:, :], c["adapter"], None, ALU.is_equal))
            link(v.tensor_scalar(lora_sel[:, :], lora_sel[:, :], scal[:, :], None, ALU.mult))

            def front(g):
                s = slot_of(g)
                for i in range(TC):
                    low_part(xTl[:, s, i, :], bank_t[i][:, :], xTh[:, s, i, :], "xt_hi", g * TC + i + 1, "xt_lo")
                dve.wait_ge(S["low_mm"], g + 1)
                v.tensor_tensor(low32[:, :].rearrange("p (b t) -> p b t", b=GB),
                                bank_x[:, :].rearrange("p (b t) -> p b t", b=GB),
                                lora_sel[:, g * GB:(g + 1) * GB].unsqueeze(2).to_broadcast([NR, GB, C]),
                                ALU.mult).then_inc(S["low_ev"], 1)
                dve.wait_ge(S["low_hi"], g + 1)
                v.tensor_tensor(lowl[:, s, :], low32[:, :], lowh[:, s, :].bitcast(F32),
                                ALU.subtract).then_inc(S["low_lo"], 1)

            def logits_out(g):
                dve.wait_ge(S["lg_mm"], g + 1)
                v.tensor_tensor(logit[:, g * NPAIR:(g + 1) * NPAIR, :],
                                bank_l[:, 0:NPAIR * NE].rearrange("p (t e) -> p t e", e=NE),
                                bg[:, :].unsqueeze(1).to_broadcast([P, NPAIR, NE]), ALU.add).then_inc(S["lg_ev"], 1)

            for g in range(NG):
                front(g)
                if g:
                    logits_out(g - 1)
            logits_out(NG - 1)
            dve.wait_ge(S["lg_ev"], NG)

            link(v.memset(cmpk[:, :, :, :], 0.0))
            for k in range(NE):
                one = logit[:, :, k:k + 1]
                if k + 1 < NE:
                    v.tensor_tensor(cmpk[:, k, :, k + 1:NE], one.to_broadcast([P, NT, NE - 1 - k]),
                                    logit[:, :, k + 1:NE], ALU.is_ge)
                if k:
                    v.tensor_tensor(cmpk[:, k, :, 0:k], one.to_broadcast([P, NT, k]), logit[:, :, 0:k], ALU.is_gt)
            link(v.tensor_reduce(lmax[:, :], logit[:, :, :], AX, ALU.max))
            link(v.tensor_reduce(rank[:, :, :], cmpk[:, :, :, :].rearrange("p k j e -> p j e k"), AX, ALU.add))
            link(v.tensor_scalar(top[:, :, :], rank[:, :, :], 1.5, None, ALU.is_lt))

            link(v.tensor_tensor(ex[:, :, :], logit[:, :, :], lmax[:, :].unsqueeze(2).to_broadcast([P, NT, NE]),
                                 ALU.subtract))
            link(v.tensor_scalar(ex[:, :, :], ex[:, :, :], -87.0, None, ALU.max))
            link(v.tensor_scalar(ey[:, :, :], ex[:, :, :], float(np.float32(np.log2(np.e))), 12582912.0,
                                 ALU.mult, ALU.add))
            link(v.tensor_scalar(ek[:, :, :], ey[:, :, :], 12582912.0, None, ALU.subtract))
            link(v.scalar_tensor_tensor(out=ex[:, :, :], in0=ek[:, :, :], scalar=-0.693359375, in1=ex[:, :, :],
                                        op0=ALU.mult, op1=ALU.add))
            link(v.scalar_tensor_tensor(out=ex[:, :, :], in0=ek[:, :, :], scalar=2.12194440e-4, in1=ex[:, :, :],
                                        op0=ALU.mult, op1=ALU.add))
            coefficients = [1.0 / n for n in (5040.0, 720.0, 120.0, 24.0, 6.0, 2.0, 1.0)]
            link(v.tensor_scalar(ep[:, :, :], ex[:, :, :], coefficients[0], None, ALU.mult))
            for k in coefficients[1:]:
                link(v.scalar_tensor_tensor(out=ep[:, :, :], in0=ep[:, :, :], scalar=k, in1=ex[:, :, :],
                                            op0=ALU.add, op1=ALU.mult))
            link(v.tensor_scalar(ei[:, :, :], ek[:, :, :], 127.0, 8388608.0, ALU.add, ALU.mult))
            link(v.scalar_tensor_tensor(out=e2[:, :, :], in0=ep[:, :, :], scalar=1.0,
                                        in1=ei[:, :, :].bitcast(F32), op0=ALU.add, op1=ALU.mult))
            link(v.tensor_tensor(e2[:, :, :], e2[:, :, :], top[:, :, :], ALU.mult))
            link(v.tensor_reduce(esum[:, :], e2[:, :, :], AX, ALU.add))
            link(v.reciprocal(einv[:, :], esum[:, :]))
            link(v.tensor_tensor(gate[:, :, :].rearrange("p e j -> p j e"), e2[:, :, :],
                                 einv[:, :].unsqueeze(2).to_broadcast([P, NT, NE]), ALU.mult))
            link(v.scalar_tensor_tensor(out=key[:, :, :].rearrange("p e j -> p j e"), in0=top[:, :, :], scalar=-1.0,
                                        in1=gate[:, :, :].rearrange("p e j -> p j e"), op0=ALU.add, op1=ALU.add))

            counts = [0]

            def total(mask, width):
                link(v.tensor_reduce(count[:, :, 0:width], mask, AX, ALU.add))
                counts[0] += 1
                v.tensor_copy(hit[:, :, 0:width], count[:, :, 0:width]).then_inc(S["count_ready"], 1)
                dve.wait_ge(S["count_mm"], counts[0])

            totals = bank_l[:, 0:NE * 3].rearrange("p (e c) -> p e c", c=3)
            link(v.memset(hit[:, :, :], 0.0))
            link(v.tensor_scalar(above[:, :, 0, :], key[:, :, :], 0.0, None, ALU.is_ge))
            total(above[:, :, 0:1, :], 1)
            link(v.tensor_scalar(positive[:, :].unsqueeze(2), totals[:, :, 0:1], float(CAP), None, ALU.is_ge))
            link(v.memset(thr[:, :], 0))
            for i in range(TRIALS):
                trial = c["trial"][:, 3 * i:3 * i + 3].bitcast(I32)
                link(v.tensor_tensor(cand[:, :, :], thr[:, :].unsqueeze(2).to_broadcast([P, NE, 3]),
                                     trial.unsqueeze(1).to_broadcast([P, NE, 3]), ALU.bitwise_or))
                link(v.tensor_tensor(above[:, :, :, :], key[:, :, :].unsqueeze(2).to_broadcast([P, NE, 3, NT]),
                                     cand[:, :, :].bitcast(F32).unsqueeze(3).to_broadcast([P, NE, 3, NT]),
                                     ALU.is_ge))
                total(above[:, :, :, :], 3)
                link(v.tensor_scalar(hit[:, :, :], totals, float(CAP), float(1 << (2 * (TRIALS - 1 - i))),
                                     ALU.is_ge, ALU.mult))
                with nc.allow_low_precision(reason="at most three equal powers of two: exact"):
                    link(v.tensor_reduce(step_bits[:, :], hit[:, :, :], AX, ALU.add))
                link(v.tensor_tensor(thr[:, :], thr[:, :], step_bits[:, :], ALU.bitwise_or))
            link(v.tensor_tensor(thrf[:, :], thr[:, :].bitcast(F32), positive[:, :], ALU.mult))
            link(v.scalar_tensor_tensor(out=thrf[:, :], in0=positive[:, :], scalar=-1.0, in1=thrf[:, :],
                                        op0=ALU.add, op1=ALU.add))

            limit = thrf[:, :].unsqueeze(2).to_broadcast([P, NE, NT])
            link(v.tensor_tensor(over[:, :, :], key[:, :, :], limit, ALU.is_gt))
            link(v.tensor_tensor(same[:, :, :], key[:, :, :], limit, ALU.is_equal))
            total(over[:, :, :].unsqueeze(2), 1)
            link(v.tensor_scalar(need[:, :].unsqueeze(2), totals[:, :, 0:1], -1.0, float(CAP), ALU.mult, ALU.add))
            link(v.tensor_copy(ones_b[:, :], c["ones"]))
            link(v.tensor_copy(before_b[:, :], c["before"]))
            link(v.tensor_copy(iota_b[:, :], c["iota"]))
            earlier = bank_x[:, 0:EJ].rearrange("p (e j) -> p e j", e=NE)
            v.tensor_copy(mark[:, :, :], same[:, :, :]).then_inc(S["prefix_ready"], 1)
            dve.wait_ge(S["prefix_mm"], 1)
            link(v.tensor_tensor(chosen[:, :, :], earlier, need[:, :].unsqueeze(2).to_broadcast([P, NE, NT]),
                                 ALU.is_lt))
            link(v.tensor_tensor(chosen[:, :, :], chosen[:, :, :], same[:, :, :], ALU.mult))
            link(v.tensor_tensor(chosen[:, :, :], chosen[:, :, :], over[:, :, :], ALU.add))
            v.tensor_copy(mark[:, :, :], chosen[:, :, :]).then_inc(S["prefix_ready"], 1)
            val = value[:, :, :].rearrange("p (e j) v -> p e j v", e=NE)
            v.tensor_copy(val[:, :, :, 0], c["tile"].unsqueeze(1).to_broadcast([P, NE, NT]))
            v.tensor_copy(val[:, :, :, 1], c["part"].unsqueeze(2).to_broadcast([P, NE, NT]))
            link(v.tensor_copy(part3[:, 0, :, :], gate[:, :, :]))
            link(v.tensor_tensor(rest[:, 0, :, :], gate[:, :, :], part3[:, 0, :, :], ALU.subtract))
            link(v.tensor_copy(part3[:, 1, :, :], rest[:, 0, :, :]))
            link(v.tensor_tensor(rest[:, 1, :, :], rest[:, 0, :, :], part3[:, 1, :, :], ALU.subtract))
            link(v.tensor_copy(part3[:, 2, :, :], rest[:, 1, :, :]))
            for k in range(3):
                link(v.tensor_copy(val[:, :, :, 2 + k], part3[:, k, :, :]))
            dve.wait_ge(S["prefix_mm"], 2)
            link(v.scalar_tensor_tensor(out=rest[:, 0, :, :], in0=earlier, scalar=1.0, in1=chosen[:, :, :],
                                        op0=ALU.add, op1=ALU.mult))
            link(v.tensor_scalar(pos[:, :, :], rest[:, 0, :, :], 1.0, None, ALU.subtract))
            v.tensor_scalar(pos_lo[:, :, :], pos[:, :, :], P - 1, None, ALU.bitwise_and)
            link(v.tensor_scalar(pos_hi[:, :, :], pos[:, :, :], 7, None, ALU.arith_shift_right))
            link(v.tensor_copy(slot_lo[:, :, :], pos_lo[:, :, :]))
            link(v.tensor_copy(slot_hi[:, :, :], pos_hi[:, :, :]))
            v.tensor_tensor(is_hi[:, :, :],
                            slot_hi[:, :, :].rearrange("p e j -> p (e j)").unsqueeze(2).to_broadcast([P, EJ, NCH]),
                            c["iota"][:, 0:NCH].unsqueeze(1).to_broadcast([P, EJ, NCH]),
                            ALU.is_equal).then_inc(S["hi_ready"], 1)

            def lo_tiles(q):
                e, j = q * LQ // NT, q * LQ % NT
                if q >= LBUF:
                    dve.wait_ge(S["list_mm"], (q - LBUF + 1) * LQ)
                v.tensor_tensor(is_lo[:, q % LBUF, :, :], iota_b[:, :].unsqueeze(1).to_broadcast([P, LQ, P]),
                                slot_lo[:, e, j:j + LQ].unsqueeze(2).to_broadcast([P, LQ, P]),
                                ALU.is_equal).then_inc(S["lo_ready"], 1)

            for q in range(LBUF):
                lo_tiles(q)
            for e in range(NE):
                for q in range(e * (NT // LQ) + LBUF, min((e + 1) * (NT // LQ) + LBUF, NE * NT // LQ)):
                    lo_tiles(q)
                dve.wait_ge(S["list_mm"], (e + 1) * NT)
                link(v.tensor_copy(listed[:, :, :], bank_l[:, 0:NV * NCH].rearrange("p (v c) -> p v c", v=NV)))
                v.scalar_tensor_tensor(out=R["token"][:, e * NCH:(e + 1) * NCH], in0=listed[:, 0, :], scalar=float(P),
                                       in1=listed[:, 1, :], op0=ALU.mult, op1=ALU.add)
                link(v.tensor_tensor(tokf[:, :], listed[:, 2, :], listed[:, 3, :], ALU.add))
                v.tensor_tensor(R["gate"][:, e * NCH:(e + 1) * NCH], tokf[:, :], listed[:, 4, :], ALU.add).then_inc(S["list_ev"], 1)
                dve.wait_ge(S["list_ev"], e + 1)

        @block.tensor
        def _(pe):
            ident = c["ident"]
            pe.wait_ge(S["w_in"], 32)
            for i in range(TC):
                for o in range(TC):
                    last = nc.tensor.transpose(bank_t[i][:, o * P:(o + 1) * P], w_raw[:, o, i * P:(i + 1) * P], ident)
                last.then_inc(S["wt_mm"], 1)
            for i in range(TC):
                last = nc.tensor.transpose(bank_x[:, i * P:(i + 1) * P], a_raw[:, i * P:(i + 1) * P], ident)
            last.then_inc(S["at_mm"], 1)
            pe.wait_ge(S["a_in"], A_IN)
            for o in range(TC):
                last = nc.tensor.transpose(bank_f[0][:, o * P:(o + 1) * P],
                                           b_raw[:, o, :, :].rearrange("p n r -> p (n r)"), ident)
            last.then_inc(S["bt_mm"], 1)
            for i in range(TC + 1):
                for o in range(TC):
                    left = w_raw[:, o, i * P:(i + 1) * P] if i < TC else b_raw[:, o, :, :].rearrange("p n r -> p (n r)")
                    last = nc.tensor.matmul(bank_l[:, i * NE:(i + 1) * NE], left, wg[:, o, :],
                                            start=o == 0, stop=o == TC - 1)
            last.then_inc(S["wg_mm"], 1)

            def front(g):
                s = slot_of(g)
                pe.wait_ge(x_in[g % 2], 16 * (g // 2 + 1))
                if g:
                    pe.wait_ge(S["xt_lo"], g * TC)
                else:
                    pe.wait_ge(S["wt_lo"], TC)
                for i in range(TC):
                    for t in range(NPAIR):
                        last = nc.tensor.transpose(bank_t[i][:, t * P:(t + 1) * P],
                                                   x_in_sb[:, g % 2, t, i * P:(i + 1) * P], ident)
                    last.then_inc(S["xt_mm"], 1)
                if g:
                    logitsT(g - 1)
                pe.wait_ge(S["at_lo"], 1)
                if g:
                    pe.wait_ge(S["low_ev"], g)
                for i in range(TC):
                    pe.wait_ge(S["xt_lo"], g * TC + i + 1)
                    last = split_product(nc, bank_x[:, :], [((ATh[:, i, :], ATl[:, i, :]),
                                                             (xTh[:, s, i, :], xTl[:, s, i, :]))],
                                         start=i == 0, stop=i == TC - 1)
                last.then_inc(S["low_mm"], 1)
                if g:
                    logits(g - 1)

            def operands(g, t):
                s, cols = slot_of(g), slice(t * P, (t + 1) * P)
                return [(xTh[:, s, i, cols], xTl[:, s, i, cols]) for i in range(TC)] + [(lowh[:, s, cols],
                                                                                         lowl[:, s, cols])]

            def logitsT(g):
                pe.wait_ge(S["low_lo"], g + 1)
                pe.wait_ge(S["wg_lo"], 1)
                if g:
                    pe.wait_ge(S["lg_ev"], g)
                s = slot_of(g)
                parts = [(xTh[:, s, i, :], xTl[:, s, i, :]) for i in range(TC)] + [(lowh[:, s, :], lowl[:, s, :])]
                for i, part in enumerate(parts):
                    for j in range(2):
                        last = nc.tensor.matmul(bank_l[0:2 * NE, :], WG[:, i, :, :].rearrange("p j e -> p (j e)"),
                                                part[j], start=i == j == 0, stop=i == TC and j == 1)
                last.then_inc(S["lgt_mm"], 1)

            def logits(g):
                pe.wait_ge(S["lgt_ev"], g + 1)
                for t in range(NPAIR):
                    last = nc.tensor.matmul(bank_l[:, t * NE:(t + 1) * NE], logitT[:, t * P:(t + 1) * P],
                                            c["fold"][0:2 * NE, :], start=True, stop=True)
                last.then_inc(S["lg_mm"], 1)

            def project(g, t):
                n = g * NPAIR + t
                pe.wait_ge(S["bt_lo"], 1)
                if n >= 2:
                    pe.wait_ge(S["fl_ev"], n - 1)
                weights = [(WTh[:, i, :], WTl[:, i, :]) for i in range(TC)] + [(BTh[:, :], BTl[:, :])]
                split_product(nc, bank_f[n % 2][:, :], list(zip(operands(g, t), weights))).then_inc(S["fl_mm"], 1)

            front(0)
            for g in range(EARLY):
                front(g + 1)
                for t in range(NPAIR):
                    project(g, t)
            late = [(g, t) for g in range(EARLY, NG) for t in range(NPAIR)]
            for g in range(EARLY + 1, NG):
                front(g)
            project(*late.pop(0))
            logitsT(NG - 1)
            project(*late.pop(0))
            logits(NG - 1)
            for _ in range(3):
                project(*late.pop(0))

            done = [0, 0]

            def count_total():
                done[0] += 1
                pe.wait_ge(S["count_ready"], done[0])
                nc.tensor.matmul(bank_l[:, 0:NE * 3], c["ones"], hit[:, :, :].rearrange("p e c -> p (e c)"),
                                 start=True, stop=True).then_inc(S["count_mm"], 1)

            def prefix():
                done[1] += 1
                pe.wait_ge(S["prefix_ready"], done[1])
                all_marks = mark[:, :, :].rearrange("p e j -> p (e j)")
                out = bank_x[:, 0:EJ].rearrange("p (e j) -> p e j", e=NE)
                nc.tensor.matmul(bank_x[:, 0:EJ], before_b[:, :], all_marks, start=True, stop=False)
                for j in range(NT - 1):
                    last = nc.tensor.matmul(out[:, :, j + 1:NT], ones_b[:, :],
                                            mark[:, :, j:j + 1].to_broadcast([P, NE, NT - 1 - j]),
                                            start=False, stop=j == NT - 2)
                last.then_inc(S["prefix_mm"], 1)

            for i in range(TRIALS + 1):
                count_total()
                if late:
                    project(*late.pop(0))
            count_total()
            prefix()
            project(*late.pop(0))
            prefix()
            project(*late.pop(0))
            for e in range(NE):
                pe.wait_ge(S["row_ready"], e + 1)
                if e:
                    pe.wait_ge(S["list_ev"], e)
                for j in range(NT):
                    n = e * NT + j
                    if late and j == NT // 2:
                        project(*late.pop(0))
                    if j % LQ == 0:
                        pe.wait_ge(S["lo_ready"], n // LQ + 1)
                    nc.tensor.matmul(bank_l[:, 0:NV * NCH], is_lo[:, n // LQ % LBUF, j % LQ, :],
                                     row[:, n, :, :].rearrange("p v c -> p (v c)"),
                                     start=j == 0, stop=j == NT - 1).then_inc(S["list_mm"], 1)


def experts(nc, K, A, out, flat, R):
    with ExitStack() as ctx:
        def sb(name, shape, dt=F32):
            return ctx.enter_context(nc.sbuf_tensor(name, shape, dt))

        def bank(name):
            return ctx.enter_context(nc.psum_tensor(name, [P, 512], F32))

        def sem(name):
            return ctx.enter_context(nc.semaphore(name))

        BT = 512
        CH = BT // P
        PER = CAP // BT
        NB = NE * PER
        PAIRS = HC // 2
        tok_in, tok_out = sb("tok_in", [P, CH], I32), sb("tok_out", [P, CH], I32)
        rows = sb("rows", [P, CH, T])
        xh, xl = sb("xh", [P, 2, TC, BT], F32R), sb("xl", [P, 2, TC, BT], F32R)
        w1_raw = sb("w1_raw", [P, PAIRS, TC, 2, P])
        w2_raw = sb("w2_raw", [P, PAIRS, 2, T])
        w1h, w1l = sb("w1h", [P, 2, TC, P], F32R), sb("w1l", [P, 2, TC, P], F32R)
        w2h, w2l = sb("w2h", [P, 2, T], F32R), sb("w2l", [P, 2, T], F32R)
        hid = sb("hid", [P, 2, BT])
        hh, hl = sb("hh", [P, 2, BT], F32R), sb("hl", [P, 2, BT], F32R)
        y_sb = sb("y_sb", [P, CH, T])
        wait_here = sb("wait_there", [1, 3])
        bank_x = [bank("e_x0"), bank("e_x1")]
        bank_h = [bank("e_h0"), bank("e_h1")]
        bank_y = [bank(f"e_y{i}") for i in range(CH)]
        names = """w1_hi w1_lo w2_hi w2_lo index_in index_out rows_in xt_mm xt_hi xt_lo h_mm h_act h_hi h_lo
            y_mm y_ev scattered here""".split()
        S = {n: sem("ex_" + n) for n in names}
        waited = [sem(f"ex_waited{k}") for k in range(2)]
        w_in = [sem(f"ex_w_in{m}") for m in range(PAIRS)]
        block = ctx.enter_context(nc.Block())
        w1_d = A["W1"].rearrange("e (c p) (m n) -> e m p c n", p=P, n=2 * P)
        w2_d = A["W2"].rearrange("e (m k p) n -> e m p k n", p=P, k=2)
        out_rows = out.rearrange("b c t -> (b c) t")

        LOOP = (HC - 4) // 2
        Y0 = 2

        def over_batches(eng, first, body):
            first()
            with eng.Fori(0, NB - 1) as b:
                body(b, True)
            body(NB - 1, False)

        def w_arrived(eng, b, pair):
            eng.wait_ge(w_in[pair], (b // PER + 1) * 32)

        def rounds(eng, b, more, one):
            with eng.Fori(0, LOOP) as i:
                for k in range(2):
                    one(b * HC + 2 * i + 2 + k, k, (b, i + 2, k), (b, i + 1 + k, 1 - k))
            last = b * HC + HC
            one(last - 2, 0, (b + 1, 0, 0) if more else None, (b, PAIRS - 1, 1))
            one(last - 1, 1, (b + 1, 0, 1) if more else None, (b + 1, 0, 0) if more else None)

        def seam(b, one, between):
            n = b * HC + HC
            one(n, 0, (b + 1, 1, 0), (b + 1, 0, 1))
            between()
            one(n + 1, 1, (b + 1, 1, 1), (b + 1, 1, 0))

        @block.sync
        def _(sp):
            def load(e, m):
                with nc.allow_non_contiguous_dma(reason="rows of 1 KiB"):
                    sp.dma_start(w1_raw[:, m, :, :, :].rearrange("p c k n -> p c (k n)"), w1_d[e, m]
                                 ).then_inc(w_in[m], 16)
                sp.dma_start(w2_raw[:, m, :, :], w2_d[e, m]).then_inc(w_in[m], 16)

            load(0, 0)
            sp.wait_ge(S["rows_in"], CH * 16)
            for m in range(1, PAIRS):
                load(0, m)
            with sp.Fori(1, NE) as e:
                for m in range(PAIRS):
                    for n in ("w1_hi", "w1_lo", "w2_hi", "w2_lo"):
                        sp.wait_ge(S[n], (e * PER - 1) * HC + 2 * m + 2)
                    load(e, m)

        @block.gpsimd
        def _(pool):
            def w1_low(n, k, b, pair, chunk):
                pool.wait_ge(S["w1_hi"], n + 1)
                nc.gpsimd.tensor_tensor(w1l[:, k, :, :], w1_raw[:, pair, :, chunk, :], w1h[:, k, :, :].bitcast(F32),
                                        ALU.subtract).then_inc(S["w1_lo"], 1)

            def w2_low(n, k, b, pair, chunk):
                pool.wait_ge(S["w2_hi"], n + 1)
                nc.gpsimd.tensor_tensor(w2l[:, k, :], w2_raw[:, pair, chunk, :], w2h[:, k, :].bitcast(F32),
                                        ALU.subtract).then_inc(S["w2_lo"], 1)

            def one(n, k, w1, w2):
                if w1:
                    w1_low(n + 2, k, *w1)
                if w2:
                    w2_low(n + 1, 1 - k, *w2)

            def take_waits(b, k):
                pool.wait_ge(waited[k], b + 1)
                nc.gpsimd.tensor_tensor(wait_here[:, 1 + k:2 + k], wait_here[:, 0:1], wait_here[:, 0:1],
                                        ALU.add).then_inc(waited[k], 1)

            def gather(b):
                pool.wait_ge(S["index_in"], b + 1)
                take_waits(b, 0)
                for c in range(CH):
                    pool.indirect_dma_start(rows[:, c, :], None, flat,
                                            bass.IndirectOffsetOnAxis(ap=tok_in[:, c:c + 1], axis=0)
                                            ).then_inc(S["rows_in"], 16)

            def scatter(b):
                pool.wait_ge(S["index_out"], b + 1)
                pool.wait_ge(S["y_ev"], (b + 1) * CH)
                take_waits(b, 1)
                for c in range(CH):
                    pool.indirect_dma_start(out_rows, bass.IndirectOffsetOnAxis(ap=tok_out[:, c:c + 1], axis=0),
                                            y_sb[:, c, :], None, compute_op=ALU.add).then_inc(S["scattered"], 16)

            def first():
                nc.gpsimd.memset(wait_here[:, :], 0.0).then_inc(S["here"], 1)
                pool.wait_ge(S["here"], 1)
                for k in range(2):
                    pool.sem_inc(waited[k], 1)
                gather(0)
                w1_low(0, 0, 0, 0, 0)
                w1_low(1, 1, 0, 0, 1)
                w2_low(0, 0, 0, 0, 0)
                one(0, 0, (0, 1, 0), (0, 0, 1))
                one(1, 1, (0, 1, 1), (0, 1, 0))

            def body(b, more):
                if more:
                    gather(b + 1)
                rounds(pool, b, more, one)
                if more:
                    seam(b, one, lambda: scatter(b))
                else:
                    scatter(b)
                pool.wait_ge(S["scattered"], (b + 1) * CH * 16)

            over_batches(pool, first, body)

        @block.scalar
        def _(act):
            def w1_high(n, k, b, pair, chunk):
                w_arrived(act, b, pair)
                nc.scalar.copy(w1h[:, k, :, :], w1_raw[:, pair, :, chunk, :]).then_inc(S["w1_hi"], 1)

            def w2_high(n, k, b, pair, chunk):
                w_arrived(act, b, pair)
                nc.scalar.copy(w2h[:, k, :], w2_raw[:, pair, chunk, :]).then_inc(S["w2_hi"], 1)

            def gelu(n, k):
                act.wait_ge(S["h_mm"], n + 1)
                nc.scalar.activation(hid[:, k, :], bank_h[k][:, :], ACT.Gelu).then_inc(S["h_act"], 1)

            def one(n, k, w1, w2, between=None):
                gelu(n, k)
                if w1:
                    w1_high(n + 2, k, *w1)
                if between:
                    between()
                if w2:
                    act.wait_ge(S["y_mm"], n + Y0)
                    w2_high(n + 1, 1 - k, *w2)

            def x_high(b):
                for i in range(TC):
                    act.wait_ge(S["xt_mm"], b * TC + i + 1)
                    nc.scalar.copy(xh[:, b % 2, i, :], bank_x[i % 2][:, :]).then_inc(S["xt_hi"], 1)

            def gated(b):
                act.wait_ge(S["y_mm"], b * HC + HC + Y0)
                for c in (0, 2):
                    nc.scalar.activation(y_sb[:, c, :], bank_y[c][:, :], ACT.Copy,
                                         scale=R["gate"][:, bass.ds(b * CH + c, 1)]).then_inc(S["y_ev"], 1)

            def first():
                w1_high(0, 0, 0, 0, 0)
                w1_high(1, 1, 0, 0, 1)
                w2_high(0, 0, 0, 0, 0)
                x_high(0)
                one(0, 0, (0, 1, 0), (0, 0, 1))
                one(1, 1, (0, 1, 1), (0, 1, 0))

            def body(b, more):
                for i in range(LOOP):
                    for k in range(2):
                        one(b * HC + 2 * i + 2 + k, k, (b, i + 2, k), (b, i + 1 + k, 1 - k))
                last = b * HC + HC
                if more:
                    x_high(b + 1)
                one(last - 2, 0, (b + 1, 0, 0) if more else None, (b, PAIRS - 1, 1))
                one(last - 1, 1, (b + 1, 0, 1) if more else None, (b + 1, 0, 0) if more else None)
                if more:
                    one(last, 0, (b + 1, 1, 0), (b + 1, 0, 1), between=lambda: gated(b))
                    one(last + 1, 1, (b + 1, 1, 1), (b + 1, 1, 0))
                else:
                    gated(b)

            over_batches(act, first, body)

        @block.vector
        def _(dve):
            def one(n, k, w1=None, w2=None):
                dve.wait_ge(S["h_act"], n + 1)
                dve.wait_ge(S["y_mm"], n + Y0 - 1)
                nc.vector.tensor_copy(hh[:, k, :], hid[:, k, :]).then_inc(S["h_hi"], 1)
                dve.wait_ge(S["h_hi"], n + 1)
                nc.vector.tensor_tensor(hl[:, k, :], hid[:, k, :], hh[:, k, :].bitcast(F32),
                                        ALU.subtract).then_inc(S["h_lo"], 1)

            def index_in(b):
                nc.vector.tensor_copy(tok_in[:, :], R["token"][:, bass.ds(b * CH, CH)]).then_inc(S["index_in"], 1)

            def x_low(b):
                for i in range(TC):
                    dve.wait_ge(S["xt_hi"], b * TC + i + 1)
                    nc.vector.tensor_tensor(xl[:, b % 2, i, :], bank_x[i % 2][:, :], xh[:, b % 2, i, :].bitcast(F32),
                                            ALU.subtract).then_inc(S["xt_lo"], 1)

            def gated(b):
                dve.wait_ge(S["y_mm"], b * HC + HC + Y0)
                for c in (1, 3):
                    nc.vector.tensor_scalar(y_sb[:, c, :], bank_y[c][:, :], R["gate"][:, bass.ds(b * CH + c, 1)],
                                            None, ALU.mult).then_inc(S["y_ev"], 1)

            def first():
                index_in(0)
                x_low(0)
                one(0, 0)
                one(1, 1)

            def body(b, more):
                if more:
                    index_in(b + 1)
                with dve.Fori(0, LOOP) as i:
                    for k in range(2):
                        one(b * HC + 2 * i + 2 + k, k)
                last = b * HC + HC
                nc.vector.tensor_copy(tok_out[:, :], R["token"][:, bass.ds(b * CH, CH)]).then_inc(S["index_out"], 1)
                if more:
                    x_low(b + 1)
                one(last - 2, 0)
                one(last - 1, 1)
                if more:
                    one(last, 0)
                gated(b)
                if more:
                    one(last + 1, 1)

            over_batches(dve, first, body)

        @block.tensor
        def _(pe):
            def hidden(n, k, b):
                pe.wait_ge(S["w1_lo"], n + 1)
                split_product(nc, bank_h[k][:, :], [((w1h[:, k, i, :], w1l[:, k, i, :]),
                                                     (xh[:, b % 2, i, :], xl[:, b % 2, i, :])) for i in range(TC)]
                              ).then_inc(S["h_mm"], 1)

            def spend(n, k, start=False, stop=False):
                pe.wait_ge(S["h_lo"], n + 1)
                pe.wait_ge(S["w2_lo"], n + 1)
                for c in range(CH):
                    cols = slice(c * P, (c + 1) * P)
                    last = split_product(nc, bank_y[c][:, :], [((hh[:, k, cols], hl[:, k, cols]),
                                                                (w2h[:, k, :], w2l[:, k, :]))], start=start, stop=stop)
                last.then_inc(S["y_mm"], 1)

            def x_transposes(b, i):
                pe.wait_ge(S["rows_in"], (b + 1) * CH * 16)
                for c in range(CH):
                    last = nc.tensor.transpose(bank_x[i % 2][:, c * P:(c + 1) * P], rows[:, c, i * P:(i + 1) * P],
                                               K.parts["ident"])
                last.then_inc(S["xt_mm"], 1)

            def x_free(b, i):
                pe.wait_ge(S["xt_lo"], b * TC + i - 1)

            def first():
                pe.sem_inc(S["y_mm"], Y0)
                for i in range(TC):
                    if i >= 2:
                        x_free(0, i)
                    x_transposes(0, i)
                pe.wait_ge(S["xt_lo"], TC)
                hidden(0, 0, 0)
                hidden(1, 1, 0)
                spend(0, 0, start=True)

            def body(b, more):
                n = b * HC
                with pe.Fori(0, LOOP) as i:
                    for k in range(2):
                        m = n + 2 * i + 2 + k
                        hidden(m, k, b)
                        spend(m - 1, 1 - k)
                last = n + HC
                if more:
                    x_transposes(b + 1, 0)
                    x_transposes(b + 1, 1)
                hidden(last - 2, 0, b)
                if more:
                    x_free(b + 1, 2)
                    x_transposes(b + 1, 2)
                    x_free(b + 1, 3)
                    x_transposes(b + 1, 3)
                spend(last - 3, 1)
                hidden(last - 1, 1, b)
                spend(last - 2, 0)
                if more:
                    pe.wait_ge(S["xt_lo"], (b + 1) * TC + TC)
                    hidden(last, 0, b + 1)
                spend(last - 1, 1, stop=True)
                if more:
                    hidden(last + 1, 1, b + 1)
                    pe.wait_ge(S["y_ev"], (b + 1) * CH)
                    spend(last, 0, start=True)

            over_batches(pe, first, body)


class Kept(dict):
    pass


def load_table(nc, ctx, K, name):
    K[name] = ctx.enter_context(nc.sbuf_tensor(f"table_{name}", [P, sum(TABLES[name].values())], F32))
    at = 0
    for part, width in TABLES[name].items():
        K.parts[part] = K[name][:, at:at + width]
        at += width


def block_program(nc, A, out):
    with ExitStack() as ctx:
        K = Kept()
        K.parts = {}
        load_table(nc, ctx, K, "always")
        with ExitStack() as early:
            def eb(name, shape, dt=F32):
                return early.enter_context(nc.sbuf_tensor(name, shape, dt))

            load_table(nc, early, K, "attend")
            K.update(bA=eb("bA", [P, 2]), bC=eb("bC", [P, NU]), bB=eb("bB", [P, 1]), bZ=eb("bZ", [P, T]),
                     wsub=eb("wsub", [P, NSUB, C]), fside=eb("fside", [NSUB, C]), subj=eb("subj", [NSUB, B], I32),
                     sel=eb("sel", [NSUB, B]), wblk=eb("wblk", [P, NPAIR, P]), qrope=eb("q_rope", [P, GB, 2, C]))
            W = dict(WAh=eb("WAh", [P, TC, 2 * L], F32R), WAl=eb("WAl", [P, TC, 2 * L], F32R),
                     WCh=eb("WCh", [P, 2, DR * NH], F32R), WCl=eb("WCl", [P, 2, DR * NH], F32R),
                     WBh=eb("WBh", [P, 2, 2, DR], F32R), WBl=eb("WBl", [P, 2, 2, DR], F32R),
                     Ah=eb("Ah", [P, NH * L], F32R), Al=eb("Al", [P, NH * L], F32R),
                     Mh=eb("Mh", [P, NH, T], F32R), Ml=eb("Ml", [P, NH, T], F32R))
            absorb_weights(nc, K, A, W)
            attention(nc, K, A, W, out)
        flat = nc.dram_tensor("flat_dram", (NTOK, T), F32, kind="Internal").ap()
        R = dict(token=ctx.enter_context(nc.sbuf_tensor("slot_token", [P, NE * NCH], I32)),
                 gate=ctx.enter_context(nc.sbuf_tensor("slot_gate", [P, NE * NCH], F32)))
        routing(nc, K, A, out, flat, R)
        experts(nc, K, A, out, flat, R)


_INS = {'x': 'x', 'subj': 'itok_B_0_7', 'fside': 'fside_8xS_0', 'adapt': 'itok_B_0_6', 'cond_weights': 'L0_cond_weights',
        'WA': 'L0_attn_WA', 'bA': 'L0_attn_bA', 'WB': 'L0_attn_WB', 'bB': 'L0_attn_bB', 'WC': 'L0_attn_WC',
        'bC': 'L0_attn_bC', 'WUQ': 'L0_attn_WUQ', 'WUK': 'L0_attn_WUK', 'WUV': 'L0_attn_WUV', 'WZ': 'L0_attn_WZ',
        'bZ': 'L0_attn_bZ', 'W': 'L0_cond2_W', 'A': 'L0_cond2_A', 'Bm': 'L0_cond2_Bm',
        'scalings': 'L0_cond2_scalings', 'Wg': 'L0_ffn_Wg', 'bg': 'L0_ffn_bg', 'W1': 'L0_ffn_W1', 'W2': 'L0_ffn_W2'}


def kernel(**inputs):
    import concourse.bacc as _bacc
    from concourse.bass_utils import run_bass_kernel_spmd as _run

    nc = _bacc.Bacc("TRN2", target_bir_lowering=False, num_devices=1)
    arrays = {f"in_{short}_dram": np.ascontiguousarray(inputs[name]) for short, name in _INS.items()}
    arrays.update({f"in_{name}_dram": const_table(name) for name in TABLES})
    args = {name[3:-5]: nc.dram_tensor(name, a.shape, mybir.dt.from_np(a.dtype), kind="ExternalInput").ap()
            for name, a in arrays.items()}
    out = nc.dram_tensor("out_0_dram", (B, C, T), F32, kind="ExternalOutput").ap()
    block_program(nc, args, out)
    r = _run(nc, [arrays], core_ids=[0])
    return r.results[0]["out_0_dram"]
```

```python
from contextlib import ExitStack

import numpy as np

import concourse.bass as bass
from concourse import mybir

F32 = mybir.dt.float32
F32R = mybir.dt.float32r
BF16 = mybir.dt.bfloat16
I32 = mybir.dt.int32
U32 = mybir.dt.uint32
ALU = mybir.AluOpType
ACT = mybir.ActivationFunctionType
AX = mybir.AxisListType.X

P = 128
B, C, T = 64, 64, 512
NSUB, NADAPT, RANK = 8, 8, 16
NH, DH, DR, L = 16, 128, 64, 128
SCALE = float(np.float32((DH + DR) ** -0.5))
MASKED = -1.0e30
TC = T // P
GB = 8
NG = B // GB
GT = GB * C
NPAIR = GT // P
NU = NH // 2
NTOK = B * C
NT = NTOK // P
NE, HID = 4, 2048
CAP = NTOK // NE
NCH = CAP // P
HC = HID // P


BITS = 3
TRIALS = 30 // BITS
CANDS = 2 ** BITS - 1
TABLES = {
    "always": {"ident": P, "ones": P, "part": 1},
    "attend": {"mask": C, "cosq": NU * C, "sinq": NU * C, "cosk": C, "sink": C},
    "route": {"before": P, "iota": P, "adapter": 1, "tile": NT, "fold": NE, "trial": CANDS * TRIALS},
}


def const_columns():
    def rope(feature, size):
        theta = np.exp(-(feature // 2).astype(np.float32) / np.float32(size)
                       * np.log(np.float32(10000.0))).astype(np.float32)
        angle = (np.arange(1, C + 1, dtype=np.float32)[None] * theta[:, None]).astype(np.float32)
        sign = np.where(feature % 2 == 0, -1.0, 1.0).astype(np.float32)[:, None]
        return np.cos(angle), np.sin(angle) * sign

    p = np.arange(P)
    pairs = [rope(u * P + p, DR * NH) for u in range(NU)]
    cosk, sink = rope(p % DR, DR)
    trial = np.array([c << (BITS * (TRIALS - 1 - i)) for i in range(TRIALS) for c in range(1, CANDS + 1)], np.int32)
    return {
        "ident": np.eye(P), "ones": np.ones((P, P)), "part": p[:, None],
        "mask": np.where(np.arange(C)[None] <= (p % C)[:, None], 0.0, MASKED),
        "cosq": np.concatenate([c for c, _ in pairs], 1), "sinq": np.concatenate([s for _, s in pairs], 1),
        "cosk": cosk, "sink": sink,
        "before": p[:, None] < p[None], "iota": np.broadcast_to(p[None], (P, P)), "adapter": p[:, None] // RANK,
        "tile": np.broadcast_to(np.arange(NT)[None], (P, NT)),
        "fold": p[:, None] % NE == np.arange(NE)[None],
        "trial": np.broadcast_to(trial.view(np.float32), (P, CANDS * TRIALS)),
    }


def const_table(name):
    columns = const_columns()
    return np.concatenate([columns[n] for n in TABLES[name]], 1).astype(np.float32)


def split_product(nc, out, pairs, start=True, stop=True):
    last = None
    for n, ((ah, al), (bh, bl)) in enumerate(pairs):
        nc.tensor.matmul(out, ah, bh, start=start and n == 0, stop=False)
        nc.tensor.matmul(out, ah, bl, start=False, stop=False)
        last = nc.tensor.matmul(out, al, bh, start=False, stop=stop and n == len(pairs) - 1)
    return last


def spread_weights(nc, K, dve, g, batches):
    for j in batches:
        h, n = j % 2, j // 2
        rows = slice(h * C, (h + 1) * C)
        s = dve.value_load(K["subj"][0:1, bass.ds(g * GB + j, 1)], min_val=0, max_val=NSUB - 1)
        nc.vector.tensor_copy(K["wblk"][rows, n, rows], K["wsub"][rows, bass.ds(s, 1), :].squeeze(1)
                              ).then_inc(K.sems["wblk_ready"], 1)


def absorb_weights(nc, K, A, W):
    HG = NH // 4
    with ExitStack() as ctx:
        def sb(name, shape, dt=F32):
            return ctx.enter_context(nc.sbuf_tensor(name, shape, dt))

        def bank(name):
            return ctx.enter_context(nc.psum_tensor(name, [P, 512], F32))

        def sem(name):
            return ctx.enter_context(nc.semaphore(name))

        up = {n: sb(f"up_{n}", [P, NH * DH]) for n in "qkv"}
        wz_own = sb("wz_raw", [P, 2, NPAIR, T])
        wz = (K["stage"], K["x_res"], wz_own[:, 0, :, :], wz_own[:, 1, :, :])
        wa = sb("wa_raw", [P, TC, 2 * L])
        wc = sb("wc_raw", [P, 2, DR * NH])
        wb = sb("wb_raw", [P, 2, DR])
        upT = {n: sb(f"upT_{n}", [P, 2, 512]) for n in "qkv"}
        bank_t = {n: bank(f"w_t{n}") for n in "qkv"}
        bank_a = bank("w_a")
        bank_m = [bank(f"w_m{i}") for i in range(4)]

        consts_in = sem("consts_in")
        up_in = {n: [sem(f"up{n}_in{i}") for i in range(HG)] for n in "qkv"}
        wz_in = [sem(f"wz_in{i}") for i in range(HG)]
        small_in, wa_in, wc_in = sem("small_in"), sem("wa_in"), sem("wc_in")
        t_mm = {n: sem(f"w_t{n}_mm") for n in "qkv"}
        t_ev = {n: sem(f"w_t{n}_ev") for n in "qkv"}
        a_mm, a_hi, a_lo = sem("w_a_mm"), sem("w_a_hi"), sem("w_a_lo")
        m_mm, m_hi, m_lo = sem("w_m_mm"), sem("w_m_hi"), sem("w_m_lo")
        s_hi, s_lo = sem("w_s_hi"), sem("w_s_lo")
        zeroed = sem("w_zeroed")

        block = ctx.enter_context(nc.Block())
        wz_d = A["WZ"].rearrange("(h d) n -> d h n", d=DH)

        @block.sync
        def _(sp):
            sp.dma_start(K["always"][:, :], A["always"]).then_inc(consts_in, 16)
            def up_chunk(i):
                cols = slice(i * 4 * DH, (i + 1) * 4 * DH)
                for n, name in (("q", "WUQ"), ("k", "WUK"), ("v", "WUV")):
                    sp.dma_start(up[n][:, cols], A[name][:, cols]).then_inc(up_in[n][i], 16)

            up_chunk(0)
            for i in range(HG):
                if i + 1 < HG:
                    up_chunk(i + 1)
                sp.dma_start(wz[i][:, :, :], wz_d[:, 4 * i:4 * i + 4, :]).then_inc(wz_in[i], 16)
                if i == 0:
                    sp.dma_start(wa[:, :, :], A["WA"].rearrange("(c p) n -> p c n", p=P)).then_inc(wa_in, 16)
                if i == 1:
                    sp.dma_start(wc[:, :, :], A["WC"].rearrange("(c p) n -> p c n", p=P)).then_inc(wc_in, 16)
            x_first = A["x"].rearrange("(g n j) c t -> g (j c) n t", n=NPAIR, j=2)[0]
            sp.wait_ge(m_mm, 4)
            sp.dma_start(K["stage"][:, :, :], x_first).then_inc(K.sems["x_in"], 16)
            sp.wait_ge(m_mm, 8)
            sp.dma_start(K["x_res"][:, :, :], x_first).then_inc(K.sems["xres_in"], 16)

        SMALL = 16 * 11

        @block.scalar
        def _(act):
            with nc.allow_non_contiguous_dma(reason="a few small vectors, once"):
                act.dma_start(K["subj"][:, :], A["subj"].partition_broadcast(NSUB)).then_inc(small_in, 16)
                for h in range(2):
                    act.dma_start(K["bB"][h * DR:(h + 1) * DR, :],
                                  A["bB"].rearrange("(p o) -> p o", o=1)).then_inc(small_in, 16)
                    act.dma_start(K["wsub"][h * C:(h + 1) * C, :, :],
                                  A["cond_weights"].rearrange("n c d -> c n d")).then_inc(small_in, 16)
                act.dma_start(K["fside"][:, :], A["fside"]).then_inc(small_in, 16)
                act.dma_start(wb[:, :, :], A["WB"].rearrange("(c p) n -> p c n", p=P)).then_inc(small_in, 16)
                act.dma_start(K["bA"][:, :], A["bA"].rearrange("(c p) -> p c", p=P)).then_inc(small_in, 16)
                act.dma_start(K["bC"][:, :], A["bC"].rearrange("(c p) -> p c", p=P)).then_inc(small_in, 16)
                act.dma_start(K["bZ"][:, :], A["bZ"].partition_broadcast(P)).then_inc(small_in, 16)
                act.dma_start(K["attend"][:, :], A["attend"]).then_inc(small_in, 16)
            def transposed(i):
                for n in "qv":
                    act.wait_ge(t_mm[n], i + 1)
                    if i >= 2:
                        act.wait_ge(a_mm if n == "q" else m_mm, i - 1 if n == "q" else 4 * (i - 1))
                    nc.scalar.copy(upT[n][:, i % 2, :], bank_t[n][:, :]).then_inc(t_ev[n], 1)

            transposed(0)
            for i in range(HG):
                if i + 1 < HG:
                    transposed(i + 1)
                act.wait_ge(a_mm, i + 1)
                nc.scalar.copy(W["Ah"][:, 512 * i:512 * i + 512], bank_a[:, :]).then_inc(a_hi, 1)
                for j in range(4):
                    act.wait_ge(m_mm, 4 * i + j + 1)
                    nc.scalar.copy(W["Mh"][:, 4 * i + j, :], bank_m[j][:, :]).then_inc(m_hi, 1)
                if i == 1:
                    act.wait_ge(wa_in, 16)
                    nc.scalar.copy(W["WAh"][:, :, :], wa[:, :, :]).then_inc(s_hi, 1)
                    act.wait_ge(wc_in, 16)
                    nc.scalar.copy(W["WCh"][:, :, :], wc[:, :, :]).then_inc(s_hi, 1)
            act.wait_ge(small_in, SMALL)
            nc.scalar.copy(W["WBh"][:, :, :, :],
                           wb[:, :, :].unsqueeze(2).to_broadcast([P, 2, 2, DR])).then_inc(s_hi, 1)

        @block.gpsimd
        def _(pool):
            nc.gpsimd.memset(K["wblk"][:, :, :], 0.0).then_inc(zeroed, 1)
            nc.gpsimd.memset(K["qrope"][:, :, :, :], 0.0).then_inc(zeroed, 1)
            pool.wait_ge(s_hi, 1)
            nc.gpsimd.tensor_tensor(W["WAl"][:, :, :], wa[:, :, :], W["WAh"][:, :, :].bitcast(F32),
                                    ALU.subtract).then_inc(s_lo, 1)
            pool.wait_ge(s_hi, 2)
            nc.gpsimd.tensor_tensor(W["WCl"][:, :, :], wc[:, :, :], W["WCh"][:, :, :].bitcast(F32),
                                    ALU.subtract).then_inc(s_lo, 1)
            pool.wait_ge(s_hi, 3)
            nc.gpsimd.tensor_tensor(W["WBl"][:, :, :, :],
                                    wb[:, :, :].unsqueeze(2).to_broadcast([P, 2, 2, DR]),
                                    W["WBh"][:, :, :, :].bitcast(F32), ALU.subtract).then_inc(s_lo, 1)

        @block.vector
        def _(dve):
            def transposed(i):
                dve.wait_ge(t_mm["k"], i + 1)
                if i >= 2:
                    dve.wait_ge(a_mm, i - 1)
                nc.vector.tensor_copy(upT["k"][:, i % 2, :], bank_t["k"][:, :]).then_inc(t_ev["k"], 1)

            transposed(0)
            for i in range(HG):
                if i + 1 < HG:
                    transposed(i + 1)
                dve.wait_ge(a_hi, i + 1)
                nc.vector.tensor_tensor(W["Al"][:, 512 * i:512 * i + 512], bank_a[:, :],
                                        W["Ah"][:, 512 * i:512 * i + 512].bitcast(F32),
                                        ALU.subtract).then_inc(a_lo, 1)
                for j in range(4):
                    h = 4 * i + j
                    dve.wait_ge(m_hi, h + 1)
                    nc.vector.tensor_tensor(W["Ml"][:, h, :], bank_m[j][:, :], W["Mh"][:, h, :].bitcast(F32),
                                            ALU.subtract).then_inc(m_lo, 1)
                if i == 1:
                    dve.wait_ge(small_in, SMALL)
                    nc.vector.tensor_scalar(K["sel"][:, :], K["subj"][:, :], K.parts["part"][0:NSUB, :], None,
                                            ALU.is_equal).then_inc(zeroed, 1)
                    dve.wait_ge(zeroed, 3)
                if i in (1, 2):
                    spread_weights(nc, K, dve, 0, range((i - 1) * GB // 2, i * GB // 2))

        @block.tensor
        def _(pe):
            def transposes(i):
                for n in "qkv":
                    pe.wait_ge(up_in[n][i], 16)
                    if i >= 1:
                        pe.wait_ge(t_ev[n], i)
                    for j in range(4):
                        h = 4 * i + j
                        last = nc.tensor.transpose(bank_t[n][:, j * P:(j + 1) * P], up[n][:, h * P:(h + 1) * P],
                                                   K.parts["ident"])
                    last.then_inc(t_mm[n], 1)

            pe.wait_ge(consts_in, 16)
            transposes(0)
            for i in range(HG):
                s = i % 2
                if i + 1 < HG:
                    transposes(i + 1)
                pe.wait_ge(t_ev["q"], i + 1)
                pe.wait_ge(t_ev["k"], i + 1)
                if i >= 1:
                    pe.wait_ge(a_lo, i)
                for j in range(4):
                    cols = slice(j * P, (j + 1) * P)
                    last = nc.tensor.matmul(bank_a[:, cols], upT["q"][:, s, cols], upT["k"][:, s, cols],
                                            start=True, stop=True)
                last.then_inc(a_mm, 1)
                pe.wait_ge(t_ev["v"], i + 1)
                pe.wait_ge(wz_in[i], 16)
                for j in range(4):
                    if i >= 1:
                        pe.wait_ge(m_lo, 4 * (i - 1) + j + 1)
                    nc.tensor.matmul(bank_m[j][:, :], upT["v"][:, s, j * P:(j + 1) * P], wz[i][:, j, :],
                                     start=True, stop=True).then_inc(m_mm, 1)


def attention(nc, K, A, W, out):
    with ExitStack() as ctx:
        def sb(name, shape, dt=F32):
            return ctx.enter_context(nc.sbuf_tensor(name, shape, dt))

        def bank(name):
            return ctx.enter_context(nc.psum_tensor(name, [P, 512], F32))

        def sem(name):
            return ctx.enter_context(nc.semaphore(name))

        x_cond = K["stage"]
        x_res = K["x_res"]
        cond_h, cond_l = sb("cond_h", [P, TC, GT], F32R), sb("cond_l", [P, TC, GT], F32R)
        lat32 = sb("lat32", [P, 2, GT])
        lat_h, lat_l = sb("lat_h", [P, 2, GT], F32R), sb("lat_l", [P, 2, GT], F32R)
        kv_tok = sb("kv_tok", [P, NPAIR, L])
        k_rope = sb("k_rope", [P, GT])
        raw, swapped = sb("rope_raw", [P, GT]), sb("rope_swapped", [P, GT])
        by_cos, by_sin = sb("rope_cos", [P, GT]), sb("rope_sin", [P, GT])
        cond32 = (raw, swapped)
        bias_bc = by_cos
        bias_sel = by_sin[0:NSUB, :].rearrange("n (b d) -> n b d", b=GB)
        q_nope = sb("q_nope", [P, GB, 2, C])
        score = sb("score", [P, GB, C])
        prob = sb("prob", [P, 2, GB, C])
        rmax, rsum, rinv = sb("rmax", [P, GB]), sb("rsum", [P, GB]), sb("rinv", [P, GB])
        wait_here = sb("wait_here", [1, 1])
        probT = sb("probT", [P, NPAIR, P])
        mix_h = sb("mix_h", [P, 2, 2, NPAIR, 2, C], F32R)
        mix_l = sb("mix_l", [P, 2, 2, NPAIR, 2, C], F32R)
        q_rope = K["qrope"]
        bank_a, bank_b, bank_d, bank_s = bank("bank_a"), bank("bank_b"), bank("bank_d"), bank("bank_s")
        bank_o = [bank(f"bank_o{t}") for t in range(NPAIR)]

        names = """xres_biased x2_out bias_sel_ready bias_mm bias_ev cond_mm cond_ev cond_hi
            cond_lo_even cond_lo_odd lat_mm lat_ev lat_hi lat_lo kb_mm kvt_mm kvt_ev raw_ev swap_ev cos_ev sin_ev rope_done
            qc_mm qn0_mm qn1_mm qn0_ev qn1_ev score_mm score_ev max_ev sub_ev exp_ev sum_ev inv_ev prob_ev pt_mm pt_ev
            mixe_mm mixo_mm mixe_hi mixo_hi mixe_lo mixo_lo wz_mm x2_ev""".split()
        S = {n: sem("at_" + n) for n in names}
        S.update((n, K.sems[n]) for n in ("x_in", "xres_in", "wblk_ready"))

        block = ctx.enter_context(nc.Block())
        x_d = A["x"].rearrange("(g n j) c t -> g (j c) n t", n=NPAIR, j=2)
        out_d = out.rearrange("(g n j) c t -> g (j c) n t", n=NPAIR, j=2)
        NR = NU + 1

        def over_groups(eng, first, body):
            first()
            with eng.Fori(0, NG - 1) as g:
                body(g, True)
            body(NG - 1, False)

        @block.sync
        def _(sp):
            def first():
                pass

            def body(g, more):
                sp.wait_ge(S["cond_mm"], g * TC + TC)
                if not more:
                    sp.dma_start(x_cond[:, :, :], A["W"].rearrange("(c p) n -> p c n", p=P)
                                 ).then_inc(K.sems["w_in"], 16)
                if more:
                    sp.dma_start(x_cond[:, :, :], x_d[g + 1]).then_inc(S["x_in"], 16)
                for t in range(NPAIR):
                    sp.wait_ge(S["x2_ev"], g * NPAIR + t + 1)
                    sp.dma_start(out_d[g, :, t, :], x_res[:, t, :]).then_inc(S["x2_out"], 16)
                sp.wait_ge(S["x2_out"], (g + 1) * NPAIR * 16)
                if more:
                    sp.dma_start(x_res[:, :, :], x_d[g + 1]).then_inc(S["xres_in"], 16)

            over_groups(sp, first, body)

        @block.gpsimd
        def _(pool):
            def bias_rows(g):
                nc.gpsimd.tensor_tensor(bias_sel[:, :, :],
                                        K["sel"][:, bass.ds(g * GB, GB)].unsqueeze(2).to_broadcast([NSUB, GB, C]),
                                        K["fside"][:, :].unsqueeze(1).to_broadcast([NSUB, GB, C]),
                                        ALU.mult).then_inc(S["bias_sel_ready"], 1)

            def cond_lo(g):
                for c in range(0, TC, 2):
                    pool.wait_ge(S["cond_hi"], g * TC + c + 1)
                    nc.gpsimd.tensor_tensor(cond_l[:, c, :], cond32[0][:, :], cond_h[:, c, :].bitcast(F32),
                                            ALU.subtract).then_inc(S["cond_lo_even"], 1)

            def rope_cos(r, cos, first=False):
                pool.wait_ge(S["raw_ev"], r + 1)
                if not first:
                    pool.wait_ge(S["rope_done"], r)
                v = raw[:, :].rearrange("p (b t) -> p b t", b=GB)
                nc.gpsimd.tensor_tensor(by_cos[:, :].rearrange("p (b t) -> p b t", b=GB), v,
                                        cos.unsqueeze(1).to_broadcast([P, GB, C]), ALU.mult).then_inc(S["cos_ev"], 1)

            def q_rope_cos(g, u):
                rope_cos(g * NR + 1 + u, K.parts["cosq"][:, u * C:(u + 1) * C])

            def first():
                bias_rows(0)
                cond_lo(0)
                rope_cos(0, K.parts["cosk"], first=True)

            def body(g, more):
                q_rope_cos(g, 0)
                for u in range(NU):
                    if u + 1 < NU:
                        q_rope_cos(g, u + 1)
                    elif more:
                        pool.wait_ge(S["rope_done"], g * NR + NR)
                        bias_rows(g + 1)
                    pool.wait_ge(S["inv_ev"], g * NU + u + 1)
                    nc.gpsimd.tensor_tensor(prob[:, u % 2, :, :], prob[:, u % 2, :, :],
                                            rinv[:, :].unsqueeze(2).to_broadcast([P, GB, C]),
                                            ALU.mult).then_inc(S["prob_ev"], 1)
                    if NU - NPAIR <= u:
                        if u == NU - NPAIR:
                            pool.wait_ge(S["xres_in"], g * 16 + 16)
                        t = u - (NU - NPAIR)
                        nc.gpsimd.tensor_tensor(x_res[:, t, :], x_res[:, t, :], K["bZ"][:, :],
                                                ALU.add).then_inc(S["xres_biased"], 1)
                if more:
                    cond_lo(g + 1)
                    rope_cos((g + 1) * NR, K.parts["cosk"])

            over_groups(pool, first, body)

        @block.scalar
        def _(act):
            def bias_evac(g):
                act.wait_ge(S["bias_mm"], g + 1)
                nc.scalar.copy(bias_bc[:, :], bank_s[:, :]).then_inc(S["bias_ev"], 1)

            def cond_hi(g, c):
                act.wait_ge(S["cond_ev"], g * TC + c + 1)
                nc.scalar.copy(cond_h[:, c, :], cond32[c % 2][:, :]).then_inc(S["cond_hi"], 1)

            def latent(g, i):
                act.wait_ge(S["lat_mm"], g * 2 + i + 1)
                nc.scalar.activation(lat32[:, i, :], (bank_a, bank_s)[i][:, :], ACT.Identity,
                                     bias=K["bA"][:, i:i + 1]).then_inc(S["lat_ev"], 1)
                act.wait_ge(S["lat_ev"], g * 2 + i + 1)
                nc.scalar.copy(lat_h[:, i, :], lat32[:, i, :]).then_inc(S["lat_hi"], 1)

            def kv_tokens(g):
                act.wait_ge(S["kvt_mm"], g + 1)
                nc.scalar.copy(kv_tok[:, :, :], bank_b[:, :].rearrange("p (n l) -> p n l", n=NPAIR)
                               ).then_inc(S["kvt_ev"], 1)

            def rope_raw(r, ready, count, source, bias, first=False):
                act.wait_ge(ready, count)
                if not first:
                    act.wait_ge(S["swap_ev"], r)
                    act.wait_ge(S["cos_ev"], r)
                nc.scalar.activation(raw[:, :], source[:, :], ACT.Identity, bias=bias).then_inc(S["raw_ev"], 1)

            def q_rope_raw(g, u):
                rope_raw(g * NR + 1 + u, S["qc_mm"], g * NU + u + 1, bank_a, K["bC"][:, u:u + 1])

            def q_nope_evac(g, u, h):
                act.wait_ge(S[f"qn{h}_mm"], g * NU + u + 1)
                nc.scalar.copy(q_nope[:, :, h, :], (bank_b, bank_d)[h][:, :].rearrange("p (b t) -> p b t", b=GB)
                               ).then_inc(S[f"qn{h}_ev"], 1)

            def exps(g, u):
                act.wait_ge(S["sub_ev"], g * NU + u + 1)
                nc.scalar.activation(prob[:, u % 2, :, :], score[:, :, :], ACT.Exp).then_inc(S["exp_ev"], 1)

            def prob_transposed(g, u):
                act.wait_ge(S["pt_mm"], g * NU + u + 1)
                nc.scalar.copy(probT[:, :, :], bank_a[:, :].rearrange("p (n q) -> p n q", n=NPAIR)
                               ).then_inc(S["pt_ev"], 1)

            def mix_hi(g, u):
                for j, (k, bk) in enumerate((("mixe", bank_b), ("mixo", bank_d))):
                    act.wait_ge(S[k + "_mm"], g * NU + u + 1)
                    nc.scalar.copy(mix_h[:, u % 2, :, :, j, :].rearrange("p h n t -> p n h t"),
                                   bk[:, :].rearrange("p (n h t) -> p n h t", n=NPAIR, h=2)
                                   ).then_inc(S[k + "_hi"], 1)

            def first():
                bias_evac(0)
                for c in range(TC):
                    cond_hi(0, c)
                latent(0, 0)
                latent(0, 1)
                kv_tokens(0)
                rope_raw(0, S["kb_mm"], 1, bank_d, K["bB"][:, 0:1], first=True)

            def body(g, more):
                q_rope_raw(g, 0)
                for h in range(2):
                    q_nope_evac(g, 0, h)
                q_rope_raw(g, 1)
                for h in range(2):
                    q_nope_evac(g, 1, h)
                exps(g, 0)
                for u in range(1, NU):
                    if u + 1 < NU:
                        q_rope_raw(g, u + 1)
                    exps(g, u)
                    if u + 1 < NU:
                        q_nope_evac(g, u + 1, 0)
                    prob_transposed(g, u - 1)
                    if u + 1 < NU:
                        q_nope_evac(g, u + 1, 1)
                    mix_hi(g, u - 1)
                if more:
                    bias_evac(g + 1)
                prob_transposed(g, NU - 1)
                if more:
                    cond_hi(g + 1, 0)
                mix_hi(g, NU - 1)
                if more:
                    for c in range(1, TC):
                        cond_hi(g + 1, c)
                    latent(g + 1, 0)
                    latent(g + 1, 1)
                    kv_tokens(g + 1)
                    rope_raw((g + 1) * NR, S["kb_mm"], g + 2, bank_d, K["bB"][:, 0:1])

            over_groups(act, first, body)

        @block.vector
        def _(dve):
            COND_BANK = (bank_d, bank_s, bank_a, bank_s)

            def cond_evac(g, c, first=False):
                dve.wait_ge(S["bias_ev"], g + 1)
                dve.wait_ge(S["cond_mm"], g * TC + c + 1)
                if not first or c >= 2:
                    dve.wait_ge(S[("cond_lo_even", "cond_lo_odd")[c % 2]], g * (TC // 2) + c // 2)
                nc.vector.tensor_tensor(cond32[c % 2][:, :], COND_BANK[c][:, :], bias_bc[:, :],
                                        ALU.add).then_inc(S["cond_ev"], 1)

            def cond_lo(g, c):
                dve.wait_ge(S["cond_hi"], g * TC + c + 1)
                nc.vector.tensor_tensor(cond_l[:, c, :], cond32[1][:, :], cond_h[:, c, :].bitcast(F32),
                                        ALU.subtract).then_inc(S["cond_lo_odd"], 1)

            def latent_lo(g, i):
                dve.wait_ge(S["lat_hi"], g * 2 + i + 1)
                nc.vector.tensor_tensor(lat_l[:, i, :], lat32[:, i, :], lat_h[:, i, :].bitcast(F32),
                                        ALU.subtract).then_inc(S["lat_lo"], 1)

            def rope_sin(r, sin, first=False):
                dve.wait_ge(S["raw_ev"], r + 1)
                if not first:
                    dve.wait_ge(S["sin_ev"], r)
                nc.vector.memset(wait_here[:, :], 0.0)
                nc.vector.stream_shuffle(swapped[:, :], raw[:, :], [i ^ 1 for i in range(32)]
                                         ).then_inc(S["swap_ev"], 1)
                dve.wait_ge(S["swap_ev"], r + 1)
                if not first:
                    dve.wait_ge(S["rope_done"], r)
                nc.vector.tensor_tensor(by_sin[:, :].rearrange("p (b t) -> p b t", b=GB),
                                        swapped[:, :].rearrange("p (b t) -> p b t", b=GB),
                                        sin.unsqueeze(1).to_broadcast([P, GB, C]), ALU.mult).then_inc(S["sin_ev"], 1)

            def q_rope_sin(g, u):
                rope_sin(g * NR + 1 + u, K.parts["sinq"][:, u * C:(u + 1) * C])

            def rope_add_keys(r):
                dve.wait_ge(S["cos_ev"], r + 1)
                dve.wait_ge(S["sin_ev"], r + 1)
                nc.vector.tensor_tensor(k_rope[:, :], by_cos[:, :], by_sin[:, :], ALU.add).then_inc(S["rope_done"], 1)

            def rope_add_queries(r):
                dve.wait_ge(S["cos_ev"], r + 1)
                dve.wait_ge(S["sin_ev"], r + 1)
                for h in range(2):
                    rows = slice(h * DR, (h + 1) * DR)
                    last = nc.vector.tensor_tensor(q_rope[rows, :, h, :],
                                                   by_cos[rows, :].rearrange("p (b t) -> p b t", b=GB),
                                                   by_sin[rows, :].rearrange("p (b t) -> p b t", b=GB), ALU.add)
                last.then_inc(S["rope_done"], 1)

            def mix_lo(g, u):
                for j, (k, bk) in enumerate((("mixe", bank_b), ("mixo", bank_d))):
                    view = mix_h[:, u % 2, :, :, j, :].rearrange("p h n t -> p n h t")
                    dve.wait_ge(S[k + "_hi"], g * NU + u + 1)
                    nc.vector.tensor_tensor(mix_l[:, u % 2, :, :, j, :].rearrange("p h n t -> p n h t"),
                                            bk[:, :].rearrange("p (n h t) -> p n h t", n=NPAIR, h=2),
                                            view.bitcast(F32), ALU.subtract).then_inc(S[k + "_lo"], 1)

            def per_batch(row):
                return row[:, :].unsqueeze(2).to_broadcast([P, GB, C])

            def score_in(g, u):
                n = g * NU + u + 1
                dve.wait_ge(S["score_mm"], n)
                if u:
                    dve.wait_ge(S["exp_ev"], n - 1)
                nc.vector.scalar_tensor_tensor(out=score[:, :, :],
                                               in0=bank_s[:, :].rearrange("p (b t) -> p b t", b=GB), scalar=SCALE,
                                               in1=K.parts["mask"].unsqueeze(1).to_broadcast([P, GB, C]),
                                               op0=ALU.mult, op1=ALU.add).then_inc(S["score_ev"], 1)

            def less_max(g, u):
                n = g * NU + u + 1
                dve.wait_ge(S["score_ev"], n)
                nc.vector.tensor_reduce(rmax[:, :], score[:, :, :], AX, ALU.max).then_inc(S["max_ev"], 1)
                dve.wait_ge(S["max_ev"], n)
                nc.vector.tensor_tensor(score[:, :, :], score[:, :, :], per_batch(rmax),
                                        ALU.subtract).then_inc(S["sub_ev"], 1)

            def softmax_sum(g, u):
                n = g * NU + u + 1
                dve.wait_ge(S["exp_ev"], n)
                nc.vector.tensor_reduce(rsum[:, :], prob[:, u % 2, :, :], AX, ALU.add).then_inc(S["sum_ev"], 1)
                dve.wait_ge(S["sum_ev"], n)
                if u:
                    dve.wait_ge(S["prob_ev"], n - 1)
                nc.vector.reciprocal(rinv[:, :], rsum[:, :]).then_inc(S["inv_ev"], 1)

            def x2_tile(g, t):
                dve.wait_ge(S["xres_biased"], g * NPAIR + t + 1)
                dve.wait_ge(S["wz_mm"], g * NPAIR + t + 1)
                nc.vector.tensor_tensor(x_res[:, t, :], bank_o[t][:, :], x_res[:, t, :],
                                        ALU.add).then_inc(S["x2_ev"], 1)

            def head(g, prev=None):
                rope_sin(g * NR, K.parts["sink"], first=prev is None)
                rope_add_keys(g * NR)
                q_rope_sin(g, 0)
                rope_add_queries(g * NR + 1)
                if prev is not None:
                    for t in range(NPAIR - 1):
                        x2_tile(prev, t)
                q_rope_sin(g, 1)
                score_in(g, 0)
                rope_add_queries(g * NR + 2)
                less_max(g, 0)
                softmax_sum(g, 0)
                if prev is not None:
                    x2_tile(prev, NPAIR - 1)

            def first():
                for c in range(TC):
                    cond_evac(0, c, first=True)
                    if c % 2:
                        cond_lo(0, c)
                latent_lo(0, 0)
                latent_lo(0, 1)
                head(0)

            def body(g, more):
                for u in range(1, NU):
                    score_in(g, u)
                    less_max(g, u)
                    if u + 1 < NU:
                        q_rope_sin(g, u + 1)
                    softmax_sum(g, u)
                    if u + 1 < NU:
                        rope_add_queries(g * NR + u + 2)
                    mix_lo(g, u - 1)
                    if more:
                        if u == 1:
                            dve.wait_ge(S["cond_mm"], g * TC + TC)
                            spread_weights(nc, K, dve, g + 1, (0, ))
                        spread_weights(nc, K, dve, g + 1, (u, ))
                if more:
                    cond_evac(g + 1, 0)
                mix_lo(g, NU - 1)
                if more:
                    cond_evac(g + 1, 1)
                    cond_evac(g + 1, 2)
                    cond_lo(g + 1, 1)
                    cond_evac(g + 1, 3)
                    cond_lo(g + 1, 3)
                    latent_lo(g + 1, 0)
                    latent_lo(g + 1, 1)
                    head(g + 1, prev=g)
                else:
                    for t in range(NPAIR):
                        x2_tile(g, t)

            over_groups(dve, first, body)

        @block.tensor
        def _(pe):
            def wz(g, u, t):
                if t == 0:
                    pe.wait_ge(S["mixe_lo"], g * NU + u + 1)
                    pe.wait_ge(S["mixo_lo"], g * NU + u + 1)
                pairs = [((mix_h[:, u % 2, h, t, :, :].rearrange("p j t -> p (j t)"),
                           mix_l[:, u % 2, h, t, :, :].rearrange("p j t -> p (j t)")),
                          (W["Mh"][:, 2 * u + h, :], W["Ml"][:, 2 * u + h, :])) for h in range(2)]
                last = split_product(nc, bank_o[t][:, :], pairs, start=u == 0, stop=u == NU - 1)
                if u == NU - 1:
                    last.then_inc(S["wz_mm"], 1)

            def bias_rows(g):
                pe.wait_ge(S["bias_sel_ready"], g + 1)
                nc.tensor.matmul(bank_s[:, :], K.parts["ones"][0:NSUB, :], bias_sel[:, :, :].rearrange("n b d -> n (b d)"),
                                 start=True, stop=True).then_inc(S["bias_mm"], 1)

            def cond(g, c, bk):
                if c == 0:
                    pe.wait_ge(S["x_in"], g * 16 + 16)
                    pe.wait_ge(S["wblk_ready"], g * GB + GB)
                for n in range(NPAIR):
                    last = nc.tensor.matmul(bk[:, n * P:(n + 1) * P], x_cond[:, n, c * P:(c + 1) * P],
                                            K["wblk"][:, n, :], start=True, stop=True)
                last.then_inc(S["cond_mm"], 1)

            def latent(g, i, bk):
                if i == 0:
                    pe.wait_ge(S["cond_ev"], g * TC + 3)
                for c in range(TC):
                    pe.wait_ge(S[("cond_lo_even", "cond_lo_odd")[c % 2]], g * (TC // 2) + c // 2 + 1)
                    last = split_product(nc, bk[:, :], [((W["WAh"][:, c, i * L:(i + 1) * L],
                                                          W["WAl"][:, c, i * L:(i + 1) * L]),
                                                         (cond_h[:, c, :], cond_l[:, c, :]))],
                                         start=c == 0, stop=c == TC - 1)
                last.then_inc(S["lat_mm"], 1)

            def kv_tokens(g):
                pe.wait_ge(S["lat_ev"], g * 2 + 1)
                for n in range(NPAIR):
                    last = nc.tensor.transpose(bank_b[:, n * P:(n + 1) * P], lat32[:, 0, n * P:(n + 1) * P], K.parts["ident"])
                last.then_inc(S["kvt_mm"], 1)

            def rope_keys(g):
                pe.wait_ge(S["lat_lo"], g * 2 + 2)
                split_product(nc, bank_d[:, :], [((W["WBh"][:, i, :, :].rearrange("p j d -> p (j d)"),
                                                   W["WBl"][:, i, :, :].rearrange("p j d -> p (j d)")),
                                                  (lat_h[:, i, :], lat_l[:, i, :])) for i in range(2)]
                              ).then_inc(S["kb_mm"], 1)

            def q_rope_mm(g, u):
                cols = slice(u * P, (u + 1) * P)
                split_product(nc, bank_a[:, :], [((W["WCh"][:, i, cols], W["WCl"][:, i, cols]),
                                                  (lat_h[:, i, :], lat_l[:, i, :])) for i in range(2)]
                              ).then_inc(S["qc_mm"], 1)

            def q_nope_mm(g, u, h):
                cols = slice((2 * u + h) * P, (2 * u + h + 1) * P)
                split_product(nc, (bank_b, bank_d)[h][:, :], [((W["Ah"][:, cols], W["Al"][:, cols]),
                                                               (lat_h[:, 1, :], lat_l[:, 1, :]))]
                              ).then_inc(S[f"qn{h}_mm"], 1)

            def scores(g, u):
                pe.wait_ge(S["qn0_ev"], g * NU + u + 1)
                pe.wait_ge(S["qn1_ev"], g * NU + u + 1)
                if u:
                    pe.wait_ge(S["score_ev"], g * NU + u)
                for b in range(GB):
                    cols = slice(b * C, (b + 1) * C)
                    nc.tensor.matmul(bank_s[:, cols], q_nope[:, b, :, :].rearrange("p h t -> p (h t)"),
                                     lat32[:, 0, cols], start=b == 0, stop=False)
                pe.wait_ge(S["rope_done"], g * NR + u + 2)
                for b in range(GB):
                    cols = slice(b * C, (b + 1) * C)
                    last = nc.tensor.matmul(bank_s[:, cols], q_rope[:, b, :, :].rearrange("p h t -> p (h t)"),
                                            k_rope[:, cols], start=False, stop=b == GB - 1)
                last.then_inc(S["score_mm"], 1)

            def prob_transpose(g, u):
                pe.wait_ge(S["prob_ev"], g * NU + u + 1)
                for n in range(NPAIR):
                    last = nc.tensor.transpose(bank_a[:, n * P:(n + 1) * P],
                                               prob[:, u % 2, 2 * n:2 * n + 2, :].rearrange("p j k -> p (j k)"),
                                               K.parts["ident"])
                last.then_inc(S["pt_mm"], 1)

            def mix(g, u, parities=(0, 1)):
                pe.wait_ge(S["pt_ev"], g * NU + u + 1)
                last = {}
                for n in range(NPAIR):
                    for j in parities:
                        rows = slice(j * C, (j + 1) * C)
                        last[j] = nc.tensor.matmul((bank_b, bank_d)[j][:, n * P:(n + 1) * P], kv_tok[rows, n, :],
                                                   probT[rows, n, :], start=True, stop=True)
                for j in parities:
                    last[j].then_inc(S[("mixe_mm", "mixo_mm")[j]], 1)

            def first():
                bias_rows(0)
                cond(0, 0, bank_d)
                pe.wait_ge(S["bias_ev"], 1)
                cond(0, 1, bank_s)
                cond(0, 2, bank_a)
                pe.wait_ge(S["cond_ev"], 2)
                cond(0, 3, bank_s)
                latent(0, 0, bank_a)
                latent(0, 1, bank_s)
                kv_tokens(0)
                head(0)

            def head(g, prev=None):
                rope_keys(g)
                q_rope_mm(g, 0)
                pe.wait_ge(S["kvt_ev"], g + 1)
                q_nope_mm(g, 0, 0)
                pe.wait_ge(S["raw_ev"], g * NR + 1)
                q_nope_mm(g, 0, 1)
                if prev is not None:
                    wz(prev, NU - 1, 2)
                pe.wait_ge(S["raw_ev"], g * NR + 2)
                q_rope_mm(g, 1)
                scores(g, 0)
                q_nope_mm(g, 1, 0)
                q_nope_mm(g, 1, 1)
                if prev is not None:
                    wz(prev, NU - 1, 3)

            def body(g, more):
                scores(g, 1)
                pe.wait_ge(S["raw_ev"], g * NR + 3)
                q_rope_mm(g, 2)
                q_nope_mm(g, 2, 0)
                pe.wait_ge(S["raw_ev"], g * NR + 4)
                prob_transpose(g, 0)
                q_nope_mm(g, 2, 1)
                for j in range(2):
                    pe.wait_ge(S[f"qn{j}_ev"], g * NU + 3)
                    mix(g, 0, (j, ))
                for u in range(2, NU):
                    scores(g, u)
                    if u + 1 < NU:
                        pe.wait_ge(S["raw_ev"], g * NR + u + 2)
                        pe.wait_ge(S["pt_ev"], g * NU + u - 1)
                        q_rope_mm(g, u + 1)
                    wz(g, u - 2, 0)
                    if u + 1 < NU:
                        pe.wait_ge(S["mixe_lo"], g * NU + u - 1)
                        q_nope_mm(g, u + 1, 0)
                        pe.wait_ge(S["raw_ev"], g * NR + u + 3)
                    else:
                        pe.wait_ge(S["pt_ev"], g * NU + u - 1)
                    prob_transpose(g, u - 1)
                    if u + 1 < NU:
                        pe.wait_ge(S["mixo_lo"], g * NU + u - 1)
                        q_nope_mm(g, u + 1, 1)
                    wz(g, u - 2, 1)
                    if u + 1 < NU:
                        pe.wait_ge(S["qn0_ev"], g * NU + u + 2)
                        pe.wait_ge(S["qn1_ev"], g * NU + u + 2)
                    else:
                        pe.wait_ge(S["mixe_lo"], g * NU + u - 1)
                        pe.wait_ge(S["mixo_lo"], g * NU + u - 1)
                    mix(g, u - 1)
                    wz(g, u - 2, 2)
                    wz(g, u - 2, 3)
                n = g * NU + NU
                g1 = g + 1
                pe.wait_ge(S["score_ev"], n)
                if more:
                    bias_rows(g1)
                wz(g, NU - 2, 0)
                pe.wait_ge(S["pt_ev"], n - 1)
                prob_transpose(g, NU - 1)
                pe.wait_ge(S["mixo_lo"], n - 1)
                if more:
                    cond(g1, 0, bank_d)
                wz(g, NU - 2, 1)
                pe.wait_ge(S["mixe_lo"], n - 1)
                if more:
                    pe.wait_ge(S["cond_ev"], g1 * TC + 1)
                mix(g, NU - 1)
                if more:
                    pe.wait_ge(S["bias_ev"], g1 + 1)
                    cond(g1, 1, bank_s)
                    pe.wait_ge(S["pt_ev"], n)
                    cond(g1, 2, bank_a)
                wz(g, NU - 2, 2)
                if more:
                    pe.wait_ge(S["cond_ev"], g1 * TC + 2)
                    cond(g1, 3, bank_s)
                wz(g, NU - 2, 3)
                if more:
                    latent(g1, 0, bank_a)
                    latent(g1, 1, bank_s)
                wz(g, NU - 1, 0)
                wz(g, NU - 1, 1)
                if more:
                    kv_tokens(g1)
                    head(g1, prev=g)
                else:
                    wz(g, NU - 1, 2)
                    wz(g, NU - 1, 3)

            over_groups(pe, first, body)


EARLY = 2
SLOTS = NG - EARLY


def slot_of(g):
    return g % 2 if g < EARLY + 2 else g - EARLY


BT = 512
CH = BT // P
PAIR = 2


def pair0_tiles(K):
    tile = K["pair0"][:, :, :].rearrange("p c n -> p (c n)")
    half = TC * PAIR * P
    return (tile[:, 0:half].rearrange("p (c k n) -> p c k n", c=TC, k=PAIR),
            tile[:, half:].rearrange("p (k n) -> p k n", k=PAIR))


def expert_weights(A):
    return (A["W1"].rearrange("e (c p) (m n) -> e m p c n", p=P, n=PAIR * P),
            A["W2"].rearrange("e (m k p) n -> e m p k n", p=P, k=PAIR))


def load_pair0(nc, K, sp, A, e):
    (w1, w2), (w1_d, w2_d) = pair0_tiles(K), expert_weights(A)
    with nc.allow_non_contiguous_dma(reason="rows of 1 KiB"):
        sp.dma_start(w1.rearrange("p c k n -> p c (k n)"), w1_d[e, 0]).then_inc(K.sems["pair0_in"], 16)
    sp.dma_start(w2, w2_d[e, 0]).then_inc(K.sems["pair0_in"], 16)


def routing(nc, K, A, x2, flat, R):
    with ExitStack() as ctx:
        def sb(name, shape, dt=F32):
            return ctx.enter_context(nc.sbuf_tensor(name, shape, dt))

        def bank(name):
            return ctx.enter_context(nc.psum_tensor(name, [P, 512], F32))

        def sem(name):
            return ctx.enter_context(nc.semaphore(name))

        NR = NADAPT * RANK
        EJ = NE * NT
        load_table(nc, ctx, K, "route")
        c = K.parts
        NV = 5
        w_raw = K["stage"]
        ROW = NT * NV * NCH // 2
        raw = sb("routing_raw", [P, ROW + TC * NR])
        a_raw = raw[:, 0:T]
        b_raw = raw[:, ROW:].rearrange("p (c n r) -> p c n r", c=TC, n=NADAPT)
        is_hi = raw[:, ROW:].bitcast(BF16).rearrange("p (n c) -> p n c", c=NCH)
        row = [tile.bitcast(BF16).rearrange("p (n v c) -> p n v c", v=NV, c=NCH)
               for tile in (raw[:, 0:ROW], sb("row_odd", [P, ROW])[:, :])]
        wg = sb("wg", [P, TC, NE])
        bg = sb("bg", [P, NE])
        adapt, scal = sb("adapt", [P, B], I32), sb("scal", [P, 1])
        lora_sel = sb("lora_sel", [P, B])
        WTh, WTl = sb("WTh", [P, TC, T], F32R), sb("WTl", [P, TC, T], F32R)
        ATh, ATl = sb("ATh", [P, TC, NR], F32R), sb("ATl", [P, TC, NR], F32R)
        BTh, BTl = sb("BTh", [NR, T], F32R), sb("BTl", [NR, T], F32R)
        WG = sb("WG", [P, TC + 1, 2, NE], F32R)
        logitT = sb("logitT", [2 * NE, GT])
        x_in_sb = (K["rows"], sb("x_odd", [P, NPAIR, T]))
        xTh, xTl = sb("xTh", [P, SLOTS, TC, GT], F32R), sb("xTl", [P, SLOTS, TC, GT], F32R)
        low32 = sb("low32", [NR, GT])
        lowh, lowl = sb("lowh", [NR, SLOTS, GT], F32R), sb("lowl", [NR, SLOTS, GT], F32R)
        flat_sb = sb("flat_sb", [P, 4, T])
        logit = sb("logit", [P, NT, NE])
        bank_t = [bank(f"r_t{i}") for i in range(TC)]
        bank_x, bank_l, bank_f = bank("r_x"), bank("r_l"), [bank("r_f0"), bank("r_f1")]
        LIST_BANK = (bank_l, bank_x)

        cmpk = sb("cmpk", [P, NE, NT, NE])
        rank, top = sb("rank", [P, NT, NE]), sb("top", [P, NT, NE])
        lmax = sb("lmax", [P, NT])
        ex, ey, ek, ep, e2 = (sb(n, [P, NT, NE]) for n in ("ex", "ey", "ek", "ep", "e2"))
        ei = sb("ei", [P, NT, NE], I32)
        esum, einv = sb("esum", [P, NT]), sb("einv", [P, NT])
        gate, key = sb("gate", [P, NE, NT]), sb("key", [P, NE, NT])
        thr = sb("thr", [P, NE], I32)
        cand = sb("cand", [P, NE, CANDS], I32)
        above = K["rows"][:, :, :].rearrange("p n t -> p (n t)")[:, 0:NE * CANDS * NT].rearrange(
            "p (e c j) -> p e c j", e=NE, c=CANDS)
        count = sb("count", [P, NE, CANDS])
        hit = sb("hit", [P, NE, CANDS])
        step_bits = sb("step_bits", [P, NE], I32)
        positive = sb("positive", [P, NE])
        thrf = sb("thrf", [P, NE])
        over, same = sb("over", [P, NE, NT]), sb("same", [P, NE, NT])
        need = sb("need", [P, NE])
        mark = sb("mark", [P, NE, NT], BF16)
        ones_b, before_b = sb("ones_b", [P, P], BF16), sb("before_b", [P, P], BF16)
        iota_b = sb("iota_b", [P, P], BF16)
        chosen = sb("chosen", [P, NE, NT])
        pos = sb("pos", [P, NE, NT], I32)
        pos_lo, slot_lo, slot_hi = sb("pos_lo", [P, NE, NT], I32), sb("slot_lo", [P, NE, NT]), sb("slot_hi", [P, NE, NT])
        pos_hi = ei[:, :, :].rearrange("p j e -> p (j e)").rearrange("p (e j) -> p e j", e=NE)
        part3 = sb("part3", [P, 3, NE, NT], BF16)
        rest = sb("rest", [P, 2, NE, NT])
        value = sb("value", [P, EJ, NV], BF16)
        LQ = NT // 2
        lo_buffers = [t[:, :, :].rearrange("p n t -> p (n t)").bitcast(BF16).rearrange(
            "p (q j s) -> p q j s", q=2, j=LQ)[:, k, :, :] for t in (x_in_sb[1], x_in_sb[0]) for k in range(2)]

        def is_lo(q):
            return lo_buffers[q if q < 4 else q % 2]

        listed = sb("listed", [P, NV, NCH])
        tokf = sb("tokf", [P, NCH])

        names = """a_in b_in wt_mm wt_hi wt_lo at_mm at_hi at_lo bt_mm bt_hi bt_lo wg_mm wg_hi wg_lo sel_ready
            xt_mm xt_hi xt_lo low_mm low_ev low_hi low_lo lgt_mm lgt_ev lg_mm lg_ev fl_mm fl_ev
            chain count_ready count_mm hi_ready row_ready prefix_ready prefix_mm lo_ready list_mm list_ev table_in""".split()
        S = {n: sem("rt_" + n) for n in names}
        x_in = [sem(f"rt_x_in{k}") for k in range(2)]
        fl_out = [sem(f"rt_fl_out{k}") for k in range(4)]
        x_d = x2.rearrange("(g n j) c t -> g (j c) n t", n=NPAIR, j=2)
        flat_d = flat.rearrange("(n p) t -> n p t", p=P)

        block = ctx.enter_context(nc.Block())

        @block.sync
        def _(sp):
            sp.dma_start(a_raw[:, :], A["A"].rearrange("n r d -> (n r) d")).then_inc(K.sems["w_in"], 16)
            for g in range(2):
                sp.dma_start(x_in_sb[g][:, :, :], x_d[g]).then_inc(x_in[g], 16)
            with nc.allow_non_contiguous_dma(reason="small operands, once"):
                sp.dma_start(bg[:, :], A["bg"].partition_broadcast(P)).then_inc(S["a_in"], 16)
                sp.dma_start(adapt[:, :], A["adapt"].partition_broadcast(P)).then_inc(S["a_in"], 16)
                for n in range(NADAPT):
                    sp.dma_start(scal[n * RANK:(n + 1) * RANK, :],
                                 A["scalings"][n:n + 1].partition_broadcast(RANK)).then_inc(S["a_in"], 16)
            sp.dma_start(K["route"][:, :], A["route"]).then_inc(S["table_in"], 16)
            for g in range(2, NG):
                sp.wait_ge(S["xt_mm"], (g - 1) * TC)
                sp.dma_start(x_in_sb[g % 2][:, :, :], x_d[g]).then_inc(x_in[g % 2], 16)
            sp.wait_ge(S["wg_mm"], 1)
            load_pair0(nc, K, sp, A, 0)

        B_IN, A_IN = 16 * (TC + 1), 16 * (2 + NADAPT)

        @block.gpsimd
        def _(pool):
            pool.wait_ge(S["hi_ready"], 1)
            for e in range(NE):
                mine = slice(e * NT, (e + 1) * NT)
                if e >= 2:
                    pool.wait_ge(S["list_mm"], (e - 1) * NT)
                nc.gpsimd.tensor_tensor(row[e % 2][:, :, :, :], is_hi[:, mine, :].unsqueeze(2).to_broadcast([P, NT, NV, NCH]),
                                        value[:, mine, :].unsqueeze(3).to_broadcast([P, NT, NV, NCH]),
                                        ALU.mult).then_inc(S["row_ready"], 1)
            for k in range(4):
                pool.wait_ge(fl_out[k], 16 * (NT // 4))
            pool.wait_ge(S["list_ev"], 1)
            for k in range(CH):
                pool.indirect_dma_start(K["rows"][:, k, :], None, flat,
                                        bass.IndirectOffsetOnAxis(ap=R["token"][:, k:k + 1], axis=0)
                                        ).then_inc(K.sems["rows_in"], 16)

        @block.scalar
        def _(act):
            def copy(out, bk, ready, count, done):
                act.wait_ge(S[ready], count)
                nc.scalar.copy(out, bk).then_inc(S[done], 1)

            with nc.allow_non_contiguous_dma(reason="small operands, once"):
                for i in range(TC):
                    act.dma_start(b_raw[:, i, :, :], A["Bm"][:, i * P:(i + 1) * P, :].rearrange("n p r -> p n r")
                                  ).then_inc(S["b_in"], 16)
                act.dma_start(wg[:, :, :], A["Wg"].rearrange("(c p) e -> p c e", p=P)).then_inc(S["b_in"], 16)
            for i in range(TC):
                copy(WTh[:, i, :], bank_t[i][:, :], "wt_mm", i + 1, "wt_hi")
            copy(ATh[:, :, :], bank_x[:, :].rearrange("p (c n) -> p c n", c=TC), "at_mm", 1, "at_hi")

            def logits(g):
                copy(logitT[:, :], bank_l[0:2 * NE, :], "lgt_mm", g + 1, "lgt_ev")

            def front(g):
                s = slot_of(g)
                for i in range(TC):
                    copy(xTh[:, s, i, :], bank_t[i][:, :], "xt_mm", g * TC + i + 1, "xt_hi")
                if g:
                    logits(g - 1)
                act.wait_ge(S["low_ev"], g + 1)
                nc.scalar.copy(lowh[:, s, :], low32[:, :]).then_inc(S["low_hi"], 1)

            def back_tile(n):
                act.wait_ge(S["fl_mm"], n + 1)
                if n >= 4:
                    act.wait_ge(fl_out[n % 4], 16 * (n // 4))
                nc.scalar.copy(flat_sb[:, n % 4, :], bank_f[n % 2][:, :]).then_inc(S["fl_ev"], 1)
                act.wait_ge(S["fl_ev"], n + 1)
                act.dma_start(flat_d[n], flat_sb[:, n % 4, :]).then_inc(fl_out[n % 4], 16)

            def back(g):
                for t in range(NPAIR):
                    back_tile(g * NPAIR + t)

            front(0)
            copy(BTh[:, :], bank_f[0][:, :], "bt_mm", 1, "bt_hi")
            copy(WG[:, :, 0, :], bank_l[:, 0:(TC + 1) * NE].rearrange("p (c e) -> p c e", e=NE), "wg_mm", 1, "wg_hi")
            for g in range(1, NG):
                front(g)
                if g <= EARLY:
                    back(g - 1)
            back_tile(EARLY * NPAIR)
            logits(NG - 1)
            for n in range(EARLY * NPAIR + 1, NT):
                back_tile(n)
            for k in range(4):
                act.wait_ge(fl_out[k], 16 * (NT // 4))

        @block.vector
        def _(dve):
            v = nc.vector
            steps = [0]

            def link(instruction):
                steps[0] += 1
                instruction.then_inc(S["chain"], 1)
                dve.wait_ge(S["chain"], steps[0])

            def low_part(out, bk, hi, ready, count, done):
                dve.wait_ge(S[ready], count)
                v.tensor_tensor(out, bk, hi.bitcast(F32), ALU.subtract).then_inc(S[done], 1)

            for i in range(TC):
                low_part(WTl[:, i, :], bank_t[i][:, :], WTh[:, i, :], "wt_hi", i + 1, "wt_lo")
            low_part(ATl[:, :, :], bank_x[:, :].rearrange("p (c n) -> p c n", c=TC), ATh[:, :, :], "at_hi", 1, "at_lo")

            def front(g):
                s = slot_of(g)
                for i in range(TC):
                    low_part(xTl[:, s, i, :], bank_t[i][:, :], xTh[:, s, i, :], "xt_hi", g * TC + i + 1, "xt_lo")
                if g == 0:
                    dve.wait_ge(S["a_in"], A_IN)
                    dve.wait_ge(S["table_in"], 16)
                    link(v.tensor_scalar(lora_sel[:, :], adapt[:, :], c["adapter"], None, ALU.is_equal))
                    link(v.tensor_scalar(lora_sel[:, :], lora_sel[:, :], scal[:, :], None, ALU.mult))
                dve.wait_ge(S["low_mm"], g + 1)
                v.tensor_tensor(low32[:, :].rearrange("p (b t) -> p b t", b=GB),
                                bank_x[:, :].rearrange("p (b t) -> p b t", b=GB),
                                lora_sel[:, g * GB:(g + 1) * GB].unsqueeze(2).to_broadcast([NR, GB, C]),
                                ALU.mult).then_inc(S["low_ev"], 1)
                dve.wait_ge(S["low_hi"], g + 1)
                v.tensor_tensor(lowl[:, s, :], low32[:, :], lowh[:, s, :].bitcast(F32),
                                ALU.subtract).then_inc(S["low_lo"], 1)

            def logits_out(g):
                dve.wait_ge(S["lg_mm"], g + 1)
                v.tensor_tensor(logit[:, g * NPAIR:(g + 1) * NPAIR, :],
                                bank_l[:, 0:NPAIR * NE].rearrange("p (t e) -> p t e", e=NE),
                                bg[:, :].unsqueeze(1).to_broadcast([P, NPAIR, NE]), ALU.add).then_inc(S["lg_ev"], 1)

            front(0)
            low_part(BTl[:, :], bank_f[0][:, :], BTh[:, :], "bt_hi", 1, "bt_lo")
            low_part(WG[:, :, 1, :], bank_l[:, 0:(TC + 1) * NE].rearrange("p (c e) -> p c e", e=NE), WG[:, :, 0, :],
                     "wg_hi", 1, "wg_lo")
            for g in range(1, NG):
                front(g)
                logits_out(g - 1)
            logits_out(NG - 1)
            dve.wait_ge(S["lg_ev"], NG)

            link(v.memset(cmpk[:, :, :, :], 0.0))
            for k in range(NE):
                one = logit[:, :, k:k + 1]
                if k + 1 < NE:
                    v.tensor_tensor(cmpk[:, k, :, k + 1:NE], one.to_broadcast([P, NT, NE - 1 - k]),
                                    logit[:, :, k + 1:NE], ALU.is_ge)
                if k:
                    v.tensor_tensor(cmpk[:, k, :, 0:k], one.to_broadcast([P, NT, k]), logit[:, :, 0:k], ALU.is_gt)
            link(v.tensor_reduce(lmax[:, :], logit[:, :, :], AX, ALU.max))
            link(v.tensor_reduce(rank[:, :, :], cmpk[:, :, :, :].rearrange("p k j e -> p j e k"), AX, ALU.add))
            link(v.tensor_scalar(top[:, :, :], rank[:, :, :], 1.5, None, ALU.is_lt))

            link(v.tensor_tensor(ex[:, :, :], logit[:, :, :], lmax[:, :].unsqueeze(2).to_broadcast([P, NT, NE]),
                                 ALU.subtract))
            link(v.tensor_scalar(ex[:, :, :], ex[:, :, :], -87.0, None, ALU.max))
            link(v.tensor_scalar(ey[:, :, :], ex[:, :, :], float(np.float32(np.log2(np.e))), 12582912.0,
                                 ALU.mult, ALU.add))
            link(v.tensor_scalar(ek[:, :, :], ey[:, :, :], 12582912.0, None, ALU.subtract))
            link(v.scalar_tensor_tensor(out=ex[:, :, :], in0=ek[:, :, :], scalar=-0.693359375, in1=ex[:, :, :],
                                        op0=ALU.mult, op1=ALU.add))
            link(v.scalar_tensor_tensor(out=ex[:, :, :], in0=ek[:, :, :], scalar=2.12194440e-4, in1=ex[:, :, :],
                                        op0=ALU.mult, op1=ALU.add))
            coefficients = [1.0 / n for n in (5040.0, 720.0, 120.0, 24.0, 6.0, 2.0, 1.0)]
            link(v.tensor_scalar(ep[:, :, :], ex[:, :, :], coefficients[0], None, ALU.mult))
            for k in coefficients[1:]:
                link(v.scalar_tensor_tensor(out=ep[:, :, :], in0=ep[:, :, :], scalar=k, in1=ex[:, :, :],
                                            op0=ALU.add, op1=ALU.mult))
            link(v.tensor_scalar(ei[:, :, :], ek[:, :, :], 127.0, 8388608.0, ALU.add, ALU.mult))
            link(v.scalar_tensor_tensor(out=e2[:, :, :], in0=ep[:, :, :], scalar=1.0,
                                        in1=ei[:, :, :].bitcast(F32), op0=ALU.add, op1=ALU.mult))
            link(v.tensor_tensor(e2[:, :, :], e2[:, :, :], top[:, :, :], ALU.mult))
            link(v.tensor_reduce(esum[:, :], e2[:, :, :], AX, ALU.add))
            link(v.reciprocal(einv[:, :], esum[:, :]))
            link(v.tensor_tensor(gate[:, :, :].rearrange("p e j -> p j e"), e2[:, :, :],
                                 einv[:, :].unsqueeze(2).to_broadcast([P, NT, NE]), ALU.mult))
            link(v.scalar_tensor_tensor(out=key[:, :, :].rearrange("p e j -> p j e"), in0=top[:, :, :], scalar=-1.0,
                                        in1=gate[:, :, :].rearrange("p e j -> p j e"), op0=ALU.add, op1=ALU.add))

            counts = [0]
            val = value[:, :, :].rearrange("p (e j) v -> p e j v", e=NE)
            meanwhile = [
                lambda: v.tensor_copy(ones_b[:, :], c["ones"]),
                lambda: v.tensor_copy(before_b[:, :], c["before"]),
                lambda: v.tensor_copy(iota_b[:, :], c["iota"]),
                lambda: v.tensor_copy(part3[:, 0, :, :], gate[:, :, :]),
                lambda: v.tensor_tensor(rest[:, 0, :, :], gate[:, :, :], part3[:, 0, :, :], ALU.subtract),
                lambda: v.tensor_copy(part3[:, 1, :, :], rest[:, 0, :, :]),
                lambda: v.tensor_tensor(rest[:, 1, :, :], rest[:, 0, :, :], part3[:, 1, :, :], ALU.subtract),
                lambda: v.tensor_copy(part3[:, 2, :, :], rest[:, 1, :, :]),
                lambda: v.tensor_copy(val[:, :, :, 0], c["tile"].unsqueeze(1).to_broadcast([P, NE, NT])),
                lambda: v.tensor_copy(val[:, :, :, 1], c["part"].unsqueeze(2).to_broadcast([P, NE, NT])),
                lambda: v.tensor_copy(val[:, :, :, 2], part3[:, 0, :, :]),
                lambda: v.tensor_copy(val[:, :, :, 3], part3[:, 1, :, :]),
                lambda: v.tensor_copy(val[:, :, :, 4], part3[:, 2, :, :]),
            ]

            def total(mask, width):
                link(v.tensor_reduce(count[:, :, 0:width], mask, AX, ALU.add))
                counts[0] += 1
                v.tensor_copy(hit[:, :, 0:width], count[:, :, 0:width]).then_inc(S["count_ready"], 1)
                for _ in range(min(2, len(meanwhile))):
                    link(meanwhile.pop(0)())
                dve.wait_ge(S["count_mm"], counts[0])

            totals = bank_l[:, 0:NE * CANDS].rearrange("p (e c) -> p e c", c=CANDS)
            link(v.memset(hit[:, :, :], 0.0))
            link(v.tensor_scalar(above[:, :, 0, :], key[:, :, :], 0.0, None, ALU.is_ge))
            total(above[:, :, 0:1, :], 1)
            link(v.tensor_scalar(positive[:, :].unsqueeze(2), totals[:, :, 0:1], float(CAP), None, ALU.is_ge))
            link(v.memset(thr[:, :], 0))
            for i in range(TRIALS):
                trial = c["trial"][:, CANDS * i:CANDS * (i + 1)].bitcast(I32)
                link(v.tensor_tensor(cand[:, :, :], thr[:, :].unsqueeze(2).to_broadcast([P, NE, CANDS]),
                                     trial.unsqueeze(1).to_broadcast([P, NE, CANDS]), ALU.bitwise_or))
                link(v.tensor_tensor(above[:, :, :, :], key[:, :, :].unsqueeze(2).to_broadcast([P, NE, CANDS, NT]),
                                     cand[:, :, :].bitcast(F32).unsqueeze(3).to_broadcast([P, NE, CANDS, NT]),
                                     ALU.is_ge))
                total(above[:, :, :, :], CANDS)
                link(v.tensor_scalar(hit[:, :, :], totals, float(CAP), float(1 << (BITS * (TRIALS - 1 - i))),
                                     ALU.is_ge, ALU.mult))
                with nc.allow_low_precision(reason="at most seven equal powers of two: exact"):
                    link(v.tensor_reduce(step_bits[:, :], hit[:, :, :], AX, ALU.add))
                link(v.tensor_tensor(thr[:, :], thr[:, :], step_bits[:, :], ALU.bitwise_or))
            link(v.tensor_tensor(thrf[:, :], thr[:, :].bitcast(F32), positive[:, :], ALU.mult))
            link(v.scalar_tensor_tensor(out=thrf[:, :], in0=positive[:, :], scalar=-1.0, in1=thrf[:, :],
                                        op0=ALU.add, op1=ALU.add))

            limit = thrf[:, :].unsqueeze(2).to_broadcast([P, NE, NT])
            link(v.tensor_tensor(over[:, :, :], key[:, :, :], limit, ALU.is_gt))
            link(v.tensor_tensor(same[:, :, :], key[:, :, :], limit, ALU.is_equal))
            total(over[:, :, :].unsqueeze(2), 1)
            link(v.tensor_scalar(need[:, :].unsqueeze(2), totals[:, :, 0:1], -1.0, float(CAP), ALU.mult, ALU.add))
            earlier = bank_x[:, 0:EJ].rearrange("p (e j) -> p e j", e=NE)
            v.tensor_copy(mark[:, :, :], same[:, :, :]).then_inc(S["prefix_ready"], 1)
            dve.wait_ge(S["prefix_mm"], 1)
            link(v.tensor_tensor(chosen[:, :, :], earlier, need[:, :].unsqueeze(2).to_broadcast([P, NE, NT]),
                                 ALU.is_lt))
            link(v.tensor_tensor(chosen[:, :, :], chosen[:, :, :], same[:, :, :], ALU.mult))
            link(v.tensor_tensor(chosen[:, :, :], chosen[:, :, :], over[:, :, :], ALU.add))
            v.tensor_copy(mark[:, :, :], chosen[:, :, :]).then_inc(S["prefix_ready"], 1)
            dve.wait_ge(S["prefix_mm"], 2)
            link(v.scalar_tensor_tensor(out=rest[:, 0, :, :], in0=earlier, scalar=1.0, in1=chosen[:, :, :],
                                        op0=ALU.add, op1=ALU.mult))
            link(v.tensor_scalar(pos[:, :, :], rest[:, 0, :, :], 1.0, None, ALU.subtract))
            v.tensor_scalar(pos_lo[:, :, :], pos[:, :, :], P - 1, None, ALU.bitwise_and)
            link(v.tensor_scalar(pos_hi[:, :, :], pos[:, :, :], 7, None, ALU.arith_shift_right))
            link(v.tensor_copy(slot_lo[:, :, :], pos_lo[:, :, :]))
            link(v.tensor_copy(slot_hi[:, :, :], pos_hi[:, :, :]))
            v.tensor_tensor(is_hi[:, :, :],
                            slot_hi[:, :, :].rearrange("p e j -> p (e j)").unsqueeze(2).to_broadcast([P, EJ, NCH]),
                            c["iota"][:, 0:NCH].unsqueeze(1).to_broadcast([P, EJ, NCH]),
                            ALU.is_equal).then_inc(S["hi_ready"], 1)

            def lo_tiles(q):
                e, j = q * LQ // NT, q * LQ % NT
                if q >= 4:
                    dve.wait_ge(S["list_mm"], (q - (4 if q < 6 else 2) + 1) * LQ)
                v.tensor_tensor(is_lo(q), iota_b[:, :].unsqueeze(1).to_broadcast([P, LQ, P]),
                                slot_lo[:, e, j:j + LQ].unsqueeze(2).to_broadcast([P, LQ, P]),
                                ALU.is_equal).then_inc(S["lo_ready"], 1)

            for q in range(2):
                lo_tiles(q)
            for e in range(NE):
                if e + 1 < NE:
                    for q in range(2 * (e + 1), 2 * (e + 2)):
                        lo_tiles(q)
                dve.wait_ge(S["list_mm"], (e + 1) * NT)
                link(v.tensor_copy(listed[:, :, :], LIST_BANK[e % 2][:, 0:NV * NCH].rearrange("p (v c) -> p v c", v=NV)))
                v.scalar_tensor_tensor(out=R["token"][:, e * NCH:(e + 1) * NCH], in0=listed[:, 0, :], scalar=float(P),
                                       in1=listed[:, 1, :], op0=ALU.mult, op1=ALU.add)
                link(v.tensor_tensor(tokf[:, :], listed[:, 2, :], listed[:, 3, :], ALU.add))
                v.tensor_tensor(R["gate"][:, e * NCH:(e + 1) * NCH], tokf[:, :], listed[:, 4, :], ALU.add).then_inc(S["list_ev"], 1)
                dve.wait_ge(S["list_ev"], e + 1)

        @block.tensor
        def _(pe):
            ident = c["ident"]
            pe.wait_ge(K.sems["w_in"], 32)
            for i in range(TC):
                for o in range(TC):
                    last = nc.tensor.transpose(bank_t[i][:, o * P:(o + 1) * P], w_raw[:, o, i * P:(i + 1) * P], ident)
                last.then_inc(S["wt_mm"], 1)
            for i in range(TC):
                last = nc.tensor.transpose(bank_x[:, i * P:(i + 1) * P], a_raw[:, i * P:(i + 1) * P], ident)
            last.then_inc(S["at_mm"], 1)

            def front(g):
                s = slot_of(g)
                pe.wait_ge(x_in[g % 2], 16 * (g // 2 + 1))
                if g:
                    pe.wait_ge(S["xt_lo"], g * TC)
                else:
                    pe.wait_ge(S["wt_lo"], TC)
                for i in range(TC):
                    for t in range(NPAIR):
                        last = nc.tensor.transpose(bank_t[i][:, t * P:(t + 1) * P],
                                                   x_in_sb[g % 2][:, t, i * P:(i + 1) * P], ident)
                    last.then_inc(S["xt_mm"], 1)
                if g:
                    logitsT(g - 1)
                pe.wait_ge(S["at_lo"], 1)
                if g:
                    pe.wait_ge(S["low_ev"], g)
                for i in range(TC):
                    pe.wait_ge(S["xt_lo"], g * TC + i + 1)
                    last = split_product(nc, bank_x[:, :], [((ATh[:, i, :], ATl[:, i, :]),
                                                             (xTh[:, s, i, :], xTl[:, s, i, :]))],
                                         start=i == 0, stop=i == TC - 1)
                last.then_inc(S["low_mm"], 1)
                if g:
                    logits(g - 1)

            def operands(g, t):
                s, cols = slot_of(g), slice(t * P, (t + 1) * P)
                return [(xTh[:, s, i, cols], xTl[:, s, i, cols]) for i in range(TC)] + [(lowh[:, s, cols],
                                                                                         lowl[:, s, cols])]

            def logitsT(g):
                pe.wait_ge(S["low_lo"], g + 1)
                pe.wait_ge(S["wg_lo"], 1)
                if g:
                    pe.wait_ge(S["lg_ev"], g)
                s = slot_of(g)
                parts = [(xTh[:, s, i, :], xTl[:, s, i, :]) for i in range(TC)] + [(lowh[:, s, :], lowl[:, s, :])]
                for i, part in enumerate(parts):
                    for j in range(2):
                        last = nc.tensor.matmul(bank_l[0:2 * NE, :], WG[:, i, :, :].rearrange("p j e -> p (j e)"),
                                                part[j], start=i == j == 0, stop=i == TC and j == 1)
                last.then_inc(S["lgt_mm"], 1)

            def logits(g):
                pe.wait_ge(S["lgt_ev"], g + 1)
                for t in range(NPAIR):
                    last = nc.tensor.matmul(bank_l[:, t * NE:(t + 1) * NE], logitT[:, t * P:(t + 1) * P],
                                            c["fold"][0:2 * NE, :], start=True, stop=True)
                last.then_inc(S["lg_mm"], 1)

            def project(g, t):
                n = g * NPAIR + t
                pe.wait_ge(S["bt_lo"], 1)
                if n >= 2:
                    pe.wait_ge(S["fl_ev"], n - 1)
                weights = [(WTh[:, i, :], WTl[:, i, :]) for i in range(TC)] + [(BTh[:, :], BTl[:, :])]
                split_product(nc, bank_f[n % 2][:, :], list(zip(operands(g, t), weights))).then_inc(S["fl_mm"], 1)

            front(0)
            pe.wait_ge(S["b_in"], B_IN)
            for o in range(TC):
                last = nc.tensor.transpose(bank_f[0][:, o * P:(o + 1) * P],
                                           b_raw[:, o, :, :].rearrange("p n r -> p (n r)"), ident)
            last.then_inc(S["bt_mm"], 1)
            for i in range(TC + 1):
                for o in range(TC):
                    left = w_raw[:, o, i * P:(i + 1) * P] if i < TC else b_raw[:, o, :, :].rearrange("p n r -> p (n r)")
                    last = nc.tensor.matmul(bank_l[:, i * NE:(i + 1) * NE], left, wg[:, o, :],
                                            start=o == 0, stop=o == TC - 1)
            last.then_inc(S["wg_mm"], 1)
            for g in range(EARLY):
                front(g + 1)
                for t in range(NPAIR):
                    project(g, t)
            late = [(g, t) for g in range(EARLY, NG) for t in range(NPAIR)]
            for g in range(EARLY + 1, NG):
                front(g)
            project(*late.pop(0))
            logitsT(NG - 1)
            project(*late.pop(0))
            logits(NG - 1)
            for _ in range(3):
                project(*late.pop(0))

            done = [0, 0]

            def count_total():
                done[0] += 1
                pe.wait_ge(S["count_ready"], done[0])
                nc.tensor.matmul(bank_l[:, 0:NE * CANDS], c["ones"], hit[:, :, :].rearrange("p e c -> p (e c)"),
                                 start=True, stop=True).then_inc(S["count_mm"], 1)

            def prefix():
                done[1] += 1
                pe.wait_ge(S["prefix_ready"], done[1])
                all_marks = mark[:, :, :].rearrange("p e j -> p (e j)")
                out = bank_x[:, 0:EJ].rearrange("p (e j) -> p e j", e=NE)
                nc.tensor.matmul(bank_x[:, 0:EJ], before_b[:, :], all_marks, start=True, stop=False)
                for j in range(NT - 1):
                    last = nc.tensor.matmul(out[:, :, j + 1:NT], ones_b[:, :],
                                            mark[:, :, j:j + 1].to_broadcast([P, NE, NT - 1 - j]),
                                            start=False, stop=j == NT - 2)
                last.then_inc(S["prefix_mm"], 1)

            for i in range(TRIALS + 1):
                count_total()
                project(*late.pop(0))
            count_total()
            prefix()
            prefix()
            for _ in range(2):
                project(*late.pop(0))
            for e in range(NE):
                if e >= 2:
                    pe.wait_ge(S["list_ev"], e - 1)
                for j in range(NT):
                    n = e * NT + j
                    if late and j % (NT // 4) == 0:
                        project(*late.pop(0))
                    if j == 0:
                        pe.wait_ge(S["row_ready"], e + 1)
                    if j % LQ == 0:
                        pe.wait_ge(S["lo_ready"], n // LQ + 1)
                    nc.tensor.matmul(LIST_BANK[e % 2][:, 0:NV * NCH], is_lo(n // LQ)[:, j % LQ, :],
                                     row[e % 2][:, j, :, :].rearrange("p v c -> p (v c)"),
                                     start=j == 0, stop=j == NT - 1).then_inc(S["list_mm"], 1)


def experts(nc, K, A, out, flat, R):
    with ExitStack() as ctx:
        def sb(name, shape, dt=F32):
            return ctx.enter_context(nc.sbuf_tensor(name, shape, dt))

        def bank(name):
            return ctx.enter_context(nc.psum_tensor(name, [P, 512], F32))

        def sem(name):
            return ctx.enter_context(nc.semaphore(name))

        PER = CAP // BT
        NB = NE * PER
        PAIRS = HC // 2
        tok_in, tok_out = sb("tok_in", [P, CH], I32), sb("tok_out", [P, CH], I32)
        rows = K["rows"]
        xh, xl = sb("xh", [P, 2, TC, BT], F32R), sb("xl", [P, 2, TC, BT], F32R)
        w1_raw, w2_raw = sb("w1_raw", [P, PAIRS - 1, TC, PAIR, P]), sb("w2_raw", [P, PAIRS - 1, PAIR, T])
        w1_pair0, w2_pair0 = pair0_tiles(K)

        def w1_at(pair, chunk):
            return w1_pair0[:, :, chunk, :] if isinstance(pair, int) and pair == 0 else w1_raw[:, pair - 1, :, chunk, :]

        def w2_at(pair, chunk):
            return w2_pair0[:, chunk, :] if isinstance(pair, int) and pair == 0 else w2_raw[:, pair - 1, chunk, :]

        w1h, w1l = sb("w1h", [P, 2, TC, P], F32R), sb("w1l", [P, 2, TC, P], F32R)
        w2h, w2l = sb("w2h", [P, 2, T], F32R), sb("w2l", [P, 2, T], F32R)
        hid = sb("hid", [P, 2, BT])
        hh, hl = sb("hh", [P, 2, BT], F32R), sb("hl", [P, 2, BT], F32R)
        y_sb = sb("y_sb", [P, CH, T])
        wait_here = sb("wait_there", [1, 3])
        bank_x = [bank("e_x0"), bank("e_x1")]
        bank_h = [bank("e_h0"), bank("e_h1")]
        bank_y = [bank(f"e_y{i}") for i in range(CH)]
        names = """w1_hi w1_lo w2_hi w2_lo index_in index_out xt_mm xt_hi xt_lo h_mm h_act h_hi h_lo
            y_mm y_ev scattered here""".split()
        S = {n: sem("ex_" + n) for n in names}
        S["rows_in"] = K.sems["rows_in"]
        waited = [sem(f"ex_waited{k}") for k in range(2)]
        w_in = [K.sems["pair0_in"]] + [sem(f"ex_w_in{m}") for m in range(1, PAIRS)]
        block = ctx.enter_context(nc.Block())
        w1_d, w2_d = expert_weights(A)
        out_rows = out.rearrange("b c t -> (b c) t")

        LOOP = (HC - 4) // 2
        Y0 = 2

        def over_batches(eng, first, body):
            first()
            with eng.Fori(0, NB - 1) as b:
                body(b, True)
            body(NB - 1, False)

        def w_arrived(eng, b, pair):
            eng.wait_ge(w_in[pair], (b // PER + 1) * 32)

        def rounds(eng, b, more, one, after_two):
            def two(i):
                for k in range(2):
                    one(b * HC + 2 * i + 2 + k, k, (b, i + 2, k), (b, i + 1 + k, 1 - k))

            two(0)
            after_two()
            with eng.Fori(1, LOOP) as i:
                two(i)
            last = b * HC + HC
            one(last - 2, 0, (b + 1, 0, 0) if more else None, (b, PAIRS - 1, 1))
            one(last - 1, 1, (b + 1, 0, 1) if more else None, (b + 1, 0, 0) if more else None)

        def seam(b, one, between):
            n = b * HC + HC
            one(n, 0, (b + 1, 1, 0), (b + 1, 0, 1))
            between()
            one(n + 1, 1, (b + 1, 1, 1), (b + 1, 1, 0))

        @block.sync
        def _(sp):
            def load(e, m):
                if m == 0:
                    load_pair0(nc, K, sp, A, e)
                    return
                with nc.allow_non_contiguous_dma(reason="rows of 1 KiB"):
                    sp.dma_start(w1_raw[:, m - 1, :, :, :].rearrange("p c k n -> p c (k n)"), w1_d[e, m]
                                 ).then_inc(w_in[m], 16)
                sp.dma_start(w2_raw[:, m - 1, :, :], w2_d[e, m]).then_inc(w_in[m], 16)

            sp.wait_ge(S["rows_in"], CH * 16)
            for m in range(1, PAIRS):
                load(0, m)
            with sp.Fori(1, NE) as e:
                for m in range(PAIRS):
                    for n in ("w1_hi", "w1_lo", "w2_hi", "w2_lo"):
                        sp.wait_ge(S[n], (e * PER - 1) * HC + 2 * m + 2)
                    load(e, m)

        @block.gpsimd
        def _(pool):
            def w1_low(n, k, b, pair, chunk):
                pool.wait_ge(S["w1_hi"], n + 1)
                nc.gpsimd.tensor_tensor(w1l[:, k, :, :], w1_at(pair, chunk), w1h[:, k, :, :].bitcast(F32),
                                        ALU.subtract).then_inc(S["w1_lo"], 1)

            def w2_low(n, k, b, pair, chunk):
                pool.wait_ge(S["w2_hi"], n + 1)
                nc.gpsimd.tensor_tensor(w2l[:, k, :], w2_at(pair, chunk), w2h[:, k, :].bitcast(F32),
                                        ALU.subtract).then_inc(S["w2_lo"], 1)

            def one(n, k, w1, w2):
                if w1:
                    w1_low(n + 2, k, *w1)
                if w2:
                    w2_low(n + 1, 1 - k, *w2)

            def take_waits(b, k):
                pool.wait_ge(waited[k], b + 1)
                nc.gpsimd.tensor_tensor(wait_here[:, 1 + k:2 + k], wait_here[:, 0:1], wait_here[:, 0:1],
                                        ALU.add).then_inc(waited[k], 1)

            def gather(b):
                pool.wait_ge(S["index_in"], b)
                take_waits(b, 0)
                for c in range(CH):
                    pool.indirect_dma_start(rows[:, c, :], None, flat,
                                            bass.IndirectOffsetOnAxis(ap=tok_in[:, c:c + 1], axis=0)
                                            ).then_inc(S["rows_in"], 16)

            def scatter(b):
                pool.wait_ge(S["index_out"], b + 1)
                pool.wait_ge(S["y_ev"], (b + 1) * CH)
                take_waits(b, 1)
                for c in range(CH):
                    pool.indirect_dma_start(out_rows, bass.IndirectOffsetOnAxis(ap=tok_out[:, c:c + 1], axis=0),
                                            y_sb[:, c, :], None, compute_op=ALU.add).then_inc(S["scattered"], 16)

            def first():
                nc.gpsimd.memset(wait_here[:, :], 0.0).then_inc(S["here"], 1)
                pool.wait_ge(S["here"], 1)
                pool.sem_inc(waited[0], 2)
                pool.sem_inc(waited[1], 1)
                w1_low(0, 0, 0, 0, 0)
                w1_low(1, 1, 0, 0, 1)
                w2_low(0, 0, 0, 0, 0)
                one(0, 0, (0, 1, 0), (0, 0, 1))
                one(1, 1, (0, 1, 1), (0, 1, 0))

            def body(b, more):
                rounds(pool, b, more, one, lambda: gather(b + 1) if more else None)
                if more:
                    seam(b, one, lambda: scatter(b))
                else:
                    scatter(b)
                pool.wait_ge(S["scattered"], (b + 1) * CH * 16)

            over_batches(pool, first, body)

        @block.scalar
        def _(act):
            def w1_high(n, k, b, pair, chunk):
                w_arrived(act, b, pair)
                nc.scalar.copy(w1h[:, k, :, :], w1_at(pair, chunk)).then_inc(S["w1_hi"], 1)

            def w2_high(n, k, b, pair, chunk):
                w_arrived(act, b, pair)
                nc.scalar.copy(w2h[:, k, :], w2_at(pair, chunk)).then_inc(S["w2_hi"], 1)

            def gelu(n, k):
                act.wait_ge(S["h_mm"], n + 1)
                nc.scalar.activation(hid[:, k, :], bank_h[k][:, :], ACT.Gelu).then_inc(S["h_act"], 1)

            def one(n, k, w1, w2, between=None):
                gelu(n, k)
                if w1:
                    w1_high(n + 2, k, *w1)
                if between:
                    between()
                if w2:
                    act.wait_ge(S["y_mm"], n + Y0)
                    w2_high(n + 1, 1 - k, *w2)

            def x_high(b):
                for i in range(TC):
                    act.wait_ge(S["xt_mm"], b * TC + i + 1)
                    nc.scalar.copy(xh[:, b % 2, i, :], bank_x[i % 2][:, :]).then_inc(S["xt_hi"], 1)

            def gated(b):
                act.wait_ge(S["y_mm"], b * HC + HC + Y0)
                for c in (0, 2):
                    nc.scalar.activation(y_sb[:, c, :], bank_y[c][:, :], ACT.Copy,
                                         scale=R["gate"][:, bass.ds(b * CH + c, 1)]).then_inc(S["y_ev"], 1)

            def first():
                w1_high(0, 0, 0, 0, 0)
                w1_high(1, 1, 0, 0, 1)
                w2_high(0, 0, 0, 0, 0)
                x_high(0)
                one(0, 0, (0, 1, 0), (0, 0, 1))
                one(1, 1, (0, 1, 1), (0, 1, 0))

            def body(b, more):
                for i in range(LOOP):
                    for k in range(2):
                        one(b * HC + 2 * i + 2 + k, k, (b, i + 2, k), (b, i + 1 + k, 1 - k))
                last = b * HC + HC
                if more:
                    x_high(b + 1)
                one(last - 2, 0, (b + 1, 0, 0) if more else None, (b, PAIRS - 1, 1))
                one(last - 1, 1, (b + 1, 0, 1) if more else None, (b + 1, 0, 0) if more else None)
                if more:
                    one(last, 0, (b + 1, 1, 0), (b + 1, 0, 1), between=lambda: gated(b))
                    one(last + 1, 1, (b + 1, 1, 1), (b + 1, 1, 0))
                else:
                    gated(b)

            over_batches(act, first, body)

        @block.vector
        def _(dve):
            def one(n, k, w1=None, w2=None):
                dve.wait_ge(S["h_act"], n + 1)
                dve.wait_ge(S["y_mm"], n + Y0 - 1)
                nc.vector.tensor_copy(hh[:, k, :], hid[:, k, :]).then_inc(S["h_hi"], 1)
                dve.wait_ge(S["h_hi"], n + 1)
                nc.vector.tensor_tensor(hl[:, k, :], hid[:, k, :], hh[:, k, :].bitcast(F32),
                                        ALU.subtract).then_inc(S["h_lo"], 1)

            def index_in(b):
                nc.vector.tensor_copy(tok_in[:, :], R["token"][:, bass.ds(b * CH, CH)]).then_inc(S["index_in"], 1)

            def x_low(b):
                for i in range(TC):
                    dve.wait_ge(S["xt_hi"], b * TC + i + 1)
                    nc.vector.tensor_tensor(xl[:, b % 2, i, :], bank_x[i % 2][:, :], xh[:, b % 2, i, :].bitcast(F32),
                                            ALU.subtract).then_inc(S["xt_lo"], 1)

            def gated(b):
                dve.wait_ge(S["y_mm"], b * HC + HC + Y0)
                for c in (1, 3):
                    nc.vector.tensor_scalar(y_sb[:, c, :], bank_y[c][:, :], R["gate"][:, bass.ds(b * CH + c, 1)],
                                            None, ALU.mult).then_inc(S["y_ev"], 1)

            def first():
                x_low(0)
                one(0, 0)
                one(1, 1)

            def body(b, more):
                if more:
                    index_in(b + 1)
                with dve.Fori(0, LOOP) as i:
                    for k in range(2):
                        one(b * HC + 2 * i + 2 + k, k)
                last = b * HC + HC
                nc.vector.tensor_copy(tok_out[:, :], R["token"][:, bass.ds(b * CH, CH)]).then_inc(S["index_out"], 1)
                if more:
                    x_low(b + 1)
                one(last - 2, 0)
                one(last - 1, 1)
                if more:
                    one(last, 0)
                gated(b)
                if more:
                    one(last + 1, 1)

            over_batches(dve, first, body)

        @block.tensor
        def _(pe):
            def hidden(n, k, b):
                pe.wait_ge(S["w1_lo"], n + 1)
                split_product(nc, bank_h[k][:, :], [((w1h[:, k, i, :], w1l[:, k, i, :]),
                                                     (xh[:, b % 2, i, :], xl[:, b % 2, i, :])) for i in range(TC)]
                              ).then_inc(S["h_mm"], 1)

            def spend(n, k, start=False, stop=False):
                pe.wait_ge(S["h_lo"], n + 1)
                pe.wait_ge(S["w2_lo"], n + 1)
                for c in range(CH):
                    cols = slice(c * P, (c + 1) * P)
                    last = split_product(nc, bank_y[c][:, :], [((hh[:, k, cols], hl[:, k, cols]),
                                                                (w2h[:, k, :], w2l[:, k, :]))], start=start, stop=stop)
                last.then_inc(S["y_mm"], 1)

            def x_transposes(b, i):
                pe.wait_ge(S["rows_in"], (b + 1) * CH * 16)
                for c in range(CH):
                    last = nc.tensor.transpose(bank_x[i % 2][:, c * P:(c + 1) * P], rows[:, c, i * P:(i + 1) * P],
                                               K.parts["ident"])
                last.then_inc(S["xt_mm"], 1)

            def x_free(b, i):
                pe.wait_ge(S["xt_lo"], b * TC + i - 1)

            def first():
                pe.sem_inc(S["y_mm"], Y0)
                for i in range(TC):
                    if i >= 2:
                        x_free(0, i)
                    x_transposes(0, i)
                pe.wait_ge(S["xt_lo"], TC)
                hidden(0, 0, 0)
                hidden(1, 1, 0)
                spend(0, 0, start=True)

            def body(b, more):
                n = b * HC
                with pe.Fori(0, LOOP) as i:
                    for k in range(2):
                        m = n + 2 * i + 2 + k
                        hidden(m, k, b)
                        spend(m - 1, 1 - k)
                last = n + HC
                if more:
                    x_transposes(b + 1, 0)
                    x_transposes(b + 1, 1)
                hidden(last - 2, 0, b)
                if more:
                    x_free(b + 1, 2)
                    x_transposes(b + 1, 2)
                    x_free(b + 1, 3)
                    x_transposes(b + 1, 3)
                spend(last - 3, 1)
                hidden(last - 1, 1, b)
                spend(last - 2, 0)
                if more:
                    pe.wait_ge(S["xt_lo"], (b + 1) * TC + TC)
                    hidden(last, 0, b + 1)
                spend(last - 1, 1, stop=True)
                if more:
                    hidden(last + 1, 1, b + 1)
                    pe.wait_ge(S["y_ev"], (b + 1) * CH)
                    spend(last, 0, start=True)

            over_batches(pe, first, body)


class Kept(dict):
    pass


def load_table(nc, ctx, K, name):
    K[name] = ctx.enter_context(nc.sbuf_tensor(f"table_{name}", [P, sum(TABLES[name].values())], F32))
    at = 0
    for part, width in TABLES[name].items():
        K.parts[part] = K[name][:, at:at + width]
        at += width


def block_program(nc, A, out):
    with ExitStack() as ctx:
        K = Kept()
        K.parts = {}
        load_table(nc, ctx, K, "always")
        K["stage"] = ctx.enter_context(nc.sbuf_tensor("stage", [P, NPAIR, T], F32))
        K.sems = {n: ctx.enter_context(nc.semaphore(n)) for n in ("x_in", "xres_in", "wblk_ready", "w_in",
                                                                "pair0_in", "rows_in")}
        with ExitStack() as early:
            def eb(name, shape, dt=F32):
                return early.enter_context(nc.sbuf_tensor(name, shape, dt))

            load_table(nc, early, K, "attend")
            K.update(bA=eb("bA", [P, 2]), bC=eb("bC", [P, NU]), bB=eb("bB", [P, 1]), bZ=eb("bZ", [P, T]),
                     wsub=eb("wsub", [P, NSUB, C]), fside=eb("fside", [NSUB, C]), subj=eb("subj", [NSUB, B], I32),
                     sel=eb("sel", [NSUB, B]), wblk=eb("wblk", [P, NPAIR, P]), x_res=eb("x_res", [P, NPAIR, T]), qrope=eb("q_rope", [P, GB, 2, C]))
            W = dict(WAh=eb("WAh", [P, TC, 2 * L], F32R), WAl=eb("WAl", [P, TC, 2 * L], F32R),
                     WCh=eb("WCh", [P, 2, DR * NH], F32R), WCl=eb("WCl", [P, 2, DR * NH], F32R),
                     WBh=eb("WBh", [P, 2, 2, DR], F32R), WBl=eb("WBl", [P, 2, 2, DR], F32R),
                     Ah=eb("Ah", [P, NH * L], F32R), Al=eb("Al", [P, NH * L], F32R),
                     Mh=eb("Mh", [P, NH, T], F32R), Ml=eb("Ml", [P, NH, T], F32R))
            absorb_weights(nc, K, A, W)
            attention(nc, K, A, W, out)
        flat = nc.dram_tensor("flat_dram", (NTOK, T), F32, kind="Internal").ap()
        R = dict(token=ctx.enter_context(nc.sbuf_tensor("slot_token", [P, NE * NCH], I32)),
                 gate=ctx.enter_context(nc.sbuf_tensor("slot_gate", [P, NE * NCH], F32)))
        K["rows"] = ctx.enter_context(nc.sbuf_tensor("rows", [P, CH, T], F32))
        K["pair0"] = K["stage"]
        routing(nc, K, A, out, flat, R)
        experts(nc, K, A, out, flat, R)


_INS = {'x': 'x', 'subj': 'itok_B_0_7', 'fside': 'fside_8xS_0', 'adapt': 'itok_B_0_6', 'cond_weights': 'L0_cond_weights',
        'WA': 'L0_attn_WA', 'bA': 'L0_attn_bA', 'WB': 'L0_attn_WB', 'bB': 'L0_attn_bB', 'WC': 'L0_attn_WC',
        'bC': 'L0_attn_bC', 'WUQ': 'L0_attn_WUQ', 'WUK': 'L0_attn_WUK', 'WUV': 'L0_attn_WUV', 'WZ': 'L0_attn_WZ',
        'bZ': 'L0_attn_bZ', 'W': 'L0_cond2_W', 'A': 'L0_cond2_A', 'Bm': 'L0_cond2_Bm',
        'scalings': 'L0_cond2_scalings', 'Wg': 'L0_ffn_Wg', 'bg': 'L0_ffn_bg', 'W1': 'L0_ffn_W1', 'W2': 'L0_ffn_W2'}


def kernel(**inputs):
    import concourse.bacc as _bacc
    from concourse.bass_utils import run_bass_kernel_spmd as _run

    nc = _bacc.Bacc("TRN2", target_bir_lowering=False, num_devices=1)
    arrays = {f"in_{short}_dram": np.ascontiguousarray(inputs[name]) for short, name in _INS.items()}
    arrays.update({f"in_{name}_dram": const_table(name) for name in TABLES})
    args = {name[3:-5]: nc.dram_tensor(name, a.shape, mybir.dt.from_np(a.dtype), kind="ExternalInput").ap()
            for name, a in arrays.items()}
    out = nc.dram_tensor("out_0_dram", (B, C, T), F32, kind="ExternalOutput").ap()
    block_program(nc, args, out)
    r = _run(nc, [arrays], core_ids=[0])
    return r.results[0]["out_0_dram"]
```
